# Optimizing a Trainium2 kernel written in Bass

```python
import numpy as np
import jax
import jax.numpy as jnp

def _softmax(x, axis=-1):
    return jax.nn.softmax(x, axis=axis)

def _gelu(x):
    return jax.nn.gelu(x, approximate=True)

def _silu(x):
    return jax.nn.silu(x)

def _sigmoid(x):
    return jax.nn.sigmoid(x)

def _layernorm(x, axis=-1, eps=1e-05):
    m = jnp.mean(x, axis=axis, keepdims=True)
    v = jnp.var(x, axis=axis, keepdims=True)
    return (x - m) / jnp.sqrt(v + eps)

def _scatter_add(tgt, idx, src, axis=0):
    return tgt.at[idx].add(src)

def _segment_sum(src, seg, n):
    return jax.ops.segment_sum(src, seg, n)
kernel_name = 'mk_xattn_ffn_d1_seqx_r4_787368'

def setup_inputs(seed: int=0):
    np.random.seed(seed)
    _w = jnp.asarray

    def _rec_inputs():
        import jax
        import jax.numpy as jnp
        _rk = jax.random.key(seed)
        x = 7.22e-05 + 1 * jax.random.normal(jax.random.fold_in(_rk, 1), (8, 512, 256), jnp.float32)
        _lenS = 512 - jax.random.randint(jax.random.fold_in(_rk, 7), (8,), 0, max(1, 512 // 4) + 1, jnp.int32)
        _lenS2 = 1601 - jax.random.randint(jax.random.fold_in(_rk, 8), (8,), 0, max(1, 1601 // 4) + 1, jnp.int32)
        _ctx_1024P = jax.random.normal(jax.random.fold_in(_rk, 11), (8, 16, 256), jnp.float32)
        _ctx_1024c = jax.random.dirichlet(jax.random.fold_in(_rk, 511), 0.3 * jnp.ones((16,), jnp.float32), (8, 1601))
        _ctx_1024t = jnp.einsum('bsk,bkd->bsd', _ctx_1024c, _ctx_1024P)
        _ctx_1024t = _ctx_1024t * jax.lax.rsqrt(jnp.mean(jnp.square(_ctx_1024t)) + 1e-12) * 0.953939
        ctx_1024 = 4.13588e-05 + 0.999923 * (_ctx_1024t + 0.3 * jax.random.normal(jax.random.fold_in(_rk, 611), (8, 1601, 256), jnp.float32))
        return (x, ctx_1024)
    x, ctx_1024 = _rec_inputs()

    def _L0_xattn_setup():
        import jax, jax.numpy as jnp
        import numpy as np
        DIM = 256
        HEADS = 16
        HEAD_DIM = DIM // HEADS
        key = jax.random.key(seed)
        ks = jax.random.split(key, 11)
        B, Sq, Skv = (4, 512, 512)
        s = 1.0 / np.sqrt(DIM)
        return {'query': jax.random.normal(ks[0], (B, Sq, DIM), jnp.float32), 'key': jax.random.normal(ks[1], (B, Skv, DIM), jnp.float32), 'value': jax.random.normal(ks[2], (B, Skv, DIM), jnp.float32), 'Wq': jax.random.normal(ks[3], (DIM, DIM), jnp.float32) * s, 'bq': jnp.zeros((DIM,), jnp.float32), 'Wk': jax.random.normal(ks[4], (DIM, DIM), jnp.float32) * s, 'bk': jnp.zeros((DIM,), jnp.float32), 'Wv': jax.random.normal(ks[5], (DIM, DIM), jnp.float32) * s, 'bv': jnp.zeros((DIM,), jnp.float32), 'Wo': jax.random.normal(ks[6], (DIM, DIM), jnp.float32) * s, 'bo': jnp.zeros((DIM,), jnp.float32)}
    _L0_xattn_all = _L0_xattn_setup()
    _L0_xattn_in = {k: v for k, v in _L0_xattn_all.items() if k in ('Wq', 'bq', 'Wk', 'bk', 'Wv', 'bv', 'Wo', 'bo')}
    del _L0_xattn_all

    def _L0_ffn_setup():
        import jax, jax.numpy as jnp
        import numpy as np
        EMBED = 256
        HEADS = 16
        HEAD_DIM = EMBED // HEADS
        NUM_EXPERTS = 8
        TOP_K = 2
        HIDDEN = (int(2 * (4 * EMBED) / 3) + 63) // 64 * 64
        SEQ = 512
        BATCH = 2
        ROPE_BASE = 10000.0
        EPS = 1e-06

        def _rope_tables(seq_len, dim):
            inv_freq = 1.0 / ROPE_BASE ** (np.arange(0, dim, 2, dtype=np.float32) / dim)
            t = np.arange(seq_len, dtype=np.float32)
            freqs = np.einsum('i,j->ij', t, inv_freq)
            emb = np.concatenate([freqs, freqs], axis=-1)
            return (jnp.asarray(np.cos(emb)), jnp.asarray(np.sin(emb)))

        def _rotate_half(x):
            x1, x2 = jnp.split(x, 2, axis=-1)
            return jnp.concatenate([-x2, x1], axis=-1)

        def _rmsnorm(x, w):
            return x * jax.lax.rsqrt(jnp.mean(x * x, axis=-1, keepdims=True) + EPS) * w

        def _attention(x, wq, wk, wv, wo):
            B, S, _ = x.shape
            q = (x @ wq).reshape(B, S, HEADS, HEAD_DIM).transpose(0, 2, 1, 3)
            k = (x @ wk).reshape(B, S, HEADS, HEAD_DIM).transpose(0, 2, 1, 3)
            v = (x @ wv).reshape(B, S, HEADS, HEAD_DIM).transpose(0, 2, 1, 3)
            cos, sin = _rope_tables(S, HEAD_DIM)
            cos = cos[None, None]
            sin = sin[None, None]
            q = q * cos + _rotate_half(q) * sin
            k = k * cos + _rotate_half(k) * sin
            scale = HEAD_DIM ** (-0.5)
            scores = jnp.einsum('bhqd,bhkd->bhqk', q, k) * scale
            causal = jnp.triu(jnp.ones((S, S), bool), k=1)
            scores = jnp.where(causal, -jnp.inf, scores)
            attn = jax.nn.softmax(scores, axis=-1)
            out = jnp.einsum('bhqk,bhkd->bhqd', attn, v)
            out = out.transpose(0, 2, 1, 3).reshape(B, S, EMBED)
            return out @ wo

        def _moe(x, w_router, wg, wu, wd):
            B, S, E = x.shape
            xf = x.reshape(-1, E)
            logits = xf @ w_router
            probs = jax.nn.softmax(logits, axis=-1)
            topw, topi = jax.lax.top_k(probs, TOP_K)
            topw = topw / jnp.sum(topw, axis=-1, keepdims=True)
            combine = jnp.sum(jax.nn.one_hot(topi, NUM_EXPERTS, dtype=xf.dtype) * topw[..., None], axis=1)
            g = jax.nn.silu(jnp.einsum('td,xdh->txh', xf, wg))
            u = jnp.einsum('td,xdh->txh', xf, wu)
            eo = jnp.einsum('txh,xhd->txd', g * u, wd)
            out = jnp.einsum('txd,tx->td', eo, combine)
            return out.reshape(B, S, E)
        key = jax.random.key(seed)
        ks = jax.random.split(key, 12)
        s = 0.02
        return {'x': jax.random.normal(ks[0], (BATCH, SEQ, EMBED), jnp.float32), 'wq': jax.random.normal(ks[1], (EMBED, EMBED), jnp.float32) * s, 'wk': jax.random.normal(ks[2], (EMBED, EMBED), jnp.float32) * s, 'wv': jax.random.normal(ks[3], (EMBED, EMBED), jnp.float32) * s, 'wo': jax.random.normal(ks[4], (EMBED, EMBED), jnp.float32) * s, 'w_router': jax.random.normal(ks[5], (EMBED, NUM_EXPERTS), jnp.float32) * s, 'wg': jax.random.normal(ks[6], (NUM_EXPERTS, EMBED, HIDDEN), jnp.float32) * s, 'wu': jax.random.normal(ks[7], (NUM_EXPERTS, EMBED, HIDDEN), jnp.float32) * s, 'wd': jax.random.normal(ks[8], (NUM_EXPERTS, HIDDEN, EMBED), jnp.float32) * s, 'g1': jnp.ones((EMBED,), jnp.float32), 'g2': jnp.ones((EMBED,), jnp.float32)}
    _L0_ffn_all = _L0_ffn_setup()
    _L0_ffn_in = {k: v for k, v in _L0_ffn_all.items() if k in ('wq', 'wk', 'wv', 'wo', 'w_router', 'wg', 'wu', 'wd', 'g1', 'g2')}
    del _L0_ffn_all
    return {'x': x, 'ctx_1024': ctx_1024, 'L0_xattn_Wq': _L0_xattn_in['Wq'], 'L0_xattn_bq': _L0_xattn_in['bq'], 'L0_xattn_Wk': _L0_xattn_in['Wk'], 'L0_xattn_bk': _L0_xattn_in['bk'], 'L0_xattn_Wv': _L0_xattn_in['Wv'], 'L0_xattn_bv': _L0_xattn_in['bv'], 'L0_xattn_Wo': _L0_xattn_in['Wo'], 'L0_xattn_bo': _L0_xattn_in['bo'], 'L0_ffn_wq': _L0_ffn_in['wq'], 'L0_ffn_wk': _L0_ffn_in['wk'], 'L0_ffn_wv': _L0_ffn_in['wv'], 'L0_ffn_wo': _L0_ffn_in['wo'], 'L0_ffn_w_router': _L0_ffn_in['w_router'], 'L0_ffn_wg': _L0_ffn_in['wg'], 'L0_ffn_wu': _L0_ffn_in['wu'], 'L0_ffn_wd': _L0_ffn_in['wd'], 'L0_ffn_g1': _L0_ffn_in['g1'], 'L0_ffn_g2': _L0_ffn_in['g2']}

def reference(x, ctx_1024, L0_xattn_Wq, L0_xattn_bq, L0_xattn_Wk, L0_xattn_bk, L0_xattn_Wv, L0_xattn_bv, L0_xattn_Wo, L0_xattn_bo, L0_ffn_wq, L0_ffn_wk, L0_ffn_wv, L0_ffn_wo, L0_ffn_w_router, L0_ffn_wg, L0_ffn_wu, L0_ffn_wd, L0_ffn_g1, L0_ffn_g2):
    import jax
    import jax.numpy as jnp

    def _L0_xattn_ref(query, key, value, Wq, bq, Wk, bk, Wv, bv, Wo, bo):
        import jax, jax.numpy as jnp
        import numpy as np
        DIM = 256
        HEADS = 16
        HEAD_DIM = DIM // HEADS
        B = query.shape[0]
        scale = HEAD_DIM ** (-0.5)
        q = (query @ Wq.T + bq).reshape(B, -1, HEADS, HEAD_DIM)
        k = (key @ Wk.T + bk).reshape(B, -1, HEADS, HEAD_DIM)
        v = (value @ Wv.T + bv).reshape(B, -1, HEADS, HEAD_DIM)
        scores = jnp.einsum('bqhd,bkhd->bhqk', q, k) * scale
        attn = jax.nn.softmax(scores, axis=-1)
        out = jnp.einsum('bhqk,bkhd->bqhd', attn, v).reshape(B, -1, DIM)
        return out @ Wo.T + bo

    def _L0_ffn_ref(x, wq, wk, wv, wo, w_router, wg, wu, wd, g1, g2):
        import jax, jax.numpy as jnp
        import numpy as np
        EMBED = 256
        HEADS = 16
        HEAD_DIM = EMBED // HEADS
        NUM_EXPERTS = 8
        TOP_K = 2
        HIDDEN = (int(2 * (4 * EMBED) / 3) + 63) // 64 * 64
        SEQ = 512
        BATCH = 2
        ROPE_BASE = 10000.0
        EPS = 1e-06

        def _rope_tables(seq_len, dim):
            inv_freq = 1.0 / ROPE_BASE ** (np.arange(0, dim, 2, dtype=np.float32) / dim)
            t = np.arange(seq_len, dtype=np.float32)
            freqs = np.einsum('i,j->ij', t, inv_freq)
            emb = np.concatenate([freqs, freqs], axis=-1)
            return (jnp.asarray(np.cos(emb)), jnp.asarray(np.sin(emb)))

        def _rotate_half(x):
            x1, x2 = jnp.split(x, 2, axis=-1)
            return jnp.concatenate([-x2, x1], axis=-1)

        def _rmsnorm(x, w):
            return x * jax.lax.rsqrt(jnp.mean(x * x, axis=-1, keepdims=True) + EPS) * w

        def _attention(x, wq, wk, wv, wo):
            B, S, _ = x.shape
            q = (x @ wq).reshape(B, S, HEADS, HEAD_DIM).transpose(0, 2, 1, 3)
            k = (x @ wk).reshape(B, S, HEADS, HEAD_DIM).transpose(0, 2, 1, 3)
            v = (x @ wv).reshape(B, S, HEADS, HEAD_DIM).transpose(0, 2, 1, 3)
            cos, sin = _rope_tables(S, HEAD_DIM)
            cos = cos[None, None]
            sin = sin[None, None]
            q = q * cos + _rotate_half(q) * sin
            k = k * cos + _rotate_half(k) * sin
            scale = HEAD_DIM ** (-0.5)
            scores = jnp.einsum('bhqd,bhkd->bhqk', q, k) * scale
            causal = jnp.triu(jnp.ones((S, S), bool), k=1)
            scores = jnp.where(causal, -jnp.inf, scores)
            attn = jax.nn.softmax(scores, axis=-1)
            out = jnp.einsum('bhqk,bhkd->bhqd', attn, v)
            out = out.transpose(0, 2, 1, 3).reshape(B, S, EMBED)
            return out @ wo

        def _moe(x, w_router, wg, wu, wd):
            B, S, E = x.shape
            xf = x.reshape(-1, E)
            logits = xf @ w_router
            probs = jax.nn.softmax(logits, axis=-1)
            topw, topi = jax.lax.top_k(probs, TOP_K)
            topw = topw / jnp.sum(topw, axis=-1, keepdims=True)
            combine = jnp.sum(jax.nn.one_hot(topi, NUM_EXPERTS, dtype=xf.dtype) * topw[..., None], axis=1)
            g = jax.nn.silu(jnp.einsum('td,xdh->txh', xf, wg))
            u = jnp.einsum('td,xdh->txh', xf, wu)
            eo = jnp.einsum('txh,xhd->txd', g * u, wd)
            out = jnp.einsum('txd,tx->td', eo, combine)
            return out.reshape(B, S, E)
        h = x + _attention(_rmsnorm(x, g1), wq, wk, wv, wo)
        y = h + _moe(_rmsnorm(h, g2), w_router, wg, wu, wd)
        return y
    x = x + _L0_xattn_ref(_layernorm(x, axis=-1), ctx_1024, ctx_1024, L0_xattn_Wq, L0_xattn_bq, L0_xattn_Wk, L0_xattn_bk, L0_xattn_Wv, L0_xattn_bv, L0_xattn_Wo, L0_xattn_bo)
    x = x + _L0_ffn_ref(_layernorm(x, axis=-1), L0_ffn_wq, L0_ffn_wk, L0_ffn_wv, L0_ffn_wo, L0_ffn_w_router, L0_ffn_wg, L0_ffn_wu, L0_ffn_wd, L0_ffn_g1, L0_ffn_g2)
    return x

_drawn_inputs = setup_inputs


def setup_inputs(seed=0):
    import zlib

    import numpy as np

    out = dict(_drawn_inputs(seed))
    spreads = {'L0_xattn_bq': (0.0, 0.413),
     'L0_xattn_bk': (0.0, 0.8),
     'L0_xattn_bv': (0.0, 0.1),
     'L0_xattn_bo': (0.0, 0.1),
     'L0_ffn_g1': (1.0, 0.6),
     'L0_ffn_g2': (1.0, 0.6)}
    factors = {'L0_ffn_wq': 8.0,
     'L0_ffn_wk': 8.0,
     'L0_ffn_w_router': 6.149,
     'L0_ffn_wg': 5.634,
     'L0_ffn_wu': 5.576,
     'L0_ffn_wd': 5.566}
    for name, (base, spread) in spreads.items():
        noise = np.random.default_rng([zlib.crc32(name.encode()), seed]).standard_normal(out[name].shape)
        drawn = base * np.exp(spread * noise) if base else spread * noise
        out[name] = jnp.asarray(drawn.astype(out[name].dtype))
    for name, factor in factors.items():
        out[name] = (out[name] * factor).astype(out[name].dtype)
    return out
```

```python
import concourse.bass as bass
from concourse import mybir
from contextlib import ExitStack

F32 = mybir.dt.float32
BF16 = mybir.dt.bfloat16
I32 = mybir.dt.int32
U32 = mybir.dt.uint32
ALU = mybir.AluOpType
ACT = mybir.ActivationFunctionType
AX = mybir.AxisListType

P = 128
DIM = 256
KC = DIM // P
HEADS = 16
HD = DIM // HEADS
GH = 4
GROUPS = HEADS // GH
GR = GH * HD
SEQ = 512
QT = SEQ // P
CTX = 1601
EXPERTS = 8
HIDDEN = 704
HC = -(-HIDDEN // P)
HLAST = HIDDEN - (HC - 1) * P
HHALF = HIDDEN // 2
SCALE = HD ** -0.5
MASKED = -1e30
LN_EPS = 1e-5
RMS_EPS = 1e-6

K_PARTS = (0, 1, 2, 0, 1, 0)
Q_PARTS = (0, 0, 0, 1, 1, 2)
PAIRS = len(K_PARTS)
SROWS = PAIRS * HD
MROWS = SROWS + 3
VW = 32


class Prog:

    def __init__(self, nc, stack, stage):
        self.nc, self.stack, self.stage, self.sems = nc, stack, stage, []

    def sb(self, name, shape, dt=F32):
        return self.stack.enter_context(self.nc.sbuf_tensor(self.stage + name, shape, dt))

    def ps(self, name, shape, dt=F32):
        return self.stack.enter_context(self.nc.psum_tensor(self.stage + name, shape, dt))

    def sem(self, name):
        self.sems.append(self.stack.enter_context(self.nc.semaphore(self.stage + name)))
        return self.sems[-1]

    def clear(self):
        for s in self.sems:
            self.nc.sync.sem_clear(s)
        self.nc.all_engine_barrier()


def prepare_weights(nc, w, keep):
    with ExitStack() as stack:
        p = Prog(nc, stack, "prep_")
        raw = {n: p.sb(f"raw_{n}", [P, KC, DIM]) for n in ("Wq", "Wk", "Wv", "Wo")}
        turned = [p.ps(f"turned{i}", [P, KC, DIM]) for i in range(4)]
        consts_in = p.sem("consts_in")
        raw_in = p.sem("raw_in")
        small_in = p.sem("small_in")
        turned_ready = p.sem("turned_ready")
        turned_kept = p.sem("turned_kept")
        rot_ready = p.sem("rot_ready")

        with nc.Block() as block:
            @block.sync
            def _(sp):
                for name in ("ident", "mask_q", "mask_kv", "before", "cos_q", "sin_q", "cos_k", "sin_k",
                             "iota_left", "iota_tile", "iota_count", "lt8"):
                    sp.dma_start(keep[name][:, :], w[name]).then_inc(consts_in, 16)
                for n in ("Wq", "Wk", "Wv", "Wo"):
                    sp.dma_start(raw[n][:, :, :], w[n].rearrange("(c p) i -> p c i", p=P)).then_inc(raw_in, 16)
                sp.wait_ge(consts_in, 16 * 12)

            @block.scalar
            def _(act):
                for n in ("bq", "bk", "g1"):
                    act.dma_start(keep[n][:, :], w[n].rearrange("(c p) -> p c", p=P),
                                  allow_slow_non_contiguous=True).then_inc(small_in, 16)
                for n in ("bv", "bo", "g2"):
                    act.dma_start(keep[n][:, :], w[n].partition_broadcast(P)).then_inc(small_in, 16)
                for n in ("wq", "wk", "wv", "wo"):
                    act.dma_start(keep[n][:, :, :], w[n].rearrange("(c p) o -> p c o", p=P)).then_inc(small_in, 16)
                act.dma_start(keep["w_router"][:, :, :], w["w_router"].rearrange("(c p) e -> p c e", p=P))\
                   .then_inc(small_in, 16)
                act.wait_ge(small_in, 16 * 11)
                nc.scalar.mul(keep["bq"][:, :], keep["bq"][:, :], SCALE)
                for src, dst in (("wq", "wq_rot"), ("wk", "wk_rot")):
                    s = keep[src][:, :, :].rearrange("p c (h t d) -> p (c h) t d", t=2, d=HD // 2)
                    d = keep[dst][:, :, :].rearrange("p c (h t d) -> p (c h) t d", t=2, d=HD // 2)
                    nc.scalar.mul(d[:, :, 0, :], s[:, :, 1, :], -1.0)
                    last = nc.scalar.copy(d[:, :, 1, :], s[:, :, 0, :])
                last.then_inc(rot_ready, 1)
                act.wait_ge(rot_ready, 1)

            @block.tensor
            def _(pe):
                pe.wait_ge(consts_in, 16 * 12)
                pe.wait_ge(raw_in, 16 * 4)
                for k, n in enumerate(("Wq", "Wk", "Wv", "Wo")):
                    for i in range(KC):
                        for o in range(KC):
                            last = nc.tensor.transpose(turned[k][:, i, o * P:(o + 1) * P],
                                                       raw[n][:, o, i * P:(i + 1) * P], keep["ident"][:, :])
                    last.then_inc(turned_ready, 1)

            @block.vector
            def _(dve):
                nc.vector.memset(keep["ln_eps"][:, :], LN_EPS)
                nc.vector.memset(keep["rms_eps"][:, :], RMS_EPS)
                for k, n in enumerate(("WqT", "WkT", "WvT", "WoT")):
                    dve.wait_ge(turned_ready, k + 1)
                    nc.vector.tensor_copy(keep[n][:, :, :], turned[k][:, :, :])
                dve.wait_ge(consts_in, 16 * 12)
                for n in ("ident", "mask_q", "mask_kv", "before"):
                    last = nc.vector.tensor_copy(keep[n + "_b"][:, :], keep[n][:, :])
                last.then_inc(turned_kept, 1)
                dve.wait_ge(turned_kept, 1)
        p.clear()


def project_context(nc, ctx_in, k_parts, v_rows, keep, batches):
    chunks = [(o, min(SEQ, CTX - o)) for o in range(0, CTX, SEQ)]
    N = len(chunks)
    assert N % 2 == 0
    with ExitStack() as stack:
        p = Prog(nc, stack, "ctx_")
        rows = [p.sb(f"ctx_rows{i}", [P, QT, DIM]) for i in range(2)]
        xT = [p.sb(f"ctxT{i}", [P, KC, SEQ]) for i in range(2)]
        kf = [p.sb(f"k_full{i}", [P, KC, SEQ]) for i in range(2)]
        rest = [p.sb(f"k_rest{i}", [P, KC, SEQ]) for i in range(2)]
        parts = [[p.sb(f"k_part{i}{a}", [P, KC, SEQ], BF16) for a in range(3)] for i in range(2)]
        vpad = [p.sb(f"v_pad{i}", [P, QT, HEADS, VW]) for i in range(2)]
        ps_t = p.ps("ps_t", [P, KC, SEQ])
        ps_k = p.ps("ps_k", [P, KC, SEQ])
        ps_v = p.ps("ps_v", [P, QT, DIM])
        rows_in = [p.sem(f"rows_in{i}") for i in range(2)]
        out_sent = [p.sem(f"out_sent{i}") for i in range(2)]
        turned = p.sem("turned")
        xT_ready = p.sem("xT_ready")
        k_done = p.sem("k_done")
        v_done = p.sem("v_done")
        k_hi = p.sem("k_hi")
        v_ready = p.sem("v_ready")
        rest_ready = p.sem("rest_ready")
        mid_ready = p.sem("mid_ready")
        low_ready = p.sem("low_ready")
        pads = p.sem("pads")
        pool_turn = p.sem("pool_turn")
        SENT = 16 * (3 * KC + GROUPS)

        def tiles(n):
            return [(t, min(P, n - t * P)) for t in range(-(-n // P))]

        with nc.Block() as block:
            @block.sync
            def _(sp):
                sp.sem_inc(turned, 2)
                for i in range(2):
                    sp.sem_inc(out_sent[i], SENT)

                def load(b, c):
                    o, n = chunks[c]
                    sp.wait_ge(turned, b * N + c + 1)
                    src = ctx_in[bass.ds(b * CTX + o, n), :]
                    if n >= P:
                        sp.dma_start(rows[c % 2][:, 0:n // P, :], src.rearrange("(t p) d -> p t d", p=P))\
                          .then_inc(rows_in[c % 2], 16)
                    else:
                        sp.dma_start(rows[c % 2][0:n, 0, :], src).then_inc(rows_in[c % 2], 16)

                def store(b, c):
                    (o, n), par = chunks[c], c % 2
                    sp.wait_ge(low_ready, b * N + c + 3)
                    for a in range(3):
                        for i in range(KC):
                            sp.dma_start(k_parts[bass.ds(b * GROUPS + i * 2, 2), a, :, o:o + n],
                                         parts[par][a][:, i, 0:n]).then_inc(out_sent[par], 16)
                    sp.wait_ge(v_ready, b * N + c + 2)
                    for g in range(GROUPS):
                        dst = v_rows[b * GROUPS + g, o:o + n, :]
                        if n >= P:
                            sp.dma_start(dst.rearrange("(t p) v -> p t v", p=P),
                                         vpad[par][:, 0:n // P, g * GH:(g + 1) * GH, :]
                                         .rearrange("p t h v -> p t (h v)")).then_inc(out_sent[par], 16)
                        else:
                            sp.dma_start(dst, vpad[par][0:n, 0, g * GH:(g + 1) * GH, :]
                                         .rearrange("p h v -> p (h v)")).then_inc(out_sent[par], 16)

                load(0, 0)
                with sp.Fori(0, batches - 1) as b:
                    for c in range(N):
                        load(*((b, c + 1) if c + 1 < N else (b + 1, 0)))
                        store(b, c)
                for c in range(N):
                    if c + 1 < N:
                        load(batches - 1, c + 1)
                    store(batches - 1, c)
                for i in range(2):
                    sp.wait_ge(out_sent[i], SENT * (batches * (N // 2) + 1))

            @block.tensor
            def _(pe):
                pe.sem_inc(k_done, 2)
                with pe.Fori(0, batches) as b:
                    for c, (o, n) in enumerate(chunks):
                        S, par = b * N + c, c % 2
                        pe.wait_ge(rows_in[par], (b * (N // 2) + c // 2 + 1) * 16)
                        pe.wait_ge(xT_ready, S + 1)
                        for t, m in tiles(n):
                            for i in range(KC):
                                last = nc.tensor.transpose(ps_t[:, i, t * P:t * P + m],
                                                           rows[par][0:m, t, i * P:(i + 1) * P],
                                                           keep["ident"][0:m, 0:m])
                        last.then_inc(turned, 1)
                        pe.wait_ge(xT_ready, S + 2)
                        pe.wait_ge(k_hi, S + 1)
                        for o2 in range(KC):
                            for i in range(KC):
                                last = nc.tensor.matmul(ps_k[:, o2, 0:n], keep["WkT"][:, i, o2 * P:(o2 + 1) * P],
                                                        xT[par][:, i, 0:n], start=(i == 0), stop=(i == KC - 1))
                        last.then_inc(k_done, 1)
                        pe.wait_ge(v_ready, S + 1)
                        for t, m in tiles(n):
                            for i in range(KC):
                                last = nc.tensor.matmul(ps_v[0:m, t, :], xT[par][:, i, t * P:t * P + m],
                                                        keep["WvT"][:, i, :], start=(i == 0), stop=(i == KC - 1))
                        last.then_inc(v_done, 1)

            @block.vector
            def _(dve):
                for i in range(2):
                    nc.vector.memset(vpad[i][:, :, :, HD:VW], 0.0).then_inc(pads, 1)
                dve.wait_ge(pads, 2)
                for i in range(2):
                    nc.vector.memset(vpad[i][:, :, :, HD:HD + 1], 1.0).then_inc(pads, 1)
                dve.wait_ge(pads, 4)
                dve.sem_inc(xT_ready, 1)
                dve.sem_inc(v_ready, 1)
                dve.sem_inc(rest_ready, 2)
                with dve.Fori(0, batches) as b:
                    for c, (o, n) in enumerate(chunks):
                        S, par = b * N + c, c % 2
                        dve.wait_ge(turned, S + 3)
                        dve.wait_ge(k_done, S + 1)
                        nc.vector.tensor_copy(xT[par][:, :, 0:n], ps_t[:, :, 0:n]).then_inc(xT_ready, 1)
                        dve.wait_ge(k_hi, S + 2)
                        dve.wait_ge(low_ready, S + 1)
                        nc.vector.tensor_tensor(rest[par][:, :, 0:n], kf[par][:, :, 0:n], parts[par][0][:, :, 0:n],
                                                ALU.subtract).then_inc(rest_ready, 1)
                        dve.wait_ge(v_done, S + 1)
                        dve.wait_ge(out_sent[par], (b * (N // 2) + c // 2 + 1) * SENT)
                        for t0, t1, m in ((0, n // P, P), (n // P, n // P + 1, n % P)):
                            if m == 0 or t1 == t0:
                                continue
                            bias = keep["bv"][0:m, :].rearrange("p (h d) -> p h d", d=HD)
                            for t in range(t0, t1):
                                last = nc.vector.tensor_tensor(
                                    vpad[par][0:m, t, :, 0:HD],
                                    ps_v[0:m, t, :].rearrange("p (h d) -> p h d", d=HD), bias, ALU.add)
                        last.then_inc(v_ready, 1)

            @block.scalar
            def _(act):
                act.sem_inc(k_hi, 1)
                with act.Fori(0, batches) as b:
                    for c, (o, n) in enumerate(chunks):
                        S, par = b * N + c, c % 2
                        act.wait_ge(k_done, S + 3)
                        act.wait_ge(rest_ready, S + 1)
                        act.wait_ge(out_sent[par], (b * (N // 2) + c // 2 + 1) * SENT)
                        for i in range(KC):
                            nc.scalar.activation(kf[par][:, i, 0:n], ps_k[:, i, 0:n], ACT.Identity,
                                                 bias=keep["bk"][:, i:i + 1])
                            last = nc.scalar.activation(parts[par][0][:, i, 0:n], ps_k[:, i, 0:n], ACT.Identity,
                                                        bias=keep["bk"][:, i:i + 1])
                        last.then_inc(k_hi, 1)

            @block.gpsimd
            def _(pool):
                pool.sem_inc(low_ready, 2)
                with pool.Fori(0, batches) as b:
                    for c, (o, n) in enumerate(chunks):
                        S, par = b * N + c, c % 2
                        pool.wait_ge(rest_ready, S + 3)
                        pool.sem_inc(pool_turn, 1)
                        nc.gpsimd.tensor_copy(parts[par][1][:, :, 0:n], rest[par][:, :, 0:n]).then_inc(mid_ready, 1)
                        pool.wait_ge(mid_ready, S + 1)
                        nc.gpsimd.tensor_tensor(parts[par][2][:, :, 0:n], rest[par][:, :, 0:n],
                                                parts[par][1][:, :, 0:n], ALU.subtract).then_inc(low_ready, 1)
        p.clear()




def project_queries(nc, x_in, q_parts, keep, batches):
    with ExitStack() as stack:
        p = Prog(nc, stack, "qry_")
        rows = [p.sb(f"x_rows{i}", [P, QT, DIM]) for i in range(2)]
        normed = [p.sb(f"x_normed{i}", [P, QT, DIM]) for i in range(2)]
        stats = p.sb("ln_stats", [P, QT, 6])
        mv = p.sb("ln_mv", [P, QT, 2])
        std = p.sb("ln_std", [P, QT])
        rstd = p.sb("ln_rstd", [P, QT])
        xT = [p.sb(f"xT{i}", [P, KC, SEQ]) for i in range(2)]
        full = [p.sb(f"q_full{i}", [P, KC, SEQ]) for i in range(2)]
        rest = [p.sb(f"q_rest{i}", [P, KC, SEQ]) for i in range(2)]
        parts = [[p.sb(f"q_part{i}{a}", [P, KC, SEQ], BF16) for a in range(3)] for i in range(2)]
        ps_t = [p.ps(f"ps_t{i}", [P, KC, SEQ]) for i in range(2)]
        ps_q = [p.ps(f"ps_q{i}", [P, KC, SEQ]) for i in range(2)]
        rows_in = [p.sem(f"rows_in{i}") for i in range(2)]
        out_sent = [p.sem(f"out_sent{i}") for i in range(2)]
        mv_ready = p.sem("mv_ready")
        std_ready = p.sem("std_ready")
        norm_ready = p.sem("norm_ready")
        turned = p.sem("turned")
        xT_ready = p.sem("xT_ready")
        q_done = p.sem("q_done")
        q_hi = p.sem("q_hi")
        rest_ready = p.sem("rest_ready")
        mid_ready = p.sem("mid_ready")
        low_ready = p.sem("low_ready")
        pool_turn = p.sem("pool_turn")
        SENT = 16 * 3 * KC

        with nc.Block() as block:
            @block.sync
            def _(sp):
                sp.sem_inc(norm_ready, 2)
                for i in range(2):
                    sp.sem_inc(out_sent[i], SENT)

                def load(S, par):
                    sp.wait_ge(norm_ready, S + 1)
                    sp.dma_start(rows[par][:, :, :],
                                 x_in[bass.ds(S * SEQ, SEQ), :].rearrange("(t p) d -> p t d", p=P))\
                      .then_inc(rows_in[par], 16)

                def store(S, par):
                    sp.wait_ge(low_ready, S + 3)
                    for a in range(3):
                        for i in range(KC):
                            sp.dma_start(q_parts[bass.ds(S * GROUPS + i * 2, 2), a, :, :],
                                         parts[par][a][:, i, :]).then_inc(out_sent[par], 16)

                load(0, 0)
                with sp.Fori(0, batches // 2 - 1) as b2:
                    for par in range(2):
                        load(b2 * 2 + par + 1, (par + 1) % 2)
                        store(b2 * 2 + par, par)
                load(batches - 1, 1)
                store(batches - 2, 0)
                store(batches - 1, 1)
                for i in range(2):
                    sp.wait_ge(out_sent[i], SENT * (batches // 2 + 1))

            @block.vector
            def _(dve):
                dve.sem_inc(rest_ready, 2)
                with dve.Fori(0, batches // 2) as b2:
                    for par in range(2):
                        S = b2 * 2 + par
                        dve.wait_ge(rows_in[par], (b2 + 1) * 16)
                        for t in range(QT):
                            nc.vector.bn_stats(stats[:, t, :], rows[par][:, t, :])
                        dve.drain()
                        for t in range(QT):
                            last = nc.vector.bn_aggr(mv[:, t, :], stats[:, t, :])
                        last.then_inc(mv_ready, 1)
                        dve.wait_ge(std_ready, S + 1)
                        nc.vector.reciprocal(rstd[:, :], std[:, :])
                        dve.drain()
                        dve.wait_ge(turned, S + 1)
                        for t in range(QT):
                            last = nc.vector.tensor_scalar(normed[par][:, t, :], rows[par][:, t, :], mv[:, t, 0:1],
                                                           rstd[:, t:t + 1], ALU.subtract, ALU.mult)
                        last.then_inc(norm_ready, 1)
                        dve.wait_ge(turned, S + 3)
                        dve.wait_ge(q_done, S + 1)
                        nc.vector.tensor_copy(xT[par][:, :, :], ps_t[par][:, :, :]).then_inc(xT_ready, 1)
                        dve.wait_ge(q_hi, S + 1)
                        dve.wait_ge(low_ready, S + 1)
                        nc.vector.tensor_tensor(rest[par][:, :, :], full[par][:, :, :], parts[par][0][:, :, :],
                                                ALU.subtract).then_inc(rest_ready, 1)

            @block.tensor
            def _(pe):
                pe.sem_inc(turned, 2)
                pe.sem_inc(q_done, 2)
                with pe.Fori(0, batches // 2) as b2:
                    for par in range(2):
                        S = b2 * 2 + par
                        pe.wait_ge(norm_ready, S + 3)
                        for t in range(QT):
                            for i in range(KC):
                                last = nc.tensor.transpose(ps_t[par][:, i, t * P:(t + 1) * P],
                                                           normed[par][:, t, i * P:(i + 1) * P], keep["ident"][:, :])
                        last.then_inc(turned, 1)
                        pe.wait_ge(xT_ready, S + 1)
                        for o in range(KC):
                            for i in range(KC):
                                last = nc.tensor.matmul(ps_q[par][:, o, :], keep["WqT"][:, i, o * P:(o + 1) * P],
                                                        xT[par][:, i, :], start=(i == 0), stop=(i == KC - 1))
                        last.then_inc(q_done, 1)

            @block.scalar
            def _(act):
                with act.Fori(0, batches // 2) as b2:
                    for par in range(2):
                        S = b2 * 2 + par
                        act.wait_ge(mv_ready, S + 1)
                        nc.scalar.activation(std[:, :], mv[:, :, 1], ACT.Sqrt, bias=keep["ln_eps"][:, :])\
                           .then_inc(std_ready, 1)
                        act.wait_ge(q_done, S + 3)
                        act.wait_ge(rest_ready, S + 1)
                        act.wait_ge(out_sent[par], (b2 + 1) * SENT)
                        for i in range(KC):
                            nc.scalar.activation(full[par][:, i, :], ps_q[par][:, i, :], ACT.Identity,
                                                 bias=keep["bq"][:, i:i + 1], scale=SCALE)
                            last = nc.scalar.activation(parts[par][0][:, i, :], ps_q[par][:, i, :], ACT.Identity,
                                                        bias=keep["bq"][:, i:i + 1], scale=SCALE)
                        last.then_inc(q_hi, 1)

            @block.gpsimd
            def _(pool):
                pool.sem_inc(low_ready, 2)
                with pool.Fori(0, batches // 2) as b2:
                    for par in range(2):
                        S = b2 * 2 + par
                        pool.wait_ge(rest_ready, S + 3)
                        pool.sem_inc(pool_turn, 1)
                        nc.gpsimd.tensor_copy(parts[par][1][:, :, :], rest[par][:, :, :]).then_inc(mid_ready, 1)
                        pool.wait_ge(mid_ready, S + 1)
                        nc.gpsimd.tensor_tensor(parts[par][2][:, :, :], rest[par][:, :, :], parts[par][1][:, :, :],
                                                ALU.subtract).then_inc(low_ready, 1)
        p.clear()


def attention(nc, q_parts, k_parts, v_rows, out_rows, kv, causal, keep, units):
    tiles = [(t, min(P, kv - t * P)) for t in range(-(-kv // P))]
    NT = len(tiles)
    STEPS = NT * GH
    RING = 8
    LAG = 4
    if causal:
        pieces = [(j, q, [(0, (q + 1) * P)]) for j in range(GH) for q in range(QT)]
        PIECES = 1
        first_step, every = 4, 1.0
    else:
        span = -(-kv // 4)
        starts = [min(i * (kv // 4), kv - span) for i in range(4)]
        pieces = [(j, q, [(s, span) for s in starts[h * 2:h * 2 + 2]])
                  for j in range(GH) for q in range(QT) for h in range(2)]
        PIECES = 2
        first_step, every = 8, 40 / 32
    NP = len(pieces)
    SLOTS = NP + 1
    with ExitStack() as stack:
        p = Prog(nc, stack, "att_self_" if causal else "att_cross_")
        kp = [p.sb(f"k_pack{i}", [P, GH, kv], BF16) for i in range(2)]
        qp = [p.sb(f"q_pack{i}", [P, GH, SEQ], BF16) for i in range(2)]
        va = [p.sb(f"v_tiles{i}", [P, NT, GH * VW]) for i in range(2)]
        pr = p.sb("probs", [P, RING, SEQ])
        nmax = p.sb("neg_max", [P, GH * QT, PIECES])
        nm = p.sb("neg_max_merged", [P, GH * QT])
        nm_rest = p.sb("neg_max_rest", [P, GH * QT])
        nm_parts = p.sb("neg_max_parts", [P, P // (GH * QT), GH * QT], BF16)
        nm_rows = p.sb("neg_max_rows", [3 * GH * QT, P], BF16)
        ob = [p.sb(f"out_buf{i}", [P, SEQ]) for i in range(2)]
        ps_s = [p.ps(f"ps_s{i}", [P, 2, SEQ]) for i in range(2)]
        ps_st = [p.ps(f"ps_st{i}", [P, SEQ]) for i in range(2)]
        ps_o = [p.ps(f"ps_o{i}", [P, SEQ]) for i in range(2)]
        ones_set = p.sem("ones_set")
        kq_in = [p.sem(f"kq_in{i}") for i in range(2)]
        v_in = [p.sem(f"v_in{i}") for i in range(2)]
        m_rows_in = p.sem("m_rows_in")
        st_done = p.sem("st_done")
        exp_done = p.sem("exp_done")
        pv_done = p.sem("pv_done")
        s_done = p.sem("s_done")
        s_read = p.sem("s_read")
        m_split = p.sem("m_split")
        m_kept = p.sem("m_kept")
        o_read = p.sem("o_read")
        o_sent = [p.sem(f"o_sent{i}") for i in range(2)]
        AHEAD = 2 * STEPS
        KQ = 16 * 2 * PAIRS

        def piece_after(step):
            lo = [i for i in range(NP) if int(first_step + i * every) == step]
            if step == STEPS - 1:
                lo += [i for i in range(NP) if int(first_step + i * every) >= STEPS]
            return lo

        with nc.Block() as block:
            @block.sync
            def _(sp):
                def load_kq(u, par):
                    sp.wait_ge(st_done, (u + 1) * STEPS)
                    for r in range(PAIRS):
                        sp.dma_start(kp[par][r * HD:(r + 1) * HD, :, :],
                                     k_parts[u, K_PARTS[r], :, :].rearrange("(j d) n -> d j n", d=HD))\
                          .then_inc(kq_in[par], 16)
                        sp.dma_start(qp[par][r * HD:(r + 1) * HD, :, :],
                                     q_parts[u, Q_PARTS[r], :, :].rearrange("(j d) n -> d j n", d=HD))\
                          .then_inc(kq_in[par], 16)

                def load_v(u, par):
                    sp.wait_ge(pv_done, (u + 1) * STEPS)
                    if kv >= P:
                        sp.dma_start(va[par][:, 0:kv // P, :],
                                     v_rows[u, 0:kv // P * P, :].rearrange("(t p) v -> p t v", p=P))\
                          .then_inc(v_in[par], 16)
                    if kv % P:
                        sp.dma_start(va[par][0:kv % P, kv // P, :], v_rows[u, kv // P * P:kv, :])\
                          .then_inc(v_in[par], 16)

                def send_max(u, par):
                    sp.wait_ge(s_read, (u + 1) * SLOTS + 2)
                    for a in range(3):
                        sp.dma_start(qp[par][SROWS + a:SROWS + a + 1, :, :].rearrange("o j n -> o (j n)"),
                                     nm_rows[a * GH * QT:(a + 1) * GH * QT, :]).then_inc(m_rows_in, 16)

                def send_out(u, par):
                    sp.wait_ge(o_read, u + 3)
                    sp.dma_start(out_rows[u, :, :], ob[par][:, :]).then_inc(o_sent[par], 16)

                def unit(u, par):
                    send_max(u + 1, (par + 1) % 2)
                    load_kq(u + 2, par)
                    send_out(u, par)
                    load_v(u + 2, par)

                sp.sem_inc(m_rows_in, 1)
                for i in range(2):
                    sp.sem_inc(o_sent[i], 16)
                    load_kq(i, i)
                    load_v(i, i)
                send_max(0, 0)
                with sp.Fori(0, units // 2 - 1) as i:
                    unit(i * 2, 0)
                    unit(i * 2 + 1, 1)
                send_max(units - 1, 1)
                send_out(units - 2, 0)
                send_out(units - 1, 1)
                for i in range(2):
                    sp.wait_ge(o_sent[i], 16 * (units // 2 + 1))

            VLOADS = 16 * ((1 if kv >= P else 0) + (1 if kv % P else 0))

            @block.tensor
            def _(pe):
                pe.sem_inc(st_done, AHEAD)
                pe.sem_inc(pv_done, AHEAD)

                def piece(u, par, k):
                    j, q, spans = pieces[k]
                    slot = (par * SLOTS + k) % 2
                    pe.wait_ge(s_read, u * SLOTS + k + 1)
                    for n, (s, w) in enumerate(spans):
                        last = nc.tensor.matmul(ps_s[slot][:, n, 0:w], qp[par][0:SROWS, j, q * P:(q + 1) * P],
                                                kp[par][0:SROWS, j, s:s + w], start=True, stop=not causal)
                        if causal:
                            last = nc.tensor.matmul(ps_s[slot][:, n, w - P:w], keep["ident_b"][:, :],
                                                    keep["mask_q_b"][:, :], start=False, stop=True)
                    last.then_inc(s_done, 1)

                def turn_max(u, par):
                    slot = (par * SLOTS + NP) % 2
                    pe.wait_ge(s_read, u * SLOTS + NP + 1)
                    pe.wait_ge(m_split, u + 1)
                    nc.tensor.transpose(ps_s[slot][:, 0, 0:P // 2].bitcast(BF16),
                                        nm_parts[:, :, :].rearrange("p a q -> p (a q)"), keep["ident_b"][:, :])\
                      .then_inc(s_done, 1)

                def unit(u, par, n, following):
                    ahead = (par + 1) % 2
                    n_ahead = n + par
                    pe.wait_ge(m_rows_in, (u + 1) * 48 + 1)
                    for s in range(STEPS + LAG):
                        if s < STEPS:
                            t, j = s // GH, s % GH
                            rows = tiles[t][1]
                            q0 = t * P if causal else 0
                            N = u * STEPS + s
                            pe.wait_ge(exp_done, N + 1)
                            mm = nc.tensor.matmul(ps_st[s % 2][0:rows, q0:SEQ], kp[par][0:MROWS, j, t * P:t * P + rows],
                                                  qp[par][0:MROWS, j, q0:SEQ], start=True, stop=not causal)
                            if causal:
                                mm = nc.tensor.matmul(ps_st[s % 2][0:rows, q0:q0 + P], keep["ident_b"][:, :],
                                                      keep["mask_kv_b"][:, :], start=False, stop=True)
                            mm.then_inc(st_done, 1)
                        if s == 0:
                            pe.wait_ge(v_in[par], (n + 1) * VLOADS)
                            pe.wait_ge(o_read, u + 1)
                        if s >= LAG:
                            r = s - LAG
                            t, j = r // GH, r % GH
                            rows = tiles[t][1]
                            q0 = t * P if causal else 0
                            pe.wait_ge(exp_done, u * STEPS + r + 3)
                            nc.tensor.matmul(ps_o[par][j * VW:(j + 1) * VW, q0:SEQ],
                                             va[par][0:rows, t, j * VW:(j + 1) * VW],
                                             pr[0:rows, (par * STEPS + r) % RING, q0:SEQ], start=(t == 0), stop=(t == NT - 1))\
                              .then_inc(pv_done, 1)
                        if following:
                            if s == first_step:
                                pe.wait_ge(kq_in[ahead], (n_ahead + 1) * KQ)
                            if s < STEPS:
                                for k in piece_after(s):
                                    piece(u + 1, ahead, k)
                    if following:
                        turn_max(u + 1, ahead)

                pe.wait_ge(ones_set, 2)
                pe.wait_ge(kq_in[0], KQ)
                for k in range(NP):
                    piece(0, 0, k)
                turn_max(0, 0)
                with pe.Fori(0, units // 2 - 1) as i:
                    unit(i * 2, 0, i, True)
                    unit(i * 2 + 1, 1, i, True)
                unit(units - 2, 0, units // 2 - 1, True)
                unit(units - 1, 1, units // 2 - 1, False)

            @block.vector
            def _(dve):
                for i in range(2):
                    nc.vector.memset(kp[i][SROWS:MROWS, :, :], 1.0).then_inc(ones_set, 1)
                nc.vector.memset(nm_parts[:, 3:, :], 0.0)
                dve.sem_inc(s_read, 2)
                dve.sem_inc(o_read, 2)

                def maxima(u, par):
                    for k, (j, q, spans) in enumerate(pieces):
                        slot = (par * SLOTS + k) % 2
                        col, half = j * QT + q, k % PIECES
                        dve.wait_ge(s_done, u * SLOTS + k + 1)
                        nc.vector.tensor_reduce(nmax[:, col, half:half + 1], ps_s[slot][:, 0:len(spans), 0:spans[0][1]],
                                                AX.XY, ALU.max, negate=True).then_inc(s_read, 1)
                    dve.drain()
                    nc.vector.tensor_reduce(nm[:, :], nmax[:, :, :], AX.X, ALU.min)
                    dve.drain()
                    nc.vector.tensor_copy(nm_parts[:, 0, :], nm[:, :])
                    dve.drain()
                    nc.vector.tensor_tensor(nm_rest[:, :], nm[:, :], nm_parts[:, 0, :], ALU.subtract)
                    dve.drain()
                    nc.vector.tensor_copy(nm_parts[:, 1, :], nm_rest[:, :])
                    dve.drain()
                    nc.vector.tensor_tensor(nm_parts[:, 2, :], nm_rest[:, :], nm_parts[:, 1, :], ALU.subtract)\
                      .then_inc(m_split, 1)
                    dve.wait_ge(s_done, u * SLOTS + NP + 1)
                    dve.wait_ge(m_rows_in, u * 48 + 1)
                    slot = (par * SLOTS + NP) % 2
                    nc.vector.tensor_copy(nm_rows[:, :], ps_s[slot][0:3 * GH * QT, 0, 0:P // 2].bitcast(BF16))\
                      .then_inc(s_read, 1)

                def unit(u, par, n, following):
                    if following:
                        maxima(u + 1, (par + 1) % 2)
                    dve.wait_ge(pv_done, (u + 1) * STEPS + AHEAD)
                    dve.wait_ge(o_sent[par], (n + 1) * 16)
                    nc.vector.tensor_copy(ob[par][:, :], ps_o[par][:, :]).then_inc(o_read, 1)

                maxima(0, 0)
                with dve.Fori(0, units // 2 - 1) as i:
                    unit(i * 2, 0, i, True)
                    unit(i * 2 + 1, 1, i, True)
                unit(units - 2, 0, units // 2 - 1, True)
                unit(units - 1, 1, units // 2 - 1, False)

            @block.scalar
            def _(act):
                act.sem_inc(exp_done, 2)

                def unit(u, par):
                    for s in range(STEPS):
                        t = s // GH
                        rows = tiles[t][1]
                        q0 = t * P if causal else 0
                        N = u * STEPS + s
                        act.wait_ge(st_done, N + 1 + AHEAD)
                        act.wait_ge(pv_done, N + 1 + AHEAD - RING)
                        nc.scalar.activation(pr[0:rows, (par * STEPS + s) % RING, q0:SEQ], ps_st[s % 2][0:rows, q0:SEQ], ACT.Exp)\
                           .then_inc(exp_done, 1)

                assert 2 * STEPS % RING == 0
                with act.Fori(0, units // 2) as i:
                    for par in range(2):
                        unit(i * 2 + par, par)
        p.clear()


def invert_denominators(nc, out_rows, inverse, own, units):
    n = units * GH
    with ExitStack() as stack:
        p = Prog(nc, stack, "inv_self_" if own else "inv_cross_")
        den = p.sb("den", [n, SEQ])
        inv = p.sb("inv", [n, SEQ])
        den_in = p.sem("den_in")
        inv_ready = p.sem("inv_ready")
        inv_sent = p.sem("inv_sent")
        with nc.Block() as block:
            @block.sync
            def _(sp):
                src = out_rows.rearrange("u (j w) n -> u j w n", w=VW)[:, :, HD, :].rearrange("u j n -> (u j) n")
                sp.dma_start(den[:, :], src).then_inc(den_in, 16)
                sp.wait_ge(inv_ready, 1)
                sp.dma_start(inverse, inv[:, :]).then_inc(inv_sent, 16)
                sp.wait_ge(inv_sent, 16)

            @block.vector
            def _(dve):
                dve.wait_ge(den_in, 16)
                nc.vector.reciprocal(inv[:, :], den[:, :]).then_inc(inv_ready, 1)
        p.clear()




def load_attention_out(eng, out_rows, inverse, oT, inv, b, arrived):
    for u2 in range(2):
        for j in range(GH):
            r = (u2 * GH + j) * HD
            src = out_rows[bass.ds(b * GROUPS, GROUPS), j * VW:j * VW + HD, :]\
                .rearrange("(c u) d n -> u d c n", u=2)[u2]
            eng.dma_start(oT[r:r + HD, :, :], src).then_inc(arrived, 16)
            rows = inverse[bass.ds(b * HEADS, HEADS), :].rearrange("(c r) n -> r c n", c=KC)[u2 * GH + j]
            eng.dma_start(inv[r:r + HD, :, :], rows.partition_broadcast(HD)).then_inc(arrived, 16)


ATT_LOADS = 16 * 4 * GH


def project_self(nc, x_in, out_rows, inverse, x1_rows, h0_rows, q_parts, k_parts, v_rows, keep, batches):
    with ExitStack() as stack:
        p = Prog(nc, stack, "slf_")
        oT = p.sb("oT", [P, KC, SEQ])
        inv = p.sb("inv_rows", [P, KC, SEQ])
        on = p.sb("o_normed", [P, KC, SEQ])
        x = p.sb("x_rows", [P, QT, DIM])
        x1 = p.sb("x1", [P, QT, DIM])
        h0 = p.sb("h0", [P, QT, DIM])
        xr = p.sb("x_rms", [P, QT, DIM])
        stats = p.sb("ln_stats", [P, QT, 6])
        mv = p.sb("ln_mv", [P, QT, 2])
        std = p.sb("ln_std", [P, QT])
        rstd = p.sb("ln_rstd", [P, QT])
        ss = p.sb("rms_sum", [P, QT])
        rms = p.sb("rms", [P, QT])
        rrms = p.sb("rms_inv", [P, QT])
        junk = p.sb("squares", [P, DIM])
        xT = p.sb("xT", [P, KC, SEQ])
        t1 = p.sb("rope_cos", [P, KC, SEQ])
        t2 = p.sb("rope_sin", [P, KC, SEQ])
        full = p.sb("roped", [P, KC, SEQ])
        rest = p.sb("roped_rest", [P, KC, SEQ])
        parts = [[p.sb(f"roped_part{i}{a}", [P, KC, SEQ], BF16) for a in range(3)] for i in range(2)]
        vpad = p.sb("v_pad", [P, QT, HEADS, VW])
        ps_o = p.ps("ps_o", [P, QT, DIM])
        ps_t = p.ps("ps_t", [P, KC, SEQ])
        ps_a = p.ps("ps_a", [P, KC, SEQ])
        ps_b = p.ps("ps_b", [P, KC, SEQ])
        ins = p.sem("ins")
        on_ready = p.sem("on_ready")
        xb_ready = p.sem("xb_ready")
        o_done = p.sem("o_done")
        x1_ready = p.sem("x1_ready")
        mv_ready = p.sem("mv_ready")
        std_ready = p.sem("std_ready")
        h0_ready = p.sem("h0_ready")
        rms_ready = p.sem("rms_ready")
        rrms_ready = p.sem("rrms_ready")
        xr_ready = p.sem("xr_ready")
        turned = p.sem("turned")
        xT_ready = p.sem("xT_ready")
        rope_done = p.sem("rope_done")
        rope_read = p.sem("rope_read")
        full_ready = p.sem("full_ready")
        hi_ready = p.sem("hi_ready")
        rest_ready = p.sem("rest_ready")
        low_ready = p.sem("low_ready")
        mid_ready = p.sem("mid_ready")
        v_done = p.sem("v_done")
        v_ready = p.sem("v_ready")
        sent = [p.sem(f"sent{i}") for i in range(2)]
        rows_sent = p.sem("rows_sent")
        v_sent = p.sem("v_sent")
        pads = p.sem("pads")
        pool_turn = p.sem("pool_turn")
        SENT = 16 * 3 * KC

        with nc.Block() as block:
            @block.sync
            def _(sp):
                def load(b):
                    sp.wait_ge(on_ready, b + 1)
                    sp.wait_ge(x1_ready, b + 1)
                    load_attention_out(sp, out_rows, inverse, oT, inv, b, ins)
                    sp.dma_start(x[:, :, :], x_in[bass.ds(b * SEQ, SEQ), :].rearrange("(t p) d -> p t d", p=P))\
                      .then_inc(ins, 16)

                def store(b):
                    sp.wait_ge(h0_ready, b + 1)
                    for src, dst in ((x1, x1_rows), (h0, h0_rows)):
                        sp.dma_start(dst[bass.ds(b * SEQ, SEQ), :].rearrange("(t p) d -> p t d", p=P), src[:, :, :])\
                          .then_inc(rows_sent, 16)
                    for w, dst in enumerate((q_parts, k_parts)):
                        sp.wait_ge(low_ready, b * 2 + w + 2)
                        for a in range(3):
                            for i in range(KC):
                                sp.dma_start(dst[bass.ds(b * GROUPS + i * 2, 2), a, :, :],
                                             parts[w][a][:, i, :]).then_inc(sent[w], 16)
                    sp.wait_ge(v_ready, b + 1)
                    for g in range(GROUPS):
                        sp.dma_start(v_rows[b * GROUPS + g, :, :].rearrange("(t p) v -> p t v", p=P),
                                     vpad[:, :, g * GH:(g + 1) * GH, :].rearrange("p t h v -> p t (h v)"))\
                          .then_inc(v_sent, 16)

                for i in range(2):
                    sp.sem_inc(sent[i], SENT)
                sp.sem_inc(v_sent, 16 * GROUPS)
                sp.sem_inc(rows_sent, 32)
                sp.sem_inc(on_ready, 1)
                sp.sem_inc(x1_ready, 1)
                load(0)
                with sp.Fori(0, batches - 1) as b:
                    load(b + 1)
                    store(b)
                store(batches - 1)
                for i in range(2):
                    sp.wait_ge(sent[i], SENT * (batches + 1))
                sp.wait_ge(v_sent, 16 * GROUPS * (batches + 1))
                sp.wait_ge(rows_sent, 32 * (batches + 1))

            @block.tensor
            def _(pe):
                def out_product(b):
                    pe.wait_ge(on_ready, b + 2)
                    for t in range(QT):
                        for i in range(KC):
                            last = nc.tensor.matmul(ps_o[:, t, :], on[:, i, t * P:(t + 1) * P], keep["WoT"][:, i, :],
                                                    start=(i == 0), stop=(i == KC - 1))
                    last.then_inc(o_done, 1)

                def step(b, following):
                    pe.wait_ge(xr_ready, b + 1)
                    for t in range(QT):
                        for i in range(KC):
                            last = nc.tensor.transpose(ps_t[:, i, t * P:(t + 1) * P], xr[:, t, i * P:(i + 1) * P],
                                                       keep["ident"][:, :])
                    last.then_inc(turned, 1)
                    if following:
                        out_product(b + 1)
                    pe.wait_ge(xT_ready, b + 1)
                    for t in range(QT):
                        for i in range(KC):
                            last = nc.tensor.matmul(ps_t[:, t // 2, t % 2 * DIM:(t % 2 + 1) * DIM],
                                                    xT[:, i, t * P:(t + 1) * P],
                                                    keep["wv"][:, i, :], start=(i == 0), stop=(i == KC - 1))
                    last.then_inc(v_done, 1)
                    for w, (plain, rot) in enumerate((("wq", "wq_rot"), ("wk", "wk_rot"))):
                        pe.wait_ge(rope_read, b * 2 + w + 1)
                        for ps, weights in ((ps_a, plain), (ps_b, rot)):
                            for o in range(KC):
                                for i in range(KC):
                                    last = nc.tensor.matmul(ps[:, o, :], keep[weights][:, i, o * P:(o + 1) * P],
                                                            xT[:, i, :], start=(i == 0), stop=(i == KC - 1))
                        last.then_inc(rope_done, 1)
                    pe.wait_ge(v_ready, b + 1)

                out_product(0)
                with pe.Fori(0, batches - 1) as b:
                    step(b, True)
                step(batches - 1, False)

            @block.vector
            def _(dve):
                nc.vector.memset(vpad[:, :, :, HD:VW], 0.0)
                dve.drain()
                nc.vector.memset(vpad[:, :, :, HD:HD + 1], 1.0).then_inc(pads, 1)
                dve.sem_inc(rope_read, 1)

                def front(b):
                    dve.wait_ge(ins, (b + 1) * (ATT_LOADS + 16))
                    nc.vector.tensor_tensor(on[:, :, :], oT[:, :, :], inv[:, :, :], ALU.mult).then_inc(on_ready, 1)

                def middle(b):
                    dve.wait_ge(o_done, b + 1)
                    dve.wait_ge(xb_ready, b + 1)
                    dve.wait_ge(rows_sent, (b + 1) * 32)
                    nc.vector.tensor_tensor(x1[:, :, :], ps_o[:, :, :], x[:, :, :], ALU.add).then_inc(x1_ready, 1)
                    dve.drain()
                    for t in range(QT):
                        nc.vector.bn_stats(stats[:, t, :], x1[:, t, :])
                    dve.drain()
                    for t in range(QT):
                        last = nc.vector.bn_aggr(mv[:, t, :], stats[:, t, :])
                    last.then_inc(mv_ready, 1)
                    dve.wait_ge(std_ready, b + 1)
                    nc.vector.reciprocal(rstd[:, :], std[:, :])
                    dve.drain()
                    for t in range(QT):
                        last = nc.vector.tensor_scalar(h0[:, t, :], x1[:, t, :], mv[:, t, 0:1], rstd[:, t:t + 1],
                                                       ALU.subtract, ALU.mult)
                    last.then_inc(h0_ready, 1)
                    dve.wait_ge(rms_ready, b + 1)
                    nc.vector.reciprocal(rrms[:, :], rms[:, :]).then_inc(rrms_ready, 1)

                def back(b, following):
                    if following:
                        front(b + 1)
                    for w, part in enumerate(("q", "k")):
                        dve.wait_ge(rope_done, b * 2 + w + 1)
                        dve.wait_ge(full_ready, b * 2 + w + 1)
                        for i in range(KC):
                            nc.vector.tensor_tensor(t1[:, i, :], ps_a[:, i, :], keep["cos_" + part][:, :], ALU.mult)
                            last = nc.vector.tensor_tensor(t2[:, i, :], ps_b[:, i, :], keep["sin_" + part][:, :],
                                                           ALU.mult)
                        last.then_inc(rope_read, 1)
                        dve.wait_ge(hi_ready, b * 2 + w + 1)
                        dve.wait_ge(low_ready, b * 2 + w + 1)
                        nc.vector.tensor_tensor(rest[:, :, :], full[:, :, :], parts[w][0][:, :, :], ALU.subtract)\
                          .then_inc(rest_ready, 1)
                    if following:
                        middle(b + 1)

                front(0)
                middle(0)
                with dve.Fori(0, batches - 1) as b:
                    back(b, True)
                back(batches - 1, False)

            @block.scalar
            def _(act):
                def middle(b):
                    act.wait_ge(mv_ready, b + 1)
                    nc.scalar.activation(std[:, :], mv[:, :, 1], ACT.Sqrt, bias=keep["ln_eps"][:, :])\
                       .then_inc(std_ready, 1)
                    act.wait_ge(h0_ready, b + 1)
                    for t in range(QT):
                        nc.scalar.activation(junk[:, :], h0[:, t, :], ACT.Square, accum_out=ss[:, t:t + 1])
                        act.drain()
                    nc.scalar.activation(rms[:, :], ss[:, :], ACT.Sqrt, bias=keep["rms_eps"][:, :], scale=1.0 / DIM)\
                       .then_inc(rms_ready, 1)
                    act.wait_ge(rrms_ready, b + 1)
                    for t in range(QT):
                        last = nc.scalar.activation(xr[:, t, :], h0[:, t, :], ACT.Copy, scale=rrms[:, t:t + 1])
                    last.then_inc(xr_ready, 1)

                def back(b, following):
                    act.wait_ge(turned, b + 1)
                    for i in range(KC):
                        last = nc.scalar.activation(xT[:, i, :], ps_t[:, i, :], ACT.Copy, scale=keep["g1"][:, i:i + 1])
                    last.then_inc(xT_ready, 1)
                    act.wait_ge(pads, 1)
                    act.wait_ge(v_done, b + 1)
                    act.wait_ge(v_sent, (b + 1) * 16 * GROUPS)
                    for t in range(QT):
                        last = nc.scalar.copy(vpad[:, t, :, 0:HD],
                                              ps_t[:, t // 2, t % 2 * DIM:(t % 2 + 1) * DIM]
                                              .rearrange("p (h d) -> p h d", d=HD))
                    last.then_inc(v_ready, 1)
                    for w in range(2):
                        act.wait_ge(full_ready, b * 2 + w + 2)
                        act.wait_ge(sent[w], (b + 1) * SENT)
                        nc.scalar.copy(parts[w][0][:, :, :], full[:, :, :]).then_inc(hi_ready, 1)
                    if following:
                        middle(b + 1)

                middle(0)
                with act.Fori(0, batches - 1) as b:
                    back(b, True)
                back(batches - 1, False)

            @block.gpsimd
            def _(pool):
                pool.sem_inc(full_ready, 1)
                pool.sem_inc(low_ready, 1)
                def front(b):
                    pool.wait_ge(ins, (b + 1) * (ATT_LOADS + 16))
                    for t in range(QT):
                        last = nc.gpsimd.tensor_tensor(x[:, t, :], x[:, t, :], keep["bo"][:, :], ALU.add)
                    last.then_inc(xb_ready, 1)

                def back(b, following):
                    if following:
                        front(b + 1)
                    for w in range(2):
                        pool.wait_ge(rope_read, b * 2 + w + 2)
                        pool.wait_ge(rest_ready, b * 2 + w + 1)
                        nc.gpsimd.tensor_tensor(full[:, :, :], t1[:, :, :], t2[:, :, :], ALU.add)\
                          .then_inc(full_ready, 1)
                        pool.wait_ge(rest_ready, b * 2 + w + 2)
                        pool.sem_inc(pool_turn, 1)
                        nc.gpsimd.tensor_copy(parts[w][1][:, :, :], rest[:, :, :]).then_inc(mid_ready, 1)
                        pool.wait_ge(mid_ready, b * 2 + w + 1)
                        nc.gpsimd.tensor_tensor(parts[w][2][:, :, :], rest[:, :, :], parts[w][1][:, :, :],
                                                ALU.subtract).then_inc(low_ready, 1)

                pool.sem_inc(rest_ready, 1)
                front(0)
                with pool.Fori(0, batches - 1) as b:
                    back(b, True)
                back(batches - 1, False)
        p.clear()


def finish_self(nc, out_rows, inverse, x1_rows, h0_rows, y_rows, hn_rows, keep, batches):
    logits = keep["logits"]
    with ExitStack() as stack:
        p = Prog(nc, stack, "fin_")
        oT = p.sb("oT", [P, KC, SEQ])
        inv = p.sb("inv_rows", [P, KC, SEQ])
        on = p.sb("o_normed", [P, KC, SEQ])
        x1 = p.sb("x1", [P, QT, DIM])
        h0 = p.sb("h0", [P, QT, DIM])
        h = p.sb("h", [P, QT, DIM])
        y = p.sb("y", [P, QT, DIM])
        hr = p.sb("h_rms", [P, QT, DIM])
        hn = p.sb("h_normed", [P, QT, DIM])
        ss = p.sb("rms_sum", [P, QT])
        rms = p.sb("rms", [P, QT])
        rrms = p.sb("rms_inv", [P, QT])
        junk = p.sb("squares", [P, DIM])
        hT = p.sb("hT", [P, KC, SEQ])
        ps_o = p.ps("ps_o", [P, QT, DIM])
        ps_t = p.ps("ps_t", [P, KC, SEQ])
        ps_l = p.ps("ps_l", [P, QT, EXPERTS])
        ins = p.sem("ins")
        on_ready = p.sem("on_ready")
        o_done = p.sem("o_done")
        h_ready = p.sem("h_ready")
        y_ready = p.sem("y_ready")
        rms_ready = p.sem("rms_ready")
        rrms_ready = p.sem("rrms_ready")
        hr_ready = p.sem("hr_ready")
        hn_ready = p.sem("hn_ready")
        turned = p.sem("turned")
        hT_ready = p.sem("hT_ready")
        l_done = p.sem("l_done")
        l_ready = p.sem("l_ready")
        y_sent = p.sem("y_sent")
        hn_sent = p.sem("hn_sent")

        with nc.Block() as block:
            @block.sync
            def _(sp):
                def load(b):
                    sp.wait_ge(on_ready, b + 1)
                    sp.wait_ge(y_ready, b + 1)
                    load_attention_out(sp, out_rows, inverse, oT, inv, b, ins)
                    for src, dst in ((x1_rows, x1), (h0_rows, h0)):
                        sp.dma_start(dst[:, :, :], src[bass.ds(b * SEQ, SEQ), :].rearrange("(t p) d -> p t d", p=P))\
                          .then_inc(ins, 16)

                def store(b):
                    sp.wait_ge(y_ready, b + 2)
                    sp.dma_start(y_rows[bass.ds(b * SEQ, SEQ), :].rearrange("(t p) d -> p t d", p=P), y[:, :, :])\
                      .then_inc(y_sent, 16)
                    sp.wait_ge(hn_ready, b + 1)
                    sp.dma_start(hn_rows[bass.ds(b * SEQ, SEQ), :].rearrange("(t p) d -> p t d", p=P), hn[:, :, :])\
                      .then_inc(hn_sent, 16)

                sp.sem_inc(on_ready, 1)
                sp.sem_inc(y_ready, 1)
                sp.sem_inc(y_sent, 16)
                sp.sem_inc(hn_sent, 16)
                load(0)
                with sp.Fori(0, batches - 1) as b:
                    load(b + 1)
                    store(b)
                store(batches - 1)
                sp.wait_ge(y_sent, 16 * (batches + 1))
                sp.wait_ge(hn_sent, 16 * (batches + 1))

            @block.tensor
            def _(pe):
                with pe.Fori(0, batches) as b:
                    pe.wait_ge(on_ready, b + 2)
                    for t in range(QT):
                        for i in range(KC):
                            last = nc.tensor.matmul(ps_o[:, t, :], on[:, i, t * P:(t + 1) * P], keep["wo"][:, i, :],
                                                    start=(i == 0), stop=(i == KC - 1))
                    last.then_inc(o_done, 1)
                    pe.wait_ge(hn_ready, b + 1)
                    for t in range(QT):
                        for i in range(KC):
                            last = nc.tensor.transpose(ps_t[:, i, t * P:(t + 1) * P], hn[:, t, i * P:(i + 1) * P],
                                                       keep["ident"][:, :])
                    last.then_inc(turned, 1)
                    pe.wait_ge(hT_ready, b + 1)
                    for t in range(QT):
                        for i in range(KC):
                            last = nc.tensor.matmul(ps_l[:, t, :], hT[:, i, t * P:(t + 1) * P],
                                                    keep["w_router"][:, i, :], start=(i == 0), stop=(i == KC - 1))
                    last.then_inc(l_done, 1)

            @block.vector
            def _(dve):
                def front(b):
                    dve.wait_ge(ins, (b + 1) * (ATT_LOADS + 32))
                    nc.vector.tensor_tensor(on[:, :, :], oT[:, :, :], inv[:, :, :], ALU.mult).then_inc(on_ready, 1)

                def step(b, following):
                    dve.wait_ge(o_done, b + 1)
                    dve.wait_ge(y_ready, b + 1)
                    nc.vector.tensor_tensor(h[:, :, :], ps_o[:, :, :], h0[:, :, :], ALU.add).then_inc(h_ready, 1)
                    dve.wait_ge(rms_ready, b + 1)
                    nc.vector.reciprocal(rrms[:, :], rms[:, :]).then_inc(rrms_ready, 1)
                    if following:
                        front(b + 1)
                    dve.wait_ge(l_done, b + 1)
                    nc.vector.tensor_copy(logits[:, bass.ds(b * QT, QT), :], ps_l[:, :, :]).then_inc(l_ready, 1)

                front(0)
                with dve.Fori(0, batches - 1) as b:
                    step(b, True)
                step(batches - 1, False)

            @block.scalar
            def _(act):
                with act.Fori(0, batches) as b:
                    act.wait_ge(h_ready, b + 1)
                    for t in range(QT):
                        nc.scalar.activation(junk[:, :], h[:, t, :], ACT.Square, accum_out=ss[:, t:t + 1])
                        act.drain()
                    nc.scalar.activation(rms[:, :], ss[:, :], ACT.Sqrt, bias=keep["rms_eps"][:, :], scale=1.0 / DIM)\
                       .then_inc(rms_ready, 1)
                    act.wait_ge(rrms_ready, b + 1)
                    for t in range(QT):
                        last = nc.scalar.activation(hr[:, t, :], h[:, t, :], ACT.Copy, scale=rrms[:, t:t + 1])
                    last.then_inc(hr_ready, 1)
                    act.wait_ge(turned, b + 1)
                    nc.scalar.copy(hT[:, :, :], ps_t[:, :, :]).then_inc(hT_ready, 1)

            @block.gpsimd
            def _(pool):
                with pool.Fori(0, batches) as b:
                    pool.wait_ge(h_ready, b + 1)
                    pool.wait_ge(y_sent, (b + 1) * 16)
                    nc.gpsimd.tensor_tensor(y[:, :, :], x1[:, :, :], h[:, :, :], ALU.add).then_inc(y_ready, 1)
                    pool.wait_ge(hr_ready, b + 1)
                    pool.wait_ge(hn_sent, (b + 1) * 16)
                    for t in range(QT):
                        last = nc.gpsimd.tensor_tensor(hn[:, t, :], hr[:, t, :], keep["g2"][:, :], ALU.mult)
                    last.then_inc(hn_ready, 1)
        p.clear()




def route(nc, keep, tokens):
    T = tokens // P
    E = EXPERTS
    TILES = 2 * T + E
    logits, slots, weights, expert = keep["logits"], keep["slots"], keep["pair_weights"], keep["tile_expert"]
    with ExitStack() as stack:
        p = Prog(nc, stack, "route_")
        probs = p.sb("probs", [P, T, E])
        work = p.sb("work", [P, T, E])
        chosen = p.sb("chosen", [P, T, E], BF16)
        first = p.sb("first_choice", [P, T, E])
        second = p.sb("second_choice", [P, T, E])
        row = p.sb("row_max", [P, T])
        left = p.sb("left", [P, T])
        top = [p.sb(f"top{i}", [P, T]) for i in range(2)]
        run = [p.sb(f"run{i}", [P, T, E]) for i in range(2)]
        place = p.sb("place", [P, T, E])
        compare = p.sb("compare", [P, E, 64])
        used = p.sb("used_tiles", [P, E])
        begin = p.sb("begin", [P, E])
        end = p.sb("end", [P, E])
        pairs = p.sb("pairs", [P, E, E])
        tile_cmp = p.sb("tile_cmp", [P, 96, E])
        tile_f = p.sb("tile_f", [P, 96])
        slot_f = p.sb("slot_f", [P, 2, T])
        ones = p.sb("ones", [P, P], BF16)
        ps_rank = p.ps("ps_rank", [P, T, E])
        ps_total = p.ps("ps_total", [P, T, E])
        shifted = p.sem("shifted")
        exp_ready = p.sem("exp_ready")
        chosen_ready = p.sem("chosen_ready")
        ranks_done = p.sem("ranks_done")
        routed = p.sem("routed")

        def over_e(a, n=T):
            return a.unsqueeze(2).broadcast_to([P, n, E])

        left_of = keep["iota_left"][:, :].unsqueeze(1).broadcast_to([P, T, E])

        with nc.Block() as block:
            @block.vector
            def _(dve):
                def tt(out, a, b, op):
                    nc.vector.tensor_tensor(out, a, b, op)
                    dve.drain()

                def reduce(out, a, op):
                    nc.vector.tensor_reduce(out, a, AX.X, op)
                    dve.drain()

                nc.vector.memset(ones[:, :], 1.0)
                reduce(row[:, :], logits[:, :, :], ALU.max)
                nc.vector.tensor_tensor(work[:, :, :], logits[:, :, :], over_e(row[:, :]), ALU.subtract)\
                  .then_inc(shifted, 1)
                dve.wait_ge(exp_ready, 1)
                reduce(row[:, :], probs[:, :, :], ALU.add)
                nc.vector.reciprocal(left[:, :], row[:, :])
                dve.drain()
                tt(probs[:, :, :], probs[:, :, :], over_e(left[:, :]), ALU.mult)
                for k, pick in enumerate((first, second)):
                    reduce(top[k][:, :], probs[:, :, :], ALU.max)
                    tt(work[:, :, :], probs[:, :, :], over_e(top[k][:, :]), ALU.is_equal)
                    tt(work[:, :, :], work[:, :, :], left_of, ALU.mult)
                    reduce(left[:, :], work[:, :, :], ALU.max)
                    tt(pick[:, :, :], over_e(left[:, :]), left_of, ALU.is_equal)
                    if k == 0:
                        nc.vector.scalar_tensor_tensor(out=probs[:, :, :], in0=pick[:, :, :], scalar=-2.0,
                                                       in1=probs[:, :, :], op0=ALU.mult, op1=ALU.add)
                        dve.drain()
                nc.vector.tensor_tensor(chosen[:, :, :], first[:, :, :], second[:, :, :], ALU.add)\
                  .then_inc(chosen_ready, 1)
                tt(row[:, :], top[0][:, :], top[1][:, :], ALU.add)
                nc.vector.reciprocal(left[:, :], row[:, :])
                dve.drain()
                for k in range(2):
                    tt(weights[:, k, :], top[k][:, :], left[:, :], ALU.mult)
                dve.wait_ge(ranks_done, 1)
                nc.vector.tensor_copy(run[0][:, :, :], ps_total[:, :, :])
                dve.drain()
                src, step = 0, 1
                while step < T:
                    a, b = run[src], run[1 - src]
                    nc.vector.tensor_copy(b[:, 0:step, :], a[:, 0:step, :])
                    tt(b[:, step:T, :], a[:, step:T, :], a[:, 0:T - step, :], ALU.add)
                    src, step = 1 - src, step * 2
                total = run[src]
                n = T + 1
                tt(compare[:, :, 0:n], total[:, T - 1, :].unsqueeze(2).broadcast_to([P, E, n]),
                   keep["iota_count"][:, 0:n].unsqueeze(1).broadcast_to([P, E, n]), ALU.is_gt)
                reduce(used[:, :], compare[:, :, 0:n], ALU.add)
                tt(pairs[:, :, :], used[:, :].unsqueeze(1).broadcast_to([P, E, E]),
                   keep["lt8"][:, :].rearrange("p (a b) -> p a b", b=E), ALU.mult)
                reduce(begin[:, :], pairs[:, :, :], ALU.add)
                tt(end[:, :], begin[:, :], used[:, :], ALU.add)
                tt(tile_cmp[:, 0:TILES, :], over_e(keep["iota_tile"][:, 0:TILES], TILES),
                   end[:, :].unsqueeze(1).broadcast_to([P, TILES, E]), ALU.is_ge)
                reduce(tile_f[:, 0:TILES], tile_cmp[:, 0:TILES, :], ALU.add)
                nc.vector.tensor_scalar(expert[:, 0:TILES], tile_f[:, 0:TILES], E - 1.0, None, ALU.min)
                tt(place[:, :, :], total[:, :, :], ps_total[:, :, :], ALU.subtract)
                tt(place[:, :, :], place[:, :, :], ps_rank[:, :, :], ALU.add)
                nc.vector.scalar_tensor_tensor(out=place[:, :, :], in0=begin[:, :].unsqueeze(1).broadcast_to([P, T, E]),
                                               scalar=float(P), in1=place[:, :, :], op0=ALU.mult, op1=ALU.add)
                dve.drain()
                for k, pick in enumerate((first, second)):
                    tt(work[:, :, :], pick[:, :, :], place[:, :, :], ALU.mult)
                    reduce(slot_f[:, k, :], work[:, :, :], ALU.add)
                nc.vector.tensor_copy(slots[:, :, :], slot_f[:, :, :]).then_inc(routed, 1)
                dve.wait_ge(routed, 1)

            @block.scalar
            def _(act):
                act.wait_ge(shifted, 1)
                nc.scalar.activation(probs[:, :, :], work[:, :, :], ACT.Exp).then_inc(exp_ready, 1)

            @block.tensor
            def _(pe):
                pe.wait_ge(chosen_ready, 1)
                nc.tensor.matmul(ps_rank[:, :, :].rearrange("p t e -> p (t e)"), keep["before_b"][:, :],
                                 chosen[:, :, :].rearrange("p t e -> p (t e)"), start=True, stop=True)
                nc.tensor.matmul(ps_total[:, :, :].rearrange("p t e -> p (t e)"), ones[:, :],
                                 chosen[:, :, :].rearrange("p t e -> p (t e)"), start=True, stop=True)\
                  .then_inc(ranks_done, 1)
        p.clear()


def scatter_rows(nc, hn_rows, in_sorted, keep, tokens):
    T = tokens // P
    slots = keep["slots"]
    with ExitStack() as stack:
        p = Prog(nc, stack, "scat_")
        rows = [p.sb(f"token_rows{i}", [P, DIM]) for i in range(4)]
        index = [p.sb(f"index{i}", [P, 2], I32) for i in range(4)]
        rows_in = [p.sem(f"rows_in{i}") for i in range(4)]
        index_ready = p.sem("index_ready")
        gone = [p.sem(f"gone{i}") for i in range(4)]
        done = p.sem("done")
        pool_turn = p.sem("pool_turn")
        with nc.Block() as block:
            @block.sync
            def _(sp):
                sp.sem_inc(done, 4)
                with sp.Fori(0, T // 4) as i:
                    for k in range(4):
                        sp.wait_ge(done, i * 4 + k + 1)
                        sp.dma_start(rows[k][:, :], hn_rows[bass.ds((i * 4 + k) * P, P), :]).then_inc(rows_in[k], 16)

            @block.gpsimd
            def _(pool):
                with pool.Fori(0, T // 4) as i:
                    for k in range(4):
                        nc.gpsimd.tensor_copy(index[k][:, :], slots[:, :, bass.ds(i * 4 + k, 1)]
                                              .rearrange("p k o -> p (k o)")).then_inc(index_ready, 1)
                    for k in range(4):
                        pool.wait_ge(rows_in[k], (i + 1) * 16)
                        pool.wait_ge(index_ready, i * 4 + 4)
                        pool.sem_inc(pool_turn, 1)
                        for c in range(2):
                            pool.indirect_dma_start(
                                out=in_sorted, out_offset=bass.IndirectOffsetOnAxis(ap=index[k][:, c:c + 1], axis=0),
                                in_=rows[k][:, :], in_offset=None).then_inc(gone[k], 16)
                    for k in range(4):
                        pool.wait_ge(gone[k], (i + 1) * 32)
                        pool.sem_inc(done, 1)
        p.clear()


def experts(nc, in_sorted, out_sorted, w, keep, tiles):
    HALVES = 2
    CH = -(-HHALF // P)
    CW = [min(P, HHALF - c * P) for c in range(CH)]
    with ExitStack() as stack:
        p = Prog(nc, stack, "moe_")
        rows = [p.sb(f"rows{i}", [P, DIM]) for i in range(2)]
        xT = [p.sb(f"rowsT{i}", [P, KC, P]) for i in range(2)]
        sil = [p.sb(f"silu{i}", [P, HHALF]) for i in range(2)]
        h = [p.sb(f"hidden{i}", [P, HHALF]) for i in range(2)]
        hT = [p.sb(f"hiddenT{i}", [P, CH, P]) for i in range(2)]
        y = [p.sb(f"y{i}", [P, DIM]) for i in range(2)]
        ps_g = [p.ps(f"ps_g{i}", [P, SEQ]) for i in range(2)]
        ps_u = [p.ps(f"ps_u{i}", [P, SEQ]) for i in range(2)]
        ps_h = [p.ps(f"ps_h{i}", [P, CH, P]) for i in range(2)]
        ps_x = p.ps("ps_x", [P, KC, P])
        ps_y = p.ps("ps_y", [P, DIM])
        rows_in = [p.sem(f"rows_in{i}") for i in range(2)]
        turned = p.sem("turned")
        xT_ready = p.sem("xT_ready")
        gu_done = p.sem("gu_done")
        sil_ready = p.sem("sil_ready")
        h_ready = p.sem("h_ready")
        h_turned = p.sem("h_turned")
        hT_ready = p.sem("hT_ready")
        down_done = p.sem("down_done")
        y_ready = p.sem("y_ready")
        sent = [p.sem(f"sent{i}") for i in range(2)]
        weights_in = keep["weights_in"]

        with nc.Block() as block:
            @block.sync
            def _(sp):
                sp.sem_inc(turned, 2)
                for i in range(2):
                    sp.sem_inc(sent[i], 16)

                def load(t, par):
                    sp.wait_ge(turned, t + 1)
                    sp.dma_start(rows[par][:, :], in_sorted[bass.ds(t * P, P), :]).then_inc(rows_in[par], 16)

                def store(t, par):
                    sp.wait_ge(y_ready, t + 2)
                    sp.dma_start(out_sorted[bass.ds(t * P, P), :], y[par][:, :]).then_inc(sent[par], 16)

                load(0, 0)
                load(1, 1)
                with sp.Fori(0, tiles // 2 - 1) as i:
                    for par in range(2):
                        load(i * 2 + par + 2, par)
                        store(i * 2 + par, par)
                store(tiles - 2, 0)
                store(tiles - 1, 1)
                for i in range(2):
                    sp.wait_ge(sent[i], 16 * (tiles // 2 + 1))

            @block.tensor
            def _(pe):
                pe.sem_inc(h_turned, 2)
                pe.sem_inc(down_done, 1)
                pe.wait_ge(weights_in, keep["weights_total"])
                wg, wu, wd = keep["wg_sb"], keep["wu_sb"], keep["wd_sb"]

                def turn_rows(t, par, n):
                    pe.wait_ge(rows_in[par], (n + 1) * 16)
                    pe.wait_ge(xT_ready, t + 1)
                    for i in range(KC):
                        last = nc.tensor.transpose(ps_x[:, i, :], rows[par][:, i * P:(i + 1) * P],
                                                   keep["ident"][:, :])
                    last.then_inc(turned, 1)

                def gate_up(t, par, half, e):
                    if half == 0:
                        pe.wait_ge(xT_ready, t + 2)
                    pe.wait_ge(h_ready, t * 2 + half + 1)
                    for ps, wt in ((ps_g, wg), (ps_u, wu)):
                        for i in range(KC):
                            at = e * (KC * HIDDEN) + i * HIDDEN + half * HHALF
                            last = nc.tensor.matmul(ps[half][:, 0:HHALF], xT[par][:, i, :],
                                                    wt[:, bass.ds(at, HHALF)], start=(i == 0), stop=(i == KC - 1))
                    last.then_inc(gu_done, 1)

                def turn_hidden(t, half):
                    pe.wait_ge(h_ready, t * 2 + half + 3)
                    pe.wait_ge(hT_ready, t * 2 + half + 1)
                    for c in range(CH):
                        last = nc.tensor.transpose(ps_h[half][0:CW[c], c, :], h[half][:, c * P:c * P + CW[c]],
                                                   keep["ident"][:, :])
                    last.then_inc(h_turned, 1)

                def down(t, e):
                    pe.wait_ge(y_ready, t + 1)
                    for half in range(HALVES):
                        pe.wait_ge(hT_ready, t * 2 + half + 3)
                        for c in range(CH):
                            at = e * (HALVES * CH * DIM) + (half * CH + c) * DIM
                            last = nc.tensor.matmul(ps_y[:, :], hT[half][0:CW[c], c, :],
                                                    wd[0:CW[c], bass.ds(at, DIM)],
                                                    start=(half == 0 and c == 0), stop=(half == 1 and c == CH - 1))
                    last.then_inc(down_done, 1)

                with pe.Fori(0, tiles // 2) as i:
                    a, b = i * 2, i * 2 + 1
                    ea = pe.value_load(keep["tile_expert"][0:1, bass.ds(a, 1)], min_val=0, max_val=EXPERTS - 1)
                    eb = pe.value_load(keep["tile_expert"][0:1, bass.ds(b, 1)], min_val=0, max_val=EXPERTS - 1)
                    turn_rows(a, 0, i)
                    gate_up(a, 0, 0, ea)
                    turn_rows(b, 1, i)
                    gate_up(a, 0, 1, ea)
                    turn_hidden(a, 0)
                    gate_up(b, 1, 0, eb)
                    turn_hidden(a, 1)
                    gate_up(b, 1, 1, eb)
                    down(a, ea)
                    turn_hidden(b, 0)
                    turn_hidden(b, 1)
                    down(b, eb)

            @block.scalar
            def _(act):
                act.sem_inc(xT_ready, 1)
                act.sem_inc(y_ready, 1)

                def turned_rows(t, par):
                    act.wait_ge(turned, t + 3)
                    nc.scalar.copy(xT[par][:, :, :], ps_x[:, :, :]).then_inc(xT_ready, 1)

                def silu(t, half):
                    act.wait_ge(gu_done, t * 2 + half + 1)
                    act.wait_ge(h_ready, t * 2 + half + 1)
                    nc.scalar.activation(sil[half][:, :], ps_g[half][:, 0:HHALF], ACT.Silu).then_inc(sil_ready, 1)

                def result(t, par, n):
                    act.wait_ge(down_done, t + 2)
                    act.wait_ge(sent[par], (n + 1) * 16)
                    nc.scalar.copy(y[par][:, :], ps_y[:, :]).then_inc(y_ready, 1)

                with act.Fori(0, tiles // 2) as i:
                    a, b = i * 2, i * 2 + 1
                    turned_rows(a, 0)
                    silu(a, 0)
                    turned_rows(b, 1)
                    silu(a, 1)
                    silu(b, 0)
                    silu(b, 1)
                    result(a, 0, i)
                    result(b, 1, i)

            @block.vector
            def _(dve):
                dve.sem_inc(h_ready, 2)
                dve.sem_inc(hT_ready, 2)

                def multiply(t, half):
                    dve.wait_ge(sil_ready, t * 2 + half + 1)
                    dve.wait_ge(h_turned, t * 2 + half + 1)
                    nc.vector.tensor_tensor(h[half][:, :], ps_u[half][:, 0:HHALF], sil[half][:, :], ALU.mult)\
                      .then_inc(h_ready, 1)

                def turned_hidden(t, half):
                    dve.wait_ge(h_turned, t * 2 + half + 3)
                    dve.wait_ge(down_done, t + 1)
                    nc.vector.tensor_copy(hT[half][:, 0:CH - 1, :], ps_h[half][:, 0:CH - 1, :])
                    nc.vector.tensor_copy(hT[half][0:CW[-1], CH - 1, :], ps_h[half][0:CW[-1], CH - 1, :])\
                      .then_inc(hT_ready, 1)

                with dve.Fori(0, tiles // 2) as i:
                    a, b = i * 2, i * 2 + 1
                    multiply(a, 0)
                    multiply(a, 1)
                    turned_hidden(a, 0)
                    multiply(b, 0)
                    turned_hidden(a, 1)
                    multiply(b, 1)
                    turned_hidden(b, 0)
                    turned_hidden(b, 1)
        p.clear()


def combine(nc, out_sorted, y_rows, out, keep, tokens):
    T = tokens // P
    slots, weights = keep["slots"], keep["pair_weights"]
    D = 4
    with ExitStack() as stack:
        p = Prog(nc, stack, "comb_")
        index = [p.sb(f"index{i}", [P, 2], I32) for i in range(D)]
        wt = [p.sb(f"pair{i}", [P, 2]) for i in range(D)]
        r = [[p.sb(f"row{i}{c}", [P, DIM]) for c in range(2)] for i in range(D)]
        y = [p.sb(f"y{i}", [P, DIM]) for i in range(D)]
        y_in = [p.sem(f"y_in{i}") for i in range(D)]
        index_ready = p.sem("index_ready")
        pool_turn = p.sem("pool_turn")
        got = [p.sem(f"got{i}") for i in range(D)]
        summed = p.sem("summed")
        sent = [p.sem(f"sent{i}") for i in range(D)]
        with nc.Block() as block:
            @block.sync
            def _(sp):
                for k in range(D):
                    sp.sem_inc(sent[k], 16)
                with sp.Fori(0, T // D) as i:
                    for k in range(D):
                        sp.wait_ge(sent[k], (i + 1) * 16)
                        sp.dma_start(y[k][:, :], y_rows[bass.ds((i * D + k) * P, P), :]).then_inc(y_in[k], 16)
                    for k in range(D):
                        sp.wait_ge(summed, i * D + k + 1 + D)
                        sp.dma_start(out[bass.ds((i * D + k) * P, P), :], y[k][:, :]).then_inc(sent[k], 16)
                for k in range(D):
                    sp.wait_ge(sent[k], 16 * (T // D + 1))

            @block.gpsimd
            def _(pool):
                with pool.Fori(0, T // D) as i:
                    for k in range(D):
                        pool.wait_ge(summed, i * D + k + 1)
                        pool.sem_inc(index_ready, 1)
                        nc.gpsimd.tensor_copy(wt[k][:, :], weights[:, :, bass.ds(i * D + k, 1)]
                                              .rearrange("p k o -> p (k o)"))
                        nc.gpsimd.tensor_copy(index[k][:, :], slots[:, :, bass.ds(i * D + k, 1)]
                                              .rearrange("p k o -> p (k o)")).then_inc(index_ready, 1)
                    for k in range(D):
                        pool.wait_ge(index_ready, i * 2 * D + 2 * D)
                        pool.sem_inc(pool_turn, 1)
                        for c in range(2):
                            pool.indirect_dma_start(
                                out=r[k][c][:, :], out_offset=None, in_=out_sorted,
                                in_offset=bass.IndirectOffsetOnAxis(ap=index[k][:, c:c + 1], axis=0))\
                                .then_inc(got[k], 16)

            @block.vector
            def _(dve):
                dve.sem_inc(summed, D)
                with dve.Fori(0, T // D) as i:
                    for k in range(D):
                        dve.wait_ge(got[k], (i + 1) * 32)
                        dve.wait_ge(y_in[k], (i + 1) * 16)
                        dve.wait_ge(index_ready, i * 2 * D + 2 * D)
                        nc.vector.scalar_tensor_tensor(out=y[k][:, :], in0=r[k][0][:, :], scalar=wt[k][:, 0:1],
                                                       in1=y[k][:, :], op0=ALU.mult, op1=ALU.add)
                        dve.drain()
                        nc.vector.scalar_tensor_tensor(out=y[k][:, :], in0=r[k][1][:, :], scalar=wt[k][:, 1:2],
                                                       in1=y[k][:, :], op0=ALU.mult, op1=ALU.add)\
                          .then_inc(summed, 1)
        p.clear()




def shape_constants():
    import numpy as np
    i = np.arange(P)
    later = (i[None, :] > i[:, None]).astype(np.float32) * np.float32(MASKED)
    t = np.arange(SEQ, dtype=np.float32)
    inv_freq = 1.0 / 10000.0 ** (np.arange(0, HD, 2, dtype=np.float32) / HD)
    angle = np.einsum("i,j->ij", t, inv_freq.astype(np.float32)).astype(np.float32)
    cos = np.tile(np.cos(angle).T, (P // (HD // 2), 1)).astype(np.float32)
    sin = np.tile(np.sin(angle).T, (P // (HD // 2), 1)).astype(np.float32)
    e = np.arange(EXPERTS, dtype=np.float32)
    out = {
        "ident": np.eye(P, dtype=np.float32),
        "mask_q": later,
        "mask_kv": np.ascontiguousarray(later.T),
        "before": (i[:, None] < i[None, :]).astype(np.float32),
        "cos_q": cos * np.float32(SCALE), "sin_q": sin * np.float32(SCALE), "cos_k": cos, "sin_k": sin,
        "iota_left": np.tile(EXPERTS - e, (P, 1)),
        "iota_tile": np.tile(np.arange(96, dtype=np.float32), (P, 1)),
        "iota_count": np.tile(np.arange(64, dtype=np.float32) * P, (P, 1)),
        "lt8": np.tile((e[None, :] < e[:, None]).astype(np.float32).reshape(1, -1), (P, 1)),
    }
    return {k: np.ascontiguousarray(v, dtype=np.float32) for k, v in out.items()}


def load_experts(nc, a, in_sorted, keep, p, tiles):
    E, CH = EXPERTS, -(-HHALF // P)
    keep["wg_sb"] = p.sb("wg_sb", [P, E * KC * HIDDEN])
    keep["wu_sb"] = p.sb("wu_sb", [P, E * KC * HIDDEN])
    keep["wd_sb"] = p.sb("wd_sb", [P, E * 2 * CH * DIM])
    keep["weights_in"] = p.sem("weights_in")
    zeros = p.sb("zeros", [P, DIM])
    zeroed = p.sem("zeroed")
    zeros_set = p.sem("zeros_set")
    count = 0
    with nc.Block() as block:
        @block.vector
        def _(dve):
            nc.vector.memset(zeros[:, :], 0.0).then_inc(zeros_set, 1)

        @block.sync
        def _(sp):
            for e in range(E):
                for n in ("wg", "wu"):
                    sp.dma_start(keep[n + "_sb"][:, e * KC * HIDDEN:(e + 1) * KC * HIDDEN]
                                 .rearrange("p (c n) -> p c n", n=HIDDEN),
                                 a[n][e].rearrange("(c p) n -> p c n", p=P)).then_inc(keep["weights_in"], 16)
                for half in range(2):
                    at = (e * 2 + half) * CH * DIM
                    full = HHALF // P
                    sp.dma_start(keep["wd_sb"][:, at:at + full * DIM].rearrange("p (c n) -> p c n", n=DIM),
                                 a["wd"][e, half * HHALF:half * HHALF + full * P, :]
                                 .rearrange("(c p) n -> p c n", p=P)).then_inc(keep["weights_in"], 16)
                    rest = HHALF - full * P
                    sp.dma_start(keep["wd_sb"][0:rest, at + full * DIM:at + CH * DIM],
                                 a["wd"][e, half * HHALF + full * P:(half + 1) * HHALF, :])\
                      .then_inc(keep["weights_in"], 16)

        @block.scalar
        def _(act):
            act.wait_ge(zeros_set, 1)
            with act.Fori(0, tiles) as t:
                act.dma_start(in_sorted[bass.ds(t * P, P), :], zeros[:, :]).then_inc(zeroed, 16)
            act.wait_ge(zeroed, 16 * tiles)
    keep["weights_total"] = 16 * E * 6


KEEP_SHAPES = {"WqT": 0, "WkT": 0, "WvT": 0, "WoT": 0, "wq": 0, "wk": 0, "wv": 0, "wo": 0, "wq_rot": 0, "wk_rot": 0}


def build(nc, a, out, batches=8):
    units = batches * GROUPS
    dram = lambda name, shape, dt=F32: nc.dram_tensor(name, shape, dt, kind="Internal").ap()
    k_parts = dram("k_parts", [units, 3, GR, CTX], BF16)
    q_parts = dram("q_parts", [units, 3, GR, SEQ], BF16)
    v_rows = dram("v_rows", [units, CTX, GH * VW])
    out_rows = dram("out_rows", [units, P, SEQ])
    inverse = dram("inverse", [units * GH, SEQ])
    k2_parts = dram("k2_parts", [units, 3, GR, SEQ], BF16)
    q2_parts = dram("q2_parts", [units, 3, GR, SEQ], BF16)
    v2_rows = dram("v2_rows", [units, SEQ, GH * VW])
    out2_rows = dram("out2_rows", [units, P, SEQ])
    inverse2 = dram("inverse2", [units * GH, SEQ])
    tokens = batches * SEQ
    x1_rows = dram("x1_rows", [tokens, DIM])
    h0_rows = dram("h0_rows", [tokens, DIM])
    y_rows = dram("y_rows", [tokens, DIM])
    hn_rows = dram("hn_rows", [tokens, DIM])
    tiles = 2 * tokens // P + EXPERTS
    in_sorted = dram("in_sorted", [tiles * P, DIM])
    out_sorted = dram("out_sorted", [tiles * P, DIM])
    with ExitStack() as stack:
        p = Prog(nc, stack, "top_")
        keep = {n: p.sb(f"keep_{n}", [P, KC, DIM]) for n in KEEP_SHAPES}
        for n, w in (("ident", P), ("mask_q", P), ("mask_kv", P), ("before", P), ("cos_q", SEQ), ("sin_q", SEQ),
                     ("cos_k", SEQ), ("sin_k", SEQ), ("iota_left", EXPERTS), ("iota_tile", 96), ("iota_count", 64),
                     ("lt8", EXPERTS * EXPERTS), ("bq", KC), ("bk", KC), ("g1", KC), ("bv", DIM), ("bo", DIM),
                     ("g2", DIM), ("ln_eps", 1), ("rms_eps", 1)):
            keep[n] = p.sb(f"keep_{n}", [P, w])
        for n in ("ident", "mask_q", "mask_kv", "before"):
            keep[n + "_b"] = p.sb(f"keep_{n}_b", [P, P], BF16)
        keep["w_router"] = p.sb("keep_w_router", [P, KC, EXPERTS])
        prepare_weights(nc, a, keep)
        project_context(nc, a["ctx"], k_parts, v_rows, keep, batches)
        project_queries(nc, a["x"], q_parts, keep, batches)
        attention(nc, q_parts, k_parts, v_rows, out_rows, CTX, False, keep, units)
        invert_denominators(nc, out_rows, inverse, False, units)
        project_self(nc, a["x"], out_rows, inverse, x1_rows, h0_rows, q2_parts, k2_parts, v2_rows, keep, batches)
        attention(nc, q2_parts, k2_parts, v2_rows, out2_rows, SEQ, True, keep, units)
        invert_denominators(nc, out2_rows, inverse2, True, units)
        keep["logits"] = p.sb("logits", [P, tokens // P, EXPERTS])
        keep["slots"] = p.sb("slots", [P, 2, tokens // P], I32)
        keep["pair_weights"] = p.sb("pair_weights", [P, 2, tokens // P])
        keep["tile_expert"] = p.sb("tile_expert", [P, tiles], I32)
        finish_self(nc, out2_rows, inverse2, x1_rows, h0_rows, y_rows, hn_rows, keep, batches)
        route(nc, keep, tokens)
        load_experts(nc, a, in_sorted, keep, p, tiles)
        scatter_rows(nc, hn_rows, in_sorted, keep, tokens)
        experts(nc, in_sorted, out_sorted, a, keep, tiles)
        combine(nc, out_sorted, y_rows, out, keep, tokens)


WEIGHTS = {n: f"L0_xattn_{n}" for n in ("Wq", "bq", "Wk", "bk", "Wv", "bv", "Wo", "bo")}
WEIGHTS.update({n: f"L0_ffn_{n}" for n in ("wq", "wk", "wv", "wo", "w_router", "wg", "wu", "wd", "g1", "g2")})


def kernel(**inputs):
    import numpy as _np
    import concourse.bacc as _bacc
    from concourse import mybir as _mybir
    from concourse.bass_utils import run_bass_kernel_spmd as _run

    x = _np.ascontiguousarray(inputs["x"])
    data = {"x": x.reshape(-1, DIM), "ctx": _np.ascontiguousarray(inputs["ctx_1024"]).reshape(-1, DIM)}
    data.update({n: _np.ascontiguousarray(inputs[full]) for n, full in WEIGHTS.items()})
    data.update(shape_constants())
    nc = _bacc.Bacc("TRN2", target_bir_lowering=False, num_devices=1)
    arrays, args = {}, {}
    for n, v in data.items():
        arrays[f"in_{n}_dram"] = v
        args[n] = nc.dram_tensor(f"in_{n}_dram", v.shape, _mybir.dt.from_np(v.dtype), kind="ExternalInput").ap()
    out = nc.dram_tensor("out_dram", data["x"].shape, _mybir.dt.from_np(x.dtype), kind="ExternalOutput").ap()
    build(nc, args, out, x.shape[0])
    got = _run(nc, [arrays], core_ids=[0]).results[0]["out_dram"]
    return got.reshape(x.shape)
```

```python
import concourse.bass as bass
from concourse import mybir
from contextlib import ExitStack

F32 = mybir.dt.float32
BF16 = mybir.dt.bfloat16
I32 = mybir.dt.int32
U32 = mybir.dt.uint32
ALU = mybir.AluOpType
ACT = mybir.ActivationFunctionType
AX = mybir.AxisListType

P = 128
DIM = 256
KC = DIM // P
HEADS = 16
HD = DIM // HEADS
GH = 4
GROUPS = HEADS // GH
GR = GH * HD
SEQ = 512
QT = SEQ // P
CTX = 1601
EXPERTS = 8
HIDDEN = 704
HC = -(-HIDDEN // P)
HLAST = HIDDEN - (HC - 1) * P
HHALF = HIDDEN // 2
SCALE = HD ** -0.5
MASKED = -1e30
LN_EPS = 1e-5
RMS_EPS = 1e-6

K_PARTS = (0, 1, 2, 0, 1, 0)
Q_PARTS = (0, 0, 0, 1, 1, 2)
PAIRS = len(K_PARTS)
SROWS = PAIRS * HD
MROWS = SROWS + 3
VW = 32


class Prog:

    def __init__(self, nc, stack, stage):
        self.nc, self.stack, self.stage, self.sems = nc, stack, stage, []

    def sb(self, name, shape, dt=F32):
        return self.stack.enter_context(self.nc.sbuf_tensor(self.stage + name, shape, dt))

    def ps(self, name, shape, dt=F32):
        return self.stack.enter_context(self.nc.psum_tensor(self.stage + name, shape, dt))

    def sem(self, name):
        self.sems.append(self.stack.enter_context(self.nc.semaphore(self.stage + name)))
        return self.sems[-1]

    def clear(self):
        for s in self.sems:
            self.nc.sync.sem_clear(s)
        self.nc.all_engine_barrier()


def prepare_weights(nc, w, keep):
    with ExitStack() as stack:
        p = Prog(nc, stack, "prep_")
        raw = {n: p.sb(f"raw_{n}", [P, KC, DIM]) for n in ("Wq", "Wk", "Wv", "Wo")}
        turned = [p.ps(f"turned{i}", [P, KC, DIM]) for i in range(4)]
        consts_in = p.sem("consts_in")
        raw_in = p.sem("raw_in")
        small_in = p.sem("small_in")
        turned_ready = p.sem("turned_ready")
        turned_kept = p.sem("turned_kept")
        rot_ready = p.sem("rot_ready")

        with nc.Block() as block:
            @block.sync
            def _(sp):
                for name in ("ident", "mask_q", "mask_kv", "before", "cos_q", "sin_q", "cos_k", "sin_k",
                             "iota_left", "iota_tile", "iota_count", "lt8"):
                    sp.dma_start(keep[name][:, :], w[name]).then_inc(consts_in, 16)
                for n in ("Wq", "Wk", "Wv", "Wo"):
                    sp.dma_start(raw[n][:, :, :], w[n].rearrange("(c p) i -> p c i", p=P)).then_inc(raw_in, 16)
                sp.wait_ge(consts_in, 16 * 12)

            @block.scalar
            def _(act):
                for n in ("bq", "bk", "g1"):
                    act.dma_start(keep[n][:, :], w[n].rearrange("(c p) -> p c", p=P),
                                  allow_slow_non_contiguous=True).then_inc(small_in, 16)
                for n in ("bv", "bo", "g2"):
                    act.dma_start(keep[n][:, :], w[n].partition_broadcast(P)).then_inc(small_in, 16)
                for n in ("wq", "wk", "wv", "wo"):
                    act.dma_start(keep[n][:, :, :], w[n].rearrange("(c p) o -> p c o", p=P)).then_inc(small_in, 16)
                act.dma_start(keep["w_router"][:, :, :], w["w_router"].rearrange("(c p) e -> p c e", p=P))\
                   .then_inc(small_in, 16)
                act.wait_ge(small_in, 16 * 11)
                nc.scalar.mul(keep["bq"][:, :], keep["bq"][:, :], SCALE)
                for src, dst in (("wq", "wq_rot"), ("wk", "wk_rot")):
                    s = keep[src][:, :, :].rearrange("p c (h t d) -> p (c h) t d", t=2, d=HD // 2)
                    d = keep[dst][:, :, :].rearrange("p c (h t d) -> p (c h) t d", t=2, d=HD // 2)
                    nc.scalar.mul(d[:, :, 0, :], s[:, :, 1, :], -1.0)
                    last = nc.scalar.copy(d[:, :, 1, :], s[:, :, 0, :])
                last.then_inc(rot_ready, 1)
                act.wait_ge(rot_ready, 1)

            @block.tensor
            def _(pe):
                pe.wait_ge(consts_in, 16 * 12)
                pe.wait_ge(raw_in, 16 * 4)
                for k, n in enumerate(("Wq", "Wk", "Wv", "Wo")):
                    for i in range(KC):
                        for o in range(KC):
                            last = nc.tensor.transpose(turned[k][:, i, o * P:(o + 1) * P],
                                                       raw[n][:, o, i * P:(i + 1) * P], keep["ident"][:, :])
                    last.then_inc(turned_ready, 1)

            @block.vector
            def _(dve):
                nc.vector.memset(keep["ln_eps"][:, :], LN_EPS)
                nc.vector.memset(keep["rms_eps"][:, :], RMS_EPS)
                for k, n in enumerate(("WqT", "WkT", "WvT", "WoT")):
                    dve.wait_ge(turned_ready, k + 1)
                    nc.vector.tensor_copy(keep[n][:, :, :], turned[k][:, :, :])
                dve.wait_ge(consts_in, 16 * 12)
                for n in ("ident", "mask_q", "mask_kv", "before"):
                    last = nc.vector.tensor_copy(keep[n + "_b"][:, :], keep[n][:, :])
                last.then_inc(turned_kept, 1)
                dve.wait_ge(turned_kept, 1)
        p.clear()


def turns(eng, steps, parts):
    deep = max(lag for lag, _ in parts)
    for t in range(deep):
        for lag, part in parts:
            if t >= lag:
                part(t - lag)
    with eng.Fori(0, steps - deep) as i:
        for lag, part in parts:
            part(i + (deep - lag))
    for t in range(steps, steps + deep):
        for lag, part in parts:
            if t - lag < steps:
                part(t - lag)


class Norms:

    def __init__(self, p):
        self.stats = p.sb("norm_stats", [P, QT, 6])
        self.mv = p.sb("norm_mean_var", [P, QT, 2])
        self.std = p.sb("norm_std", [P, QT])
        self.rstd = p.sb("norm_std_inv", [P, QT])
        self.stats2 = p.sb("norm_stats2", [P, QT, 6])
        self.mv2 = p.sb("norm_mean_var2", [P, QT, 2])
        self.square = p.sb("norm_mean2", [P, QT])
        self.ms = p.sb("norm_mean_square", [P, QT])
        self.rms = p.sb("norm_rms", [P, QT])
        self.rrms = p.sb("norm_rms_inv", [P, QT])

    def sums(self, nc, dve, rows, stats, mv):
        for t in range(QT):
            nc.vector.bn_stats(stats[:, t, :], rows[:, t, :])
        dve.drain()
        for t in range(QT):
            last = nc.vector.bn_aggr(mv[:, t, :], stats[:, t, :])
        return last

    def moments(self, nc, dve, rows):
        return self.sums(nc, dve, rows, self.stats, self.mv)

    def mean_square(self, nc, dve, rows):
        self.sums(nc, dve, rows, self.stats2, self.mv2)
        dve.drain()
        nc.vector.tensor_tensor(self.square[:, :], self.mv2[:, :, 0], self.mv2[:, :, 0], ALU.mult)
        dve.drain()
        return nc.vector.tensor_tensor(self.ms[:, :], self.square[:, :], self.mv2[:, :, 1], ALU.add)


def with_next(eng, batches, N, body, ahead=1):
    def at(b, c):
        return (b + c // N, c % N)

    with eng.Fori(0, batches - 1) as b:
        for c in range(N):
            body((b, c), at(b, c + ahead))
    for c in range(N):
        body((batches - 1, c), (batches - 1, c + ahead) if c + ahead < N else None)


def project_context(nc, ctx_in, k_parts, v_rows, keep, batches):
    chunks = [(o, min(SEQ, CTX - o)) for o in range(0, CTX, SEQ)]
    N = len(chunks)
    assert N == 4
    with ExitStack() as stack:
        p = Prog(nc, stack, "ctx_")
        rows = [p.sb(f"ctx_rows{i}", [P, QT, DIM]) for i in range(N)]
        xT = [p.sb(f"ctxT{i}", [P, KC, SEQ]) for i in range(2)]
        kf = [p.sb(f"k_full{i}", [P, KC, SEQ]) for i in range(2)]
        rest = [p.sb(f"k_rest{i}", [P, KC, SEQ]) for i in range(2)]
        parts = [[p.sb(f"k_part{i}{a}", [P, KC, SEQ], BF16) for a in range(3)] for i in range(N)]
        vpad = [p.sb(f"v_pad{i}", [P, QT, HEADS, VW]) for i in range(2)]
        ps_t = [p.ps(f"ps_t{i}", [P, KC, SEQ]) for i in range(2)]
        ps_k = p.ps("ps_k", [P, KC, SEQ])
        ps_v = p.ps("ps_v", [P, QT, DIM])
        rows_in = [p.sem(f"rows_in{i}") for i in range(N)]
        v_sent = [p.sem(f"v_sent{i}") for i in range(2)]
        k_sent = [p.sem(f"k_sent{i}") for i in range(N)]
        turned = p.sem("turned")
        xT_ready = p.sem("xT_ready")
        k_done = p.sem("k_done")
        v_done = p.sem("v_done")
        k_hi = p.sem("k_hi")
        v_ready = p.sem("v_ready")
        rest_ready = p.sem("rest_ready")
        mid_ready = p.sem("mid_ready")
        low_ready = p.sem("low_ready")
        pads = p.sem("pads")
        pool_turn = p.sem("pool_turn")
        KSENT = 16 * 3 * KC
        VSENT = 16 * GROUPS

        def tiles(n):
            return [(t, min(P, n - t * P)) for t in range(-(-n // P))]

        with nc.Block() as block:
            @block.sync
            def _(sp):
                for s in v_sent:
                    sp.sem_inc(s, VSENT)
                for s in k_sent:
                    sp.sem_inc(s, KSENT)

                def load(b, c):
                    o, n = chunks[c]
                    src = ctx_in[bass.ds(b * CTX + o, n), :]
                    if n >= P:
                        sp.dma_start(rows[c][:, 0:n // P, :], src.rearrange("(t p) d -> p t d", p=P))\
                          .then_inc(rows_in[c], 16)
                    else:
                        sp.dma_start(rows[c][0:n, 0, :], src).then_inc(rows_in[c], 16)

                def step(now, later):
                    b, c = now
                    (o, n), par = chunks[c], c % 2
                    if later:
                        sp.wait_ge(turned, b * N + c + 1)
                        load(*later)
                    sp.wait_ge(v_ready, b * N + c + 2)
                    for g in range(GROUPS):
                        dst = v_rows[b * GROUPS + g, o:o + n, :]
                        if n >= P:
                            sp.dma_start(dst.rearrange("(t p) v -> p t v", p=P),
                                         vpad[par][:, 0:n // P, g * GH:(g + 1) * GH, :]
                                         .rearrange("p t h v -> p t (h v)")).then_inc(v_sent[par], 16)
                        else:
                            sp.dma_start(dst, vpad[par][0:n, 0, g * GH:(g + 1) * GH, :]
                                         .rearrange("p h v -> p (h v)")).then_inc(v_sent[par], 16)
                    sp.wait_ge(low_ready, b * N + c + 3)
                    for a in range(3):
                        for i in range(KC):
                            sp.dma_start(k_parts[bass.ds(b * GROUPS + i * 2, 2), a, :, o:o + n],
                                         parts[c][a][:, i, 0:n]).then_inc(k_sent[c], 16)

                for c in range(N):
                    load(0, c)
                with_next(sp, batches, N, step, ahead=N)
                for s in v_sent:
                    sp.wait_ge(s, VSENT * (batches * (N // 2) + 1))
                for s in k_sent:
                    sp.wait_ge(s, KSENT * (batches + 1))

            @block.tensor
            def _(pe):
                pe.sem_inc(k_done, 2)

                def turn(b, c):
                    n = chunks[c][1]
                    pe.wait_ge(rows_in[c], (b + 1) * 16)
                    pe.wait_ge(xT_ready, b * N + c + 1)
                    for t, m in tiles(n):
                        for i in range(KC):
                            last = nc.tensor.transpose(ps_t[c % 2][:, i, t * P:t * P + m],
                                                       rows[c][0:m, t, i * P:(i + 1) * P],
                                                       keep["ident"][0:m, 0:m])
                    last.then_inc(turned, 1)

                def step(now, later):
                    b, c = now
                    (o, n), par, S = chunks[c], c % 2, b * N + c
                    if later:
                        turn(*later)
                    pe.wait_ge(xT_ready, S + 3)
                    pe.wait_ge(k_hi, S + 1)
                    for o2 in range(KC):
                        for i in range(KC):
                            last = nc.tensor.matmul(ps_k[:, o2, 0:n], keep["WkT"][:, i, o2 * P:(o2 + 1) * P],
                                                    xT[par][:, i, 0:n], start=(i == 0), stop=(i == KC - 1))
                    last.then_inc(k_done, 1)
                    pe.wait_ge(v_ready, S + 1)
                    for t, m in tiles(n):
                        for i in range(KC):
                            last = nc.tensor.matmul(ps_v[0:m, t, :], xT[par][:, i, t * P:t * P + m],
                                                    keep["WvT"][:, i, :], start=(i == 0), stop=(i == KC - 1))
                    last.then_inc(v_done, 1)

                turn(0, 0)
                with_next(pe, batches, N, step)

            @block.vector
            def _(dve):
                for i in range(2):
                    nc.vector.memset(vpad[i][:, :, :, HD:VW], 0.0).then_inc(pads, 1)
                dve.wait_ge(pads, 2)
                for i in range(2):
                    nc.vector.memset(vpad[i][:, :, :, HD:HD + 1], 1.0).then_inc(pads, 1)
                dve.wait_ge(pads, 4)
                dve.sem_inc(xT_ready, 2)
                dve.sem_inc(v_ready, 1)
                dve.sem_inc(rest_ready, 2)

                def copy(b, c):
                    n = chunks[c][1]
                    dve.wait_ge(turned, b * N + c + 1)
                    dve.wait_ge(k_done, b * N + c + 1)
                    nc.vector.tensor_copy(xT[c % 2][:, :, 0:n], ps_t[c % 2][:, :, 0:n]).then_inc(xT_ready, 1)

                def step(now, later):
                    b, c = now
                    (o, n), par, S = chunks[c], c % 2, b * N + c
                    if later:
                        copy(*later)
                    dve.wait_ge(k_hi, S + 2)
                    dve.wait_ge(low_ready, S + 1)
                    nc.vector.tensor_tensor(rest[par][:, :, 0:n], kf[par][:, :, 0:n], parts[c][0][:, :, 0:n],
                                            ALU.subtract).then_inc(rest_ready, 1)
                    dve.wait_ge(v_done, S + 1)
                    dve.wait_ge(v_sent[par], (b * (N // 2) + c // 2 + 1) * VSENT)
                    for t, m in tiles(n):
                        last = nc.vector.tensor_tensor(vpad[par][0:m, t, :, 0:HD],
                                                       ps_v[0:m, t, :].rearrange("p (h d) -> p h d", d=HD),
                                                       keep["bv"][0:m, :].rearrange("p (h d) -> p h d", d=HD), ALU.add)
                    last.then_inc(v_ready, 1)

                copy(0, 0)
                with_next(dve, batches, N, step)

            @block.scalar
            def _(act):
                act.sem_inc(k_hi, 1)
                with act.Fori(0, batches) as b:
                    for c, (o, n) in enumerate(chunks):
                        S, par = b * N + c, c % 2
                        act.wait_ge(k_done, S + 3)
                        act.wait_ge(rest_ready, S + 1)
                        act.wait_ge(k_sent[c], (b + 1) * KSENT)
                        for i in range(KC):
                            nc.scalar.activation(kf[par][:, i, 0:n], ps_k[:, i, 0:n], ACT.Identity,
                                                 bias=keep["bk"][:, i:i + 1])
                            last = nc.scalar.activation(parts[c][0][:, i, 0:n], ps_k[:, i, 0:n], ACT.Identity,
                                                        bias=keep["bk"][:, i:i + 1])
                        last.then_inc(k_hi, 1)

            @block.gpsimd
            def _(pool):
                pool.sem_inc(low_ready, 2)
                with pool.Fori(0, batches) as b:
                    for c, (o, n) in enumerate(chunks):
                        S, par = b * N + c, c % 2
                        pool.wait_ge(rest_ready, S + 3)
                        pool.sem_inc(pool_turn, 1)
                        nc.gpsimd.tensor_copy(parts[c][1][:, :, 0:n], rest[par][:, :, 0:n]).then_inc(mid_ready, 1)
                        pool.wait_ge(mid_ready, S + 1)
                        nc.gpsimd.tensor_tensor(parts[c][2][:, :, 0:n], rest[par][:, :, 0:n],
                                                parts[c][1][:, :, 0:n], ALU.subtract).then_inc(low_ready, 1)
        p.clear()




def project_queries(nc, x_in, q_parts, keep, batches):
    with ExitStack() as stack:
        p = Prog(nc, stack, "qry_")
        rows = p.sb("x_rows", [P, QT, DIM])
        normed = p.sb("x_normed", [P, QT, DIM])
        norm = Norms(p)
        xT = p.sb("xT", [P, KC, SEQ])
        full = p.sb("q_full", [P, KC, SEQ])
        rest = p.sb("q_rest", [P, KC, SEQ])
        parts = [p.sb(f"q_part{a}", [P, KC, SEQ], BF16) for a in range(3)]
        ps_t = p.ps("ps_t", [P, KC, SEQ])
        ps_q = p.ps("ps_q", [P, KC, SEQ])
        rows_in = p.sem("rows_in")
        high_sent = p.sem("high_sent")
        low_sent = p.sem("low_sent")
        mv_ready = p.sem("mv_ready")
        std_ready = p.sem("std_ready")
        norm_ready = p.sem("norm_ready")
        turned = p.sem("turned")
        xT_ready = p.sem("xT_ready")
        q_done = p.sem("q_done")
        q_hi = p.sem("q_hi")
        rest_ready = p.sem("rest_ready")
        mid_ready = p.sem("mid_ready")
        low_ready = p.sem("low_ready")
        pool_turn = p.sem("pool_turn")

        with nc.Block() as block:
            @block.sync
            def _(sp):
                sp.sem_inc(high_sent, 16 * KC)
                sp.sem_inc(low_sent, 16 * KC * 2)

                def load(b):
                    sp.wait_ge(norm_ready, b + 1)
                    sp.dma_start(rows[:, :, :], x_in[bass.ds(b * SEQ, SEQ), :].rearrange("(t p) d -> p t d", p=P))\
                      .then_inc(rows_in, 16)

                def store(a, b, sem):
                    for i in range(KC):
                        sp.dma_start(q_parts[bass.ds(b * GROUPS + i * 2, 2), a, :, :], parts[a][:, i, :])\
                          .then_inc(sem, 16)

                def store_high(b):
                    sp.wait_ge(q_hi, b + 2)
                    store(0, b, high_sent)

                def store_low(b):
                    sp.wait_ge(mid_ready, b + 1)
                    store(1, b, low_sent)
                    sp.wait_ge(low_ready, b + 2)
                    store(2, b, low_sent)

                turns(sp, batches, ((0, load), (2, store_high), (3, store_low)))
                sp.wait_ge(high_sent, 16 * KC * (batches + 1))
                sp.wait_ge(low_sent, 16 * KC * 2 * (batches + 1))

            @block.tensor
            def _(pe):
                pe.sem_inc(turned, 1)
                pe.sem_inc(q_done, 1)

                def turn_rows(b):
                    pe.wait_ge(norm_ready, b + 2)
                    for t in range(QT):
                        for i in range(KC):
                            last = nc.tensor.transpose(ps_t[:, i, t * P:(t + 1) * P],
                                                       normed[:, t, i * P:(i + 1) * P], keep["ident"][:, :])
                    last.then_inc(turned, 1)

                def product(b):
                    pe.wait_ge(xT_ready, b + 1)
                    pe.wait_ge(q_hi, b + 1)
                    for o in range(KC):
                        for i in range(KC):
                            last = nc.tensor.matmul(ps_q[:, o, :], keep["WqT"][:, i, o * P:(o + 1) * P],
                                                    xT[:, i, :], start=(i == 0), stop=(i == KC - 1))
                    last.then_inc(q_done, 1)

                turns(pe, batches, ((1, product), (0, turn_rows)))

            @block.vector
            def _(dve):
                dve.sem_inc(norm_ready, 1)
                dve.sem_inc(rest_ready, 1)

                def moments(b):
                    dve.wait_ge(rows_in, (b + 1) * 16)
                    norm.moments(nc, dve, rows).then_inc(mv_ready, 1)

                def normalise(b):
                    dve.wait_ge(std_ready, b + 1)
                    nc.vector.reciprocal(norm.rstd[:, :], norm.std[:, :])
                    dve.drain()
                    dve.wait_ge(turned, b + 1)
                    for t in range(QT):
                        last = nc.vector.tensor_scalar(normed[:, t, :], rows[:, t, :], norm.mv[:, t, 0:1],
                                                       norm.rstd[:, t:t + 1], ALU.subtract, ALU.mult)
                    last.then_inc(norm_ready, 1)

                def take_turned(b):
                    dve.wait_ge(turned, b + 2)
                    dve.wait_ge(q_done, b + 1)
                    nc.vector.tensor_copy(xT[:, :, :], ps_t[:, :, :]).then_inc(xT_ready, 1)

                def subtract_high(b):
                    dve.wait_ge(q_hi, b + 2)
                    dve.wait_ge(low_ready, b + 1)
                    nc.vector.tensor_tensor(rest[:, :, :], full[:, :, :], parts[0][:, :, :], ALU.subtract)\
                      .then_inc(rest_ready, 1)

                turns(dve, batches, ((1, take_turned), (0, moments), (2, subtract_high), (0, normalise)))

            @block.scalar
            def _(act):
                act.sem_inc(q_hi, 1)

                def deviation(b):
                    act.wait_ge(mv_ready, b + 1)
                    nc.scalar.activation(norm.std[:, :], norm.mv[:, :, 1], ACT.Sqrt, bias=keep["ln_eps"][:, :])\
                       .then_inc(std_ready, 1)

                def high(b):
                    act.wait_ge(q_done, b + 2)
                    act.wait_ge(rest_ready, b + 1)
                    act.wait_ge(high_sent, (b + 1) * 16 * KC)
                    for i in range(KC):
                        nc.scalar.activation(full[:, i, :], ps_q[:, i, :], ACT.Identity,
                                             bias=keep["bq"][:, i:i + 1], scale=SCALE)
                        last = nc.scalar.activation(parts[0][:, i, :], ps_q[:, i, :], ACT.Identity,
                                                    bias=keep["bq"][:, i:i + 1], scale=SCALE)
                    last.then_inc(q_hi, 1)

                turns(act, batches, ((2, high), (0, deviation)))

            @block.gpsimd
            def _(pool):
                pool.sem_inc(low_ready, 1)

                def split(b):
                    pool.wait_ge(rest_ready, b + 2)
                    pool.wait_ge(low_sent, (b + 1) * 16 * KC * 2)
                    pool.sem_inc(pool_turn, 1)
                    nc.gpsimd.tensor_copy(parts[1][:, :, :], rest[:, :, :]).then_inc(mid_ready, 1)
                    pool.wait_ge(mid_ready, b + 1)
                    nc.gpsimd.tensor_tensor(parts[2][:, :, :], rest[:, :, :], parts[1][:, :, :],
                                            ALU.subtract).then_inc(low_ready, 1)

                turns(pool, batches, ((0, split),))
        p.clear()


def attention(nc, q_parts, k_parts, v_rows, out_rows, kv, causal, keep, units, beside=None):
    tiles = [(t, min(P, kv - t * P)) for t in range(-(-kv // P))]
    NT = len(tiles)
    STEPS = NT * GH
    RING = 8
    LAG = 4
    BUFS = 4
    VBUFS = 4 if causal else 2
    if causal:
        pieces = [(j, q, [(0, (q + 1) * P)]) for j in range(GH) for q in range(QT)]
        PIECES = 1
    else:
        span = -(-kv // 4)
        starts = [min(i * (kv // 4), kv - span) for i in range(4)]
        pieces = [(j, q, [(s, span) for s in starts[h * 2:h * 2 + 2]])
                  for j in range(GH) for q in range(QT) for h in range(2)]
        PIECES = 2
    NP = len(pieces)
    SLOTS = NP + 1
    TAIL = min(STEPS - 2, 15)
    KT = 3
    step_of = [STEPS - TAIL + int((k - NP) * STEPS / NP) for k in range(NP)]
    EARLY = sum(s < 0 for s in step_of)
    assert EARLY > KT and (units - 4) % 4 == 0
    with ExitStack() as stack:
        p = Prog(nc, stack, "att_self_" if causal else "att_cross_")
        kp = [p.sb(f"k_pack{i}", [P, GH, kv], BF16) for i in range(BUFS)]
        qp = [p.sb(f"q_pack{i}", [P, GH, SEQ], BF16) for i in range(BUFS)]
        va = [p.sb(f"v_tiles{i}", [P, NT, GH * VW]) for i in range(VBUFS)]
        pr = p.sb("probs", [P, RING, SEQ])
        nmax = [p.sb(f"neg_max{i}", [P, GH * QT, PIECES]) for i in range(2)]
        nm = p.sb("neg_max_merged", [P, GH * QT])
        nm_rest = p.sb("neg_max_rest", [P, GH * QT])
        nm_parts = p.sb("neg_max_parts", [P, P // (GH * QT), GH * QT], BF16)
        nm_rows = p.sb("neg_max_rows", [3 * GH * QT, P], BF16)
        ob = [p.sb(f"out_buf{i}", [P, SEQ]) for i in range(2)]
        ps_s = [p.ps(f"ps_s{i}", [P, 2, SEQ]) for i in range(2)]
        ps_st = [p.ps(f"ps_st{i}", [P, SEQ]) for i in range(3)]
        ps_o = p.ps("ps_o", [P, SEQ])
        ones_set = p.sem("ones_set")
        kq_in = [p.sem(f"kq_in{i}") for i in range(BUFS)]
        v_in = [p.sem(f"v_in{i}") for i in range(VBUFS)]
        m_rows_in = p.sem("m_rows_in")
        st_done = p.sem("st_done")
        exp_done = p.sem("exp_done")
        pv_done = p.sem("pv_done")
        s_done = p.sem("s_done")
        s_read = p.sem("s_read")
        m_merged = p.sem("m_merged")
        m_step = p.sem("m_step")
        m_split = p.sem("m_split")
        m_read = p.sem("m_read")
        pool_turn = p.sem("pool_turn")
        o_read = p.sem("o_read")
        o_sent = [p.sem(f"o_sent{i}") for i in range(2)]
        KQ = 16 * 2 * PAIRS
        VLOADS = 16 * ((1 if kv >= P else 0) + (1 if kv % P else 0))

        bank_of_step = [s % 3 for s in range(STEPS - 1)] + [1]
        assert STEPS % 3 == 1

        def bank_age(s):
            return next(d for d in range(1, 6) if bank_of_step[(s - d) % STEPS] == bank_of_step[s])

        class Unit:

            def __init__(self, i, r):
                self.i, self.r = i, r
                self.n = i * 4 + r
                self.odd = r % 2
                self.buf = r % BUFS
                self.vbuf = r % VBUFS

            def next(self, d):
                return Unit(self.i, self.r + d)

            def loads(self, bufs):
                return self.i * (4 // bufs) + self.r // bufs + 1

        def turn(v, k):
            return v.n * SLOTS + (k + (k >= KT) - 1)

        def bank_of(v, k):
            return (v.r * SLOTS + k + (k >= KT) - 1) % 2

        def bank_of_max(v, last):
            return ((v.r + 1) * SLOTS - 1 + (0 if last else KT)) % 2

        def in_order(u, after):
            out = []
            if after >= 1:
                out += [(step_of[k], "piece", u.next(1), k) for k in range(EARLY, NP)]
                out.append((step_of[NP - 1], "split", u.next(1), 0))
                if after >= 2:
                    out += [(step_of[k] + STEPS, "piece", u.next(2), k) for k in range(KT)]
                out.append((step_of[KT] + STEPS, "turn", u.next(1), int(after < 2)))
                if after >= 2:
                    out += [(step_of[k] + STEPS, "piece", u.next(2), k) for k in range(KT, EARLY)]
            return out

        def before_all():
            u0 = Unit(0, 0)
            out = [(0, "piece0", u0, k) for k in range(NP)] + [(0, "split", u0, 0)]
            out += [(0, "piece", u0.next(1), k) for k in range(KT)] + [(0, "turn", u0, 0)]
            return out + [(0, "piece", u0.next(1), k) for k in range(KT, EARLY)]

        with nc.Block() as block:
            @block.sync
            def _(sp):
                def load_kq(v):
                    for r in range(PAIRS):
                        sp.dma_start(kp[v.buf][r * HD:(r + 1) * HD, :, :],
                                     k_parts[v.n, K_PARTS[r], :, :].rearrange("(j d) n -> d j n", d=HD))\
                          .then_inc(kq_in[v.buf], 16)
                        sp.dma_start(qp[v.buf][r * HD:(r + 1) * HD, :, :],
                                     q_parts[v.n, Q_PARTS[r], :, :].rearrange("(j d) n -> d j n", d=HD))\
                          .then_inc(kq_in[v.buf], 16)

                def load_v(v):
                    if kv >= P:
                        sp.dma_start(va[v.vbuf][:, 0:kv // P, :],
                                     v_rows[v.n, 0:kv // P * P, :].rearrange("(t p) v -> p t v", p=P))\
                          .then_inc(v_in[v.vbuf], 16)
                    if kv % P:
                        sp.dma_start(va[v.vbuf][0:kv % P, kv // P, :], v_rows[v.n, kv // P * P:kv, :])\
                          .then_inc(v_in[v.vbuf], 16)

                def send_out(v):
                    sp.wait_ge(o_read, v.n + 2)
                    sp.dma_start(out_rows[v.n, :, :], ob[v.odd][:, :]).then_inc(o_sent[v.odd], 16)

                def unit(u, after, before=True):
                    if after >= VBUFS - 1:
                        if before:
                            sp.wait_ge(pv_done, u.n * STEPS + RING)
                        load_v(u.next(VBUFS - 1))
                    if after >= 3:
                        if before:
                            sp.wait_ge(st_done, u.n * STEPS + RING)
                        load_kq(u.next(3))
                    if before:
                        send_out(u.next(-1))

                for k in range(2):
                    sp.sem_inc(o_sent[k], 16)
                for r in range(3):
                    load_kq(Unit(0, r))
                for r in range(VBUFS - 1):
                    load_v(Unit(0, r))
                unit(Unit(0, 0), units - 1, False)
                with sp.Fori(0, units // 4 - 1) as i:
                    for r in range(1, 5):
                        unit(Unit(i, r), 3)
                for r in range(1, 4):
                    unit(Unit(units // 4 - 1, r), 3 - r)
                send_out(Unit(units // 4 - 1, 3))
                for k in range(2):
                    sp.wait_ge(o_sent[k], 16 * (units // 2 + 1))

            @block.tensor
            def _(pe):
                pe.sem_inc(st_done, RING)
                pe.sem_inc(pv_done, RING)

                def maxima(what, v, k):
                    if what in ("piece", "piece0"):
                        j, q, spans = pieces[k]
                        bank = bank_of(v, k) if what == "piece" else k % 2
                        if k == 0:
                            pe.wait_ge(kq_in[v.buf], v.loads(BUFS) * KQ)
                        if what == "piece" and k == KT + 1:
                            pe.wait_ge(m_read, v.n)
                        else:
                            pe.wait_ge(s_read, v.n * NP + (k + 1 + (what == "piece" and k == KT)))
                        for n, (s, w) in enumerate(spans):
                            last = nc.tensor.matmul(ps_s[bank][:, n, 0:w], qp[v.buf][0:SROWS, j, q * P:(q + 1) * P],
                                                    kp[v.buf][0:SROWS, j, s:s + w], start=True, stop=not causal)
                            if causal:
                                last = nc.tensor.matmul(ps_s[bank][:, n, w - P:w], keep["ident_b"][:, :],
                                                        keep["mask_q_b"][:, :], start=False, stop=True)
                        last.then_inc(s_done, 1)
                    elif what == "turn":
                        pe.wait_ge(s_read, (v.n + 1) * NP + (1 if k else KT + 1))
                        pe.wait_ge(m_split, v.n + 1)
                        nc.tensor.transpose(ps_s[bank_of_max(v, k)][:, 0, 0:P // 2].bitcast(BF16),
                                            nm_parts[:, :, :].rearrange("p a q -> p (a q)"), keep["ident_b"][:, :])\
                          .then_inc(s_done, 1)

                def scores(u, s):
                    t, j = s // GH, s % GH
                    rows = tiles[t][1]
                    q0 = t * P if causal else 0
                    pe.wait_ge(exp_done, u.n * STEPS + s - bank_age(s) + 4)
                    mm = nc.tensor.matmul(ps_st[bank_of_step[s]][0:rows, q0:SEQ], kp[u.buf][0:MROWS, j, t * P:t * P + rows],
                                          qp[u.buf][0:MROWS, j, q0:SEQ], start=True, stop=not causal)
                    if causal:
                        mm = nc.tensor.matmul(ps_st[bank_of_step[s]][0:rows, q0:q0 + P], keep["ident_b"][:, :],
                                              keep["mask_kv_b"][:, :], start=False, stop=True)
                    mm.then_inc(st_done, 1)

                def product(u, s):
                    t, j = s // GH, s % GH
                    rows = tiles[t][1]
                    q0 = t * P if causal else 0
                    if s == 0:
                        pe.wait_ge(v_in[u.vbuf], u.loads(VBUFS) * VLOADS)
                        pe.wait_ge(o_read, u.n + 1)
                    pe.wait_ge(exp_done, u.n * STEPS + s + 4)
                    nc.tensor.matmul(ps_o[j * VW:(j + 1) * VW, q0:SEQ],
                                     va[u.vbuf][0:rows, t, j * VW:(j + 1) * VW],
                                     pr[0:rows, (u.odd * STEPS + s) % RING, q0:SEQ],
                                     start=(t == 0), stop=(t == NT - 1)).then_inc(pv_done, 1)

                def unit(u, after, before=True):
                    todo = in_order(u, after)
                    pe.wait_ge(m_rows_in, (u.n + 1) * 16 + 1)
                    for s in range(STEPS):
                        scores(u, s)
                        if s > LAG:
                            if s == LAG + 1:
                                product(u, 0)
                            product(u, s - LAG)
                        elif s < LAG and before:
                            product(u.next(-1), STEPS - LAG + s)
                        while todo and (todo[0][0] <= s or s == STEPS - 1):
                            maxima(*todo.pop(0)[1:])

                for event in before_all():
                    maxima(*event[1:])
                pe.wait_ge(ones_set, BUFS + 1)
                unit(Unit(0, 0), units - 1, False)
                with pe.Fori(0, units // 4 - 1) as i:
                    for r in range(1, 5):
                        unit(Unit(i, r), 3)
                for r in range(1, 4):
                    unit(Unit(units // 4 - 1, r), 3 - r)
                for s in range(STEPS - LAG, STEPS):
                    product(Unit(units // 4 - 1, 3), s)

            @block.vector
            def _(dve):
                dve.sem_inc(s_read, 2)
                if beside and beside[0]:
                    beside[0](dve)

                def maxima(what, v, k):
                    if what == "split" and PIECES == 2:
                        dve.wait_ge(s_read, (v.n + 1) * NP + 2)
                        nc.vector.tensor_tensor(nm[:, :], nmax[v.odd][:, :, 0], nmax[v.odd][:, :, 1], ALU.min)\
                          .then_inc(m_merged, 1)
                    if what not in ("piece", "piece0"):
                        return
                    j, q, spans = pieces[k]
                    at, bank = (turn(v, k), bank_of(v, k)) if what == "piece" else (k, k % 2)
                    col, half = j * QT + q, k % PIECES
                    dve.wait_ge(s_done, at + 1)
                    nc.vector.tensor_reduce(nmax[v.odd][:, col, half:half + 1], ps_s[bank][:, 0:len(spans), 0:spans[0][1]],
                                            AX.XY, ALU.max, negate=True).then_inc(s_read, 1)

                def unit(u, after):
                    for event in in_order(u, after):
                        maxima(*event[1:])

                for event in before_all():
                    maxima(*event[1:])
                unit(Unit(0, 0), units - 1)
                with dve.Fori(0, units // 4 - 1) as i:
                    for r in range(1, 5):
                        unit(Unit(i, r), 3)
                for r in range(1, 4):
                    unit(Unit(units // 4 - 1, r), 3 - r)

            @block.gpsimd
            def _(pool):
                for k in range(BUFS):
                    nc.gpsimd.memset(kp[k][SROWS:MROWS, :, :], 1.0).then_inc(ones_set, 1)
                pool.wait_ge(ones_set, BUFS)
                nc.gpsimd.memset(nm_parts[:, 3:, :], 0.0).then_inc(ones_set, 1)
                pool.wait_ge(ones_set, BUFS + 1)
                LINKS = 3

                def split(v):
                    done = [0]

                    def link(ins):
                        done[0] += 1
                        ins.then_inc(m_step, 1)
                        pool.wait_ge(m_step, v.n * LINKS + done[0])

                    if PIECES == 2:
                        pool.wait_ge(m_merged, v.n + 1)
                        full = nm[:, :]
                    else:
                        pool.wait_ge(s_read, (v.n + 1) * NP + 2)
                        full = nmax[v.odd][:, :, 0]
                    pool.sem_inc(pool_turn, 1)
                    link(nc.gpsimd.tensor_copy(nm_parts[:, 0, :], full))
                    link(nc.gpsimd.tensor_tensor(nm_rest[:, :], full, nm_parts[:, 0, :], ALU.subtract))
                    pool.sem_inc(pool_turn, 1)
                    link(nc.gpsimd.tensor_copy(nm_parts[:, 1, :], nm_rest[:, :]))
                    nc.gpsimd.tensor_tensor(nm_parts[:, 2, :], nm_rest[:, :], nm_parts[:, 1, :], ALU.subtract)\
                      .then_inc(m_split, 1)

                with pool.Fori(0, units // 4) as i:
                    for r in range(4):
                        split(Unit(i, r))
                        if beside:
                            beside[1](pool, i, r)
                if beside and beside[2]:
                    beside[2](pool)

            @block.scalar
            def _(act):
                act.sem_inc(exp_done, 3)
                act.sem_inc(o_read, 1)
                act.sem_inc(m_rows_in, 1)
                assert 2 * STEPS % RING == 0

                def exponential(u, s):
                    t = s // GH
                    rows = tiles[t][1]
                    q0 = t * P if causal else 0
                    act.wait_ge(st_done, u.n * STEPS + s + 1 + RING)
                    act.wait_ge(pv_done, u.n * STEPS + s + 1)
                    nc.scalar.activation(pr[0:rows, (u.odd * STEPS + s) % RING, q0:SEQ],
                                         ps_st[bank_of_step[s]][0:rows, q0:SEQ], ACT.Exp).then_inc(exp_done, 1)

                def copy_max(v, last):
                    act.wait_ge(s_done, (v.n + 1) * SLOTS + (0 if last else KT))
                    act.wait_ge(m_rows_in, v.n * 16 + 1)
                    nc.scalar.copy(nm_rows[:, :], ps_s[bank_of_max(v, last)][0:3 * GH * QT, 0, 0:P // 2]
                                   .bitcast(BF16)).then_inc(m_read, 1)

                def send_max(v):
                    act.wait_ge(m_read, v.n + 1)
                    act.dma_start(qp[v.buf][SROWS:MROWS, :, :].rearrange("a j n -> a (j n)"), nm_rows[:, :])\
                       .then_inc(m_rows_in, 16)

                def take_out(u):
                    act.wait_ge(pv_done, (u.n + 1) * STEPS + RING)
                    act.wait_ge(o_sent[u.odd], u.loads(2) * 16)
                    nc.scalar.copy(ob[u.odd][:, :], ps_o[:, :]).then_inc(o_read, 1)

                def unit(u, after, before=True):
                    turned_at = [e[0] for e in in_order(u, after) if e[1] == "turn"]
                    for s in range(STEPS):
                        if s == LAG and before:
                            take_out(u.next(-1))
                        exponential(u, s)
                        if turned_at and s == min(turned_at[0], STEPS - 1):
                            copy_max(u.next(1), after < 2)
                        if turned_at and s == min(turned_at[0] + 1, STEPS - 1):
                            send_max(u.next(1))

                copy_max(Unit(0, 0), False)
                send_max(Unit(0, 0))
                unit(Unit(0, 0), units - 1, False)
                with act.Fori(0, units // 4 - 1) as i:
                    for r in range(1, 5):
                        unit(Unit(i, r), 3)
                for r in range(1, 4):
                    unit(Unit(units // 4 - 1, r), 3 - r)
                take_out(Unit(units // 4 - 1, 3))

        p.clear()


def invert_denominators(nc, out_rows, inverse, own, units):
    n = units * GH
    with ExitStack() as stack:
        p = Prog(nc, stack, "inv_self_" if own else "inv_cross_")
        den = p.sb("den", [n, SEQ])
        inv = p.sb("inv", [n, SEQ])
        den_in = p.sem("den_in")
        inv_ready = p.sem("inv_ready")
        inv_sent = p.sem("inv_sent")
        with nc.Block() as block:
            @block.sync
            def _(sp):
                src = out_rows.rearrange("u (j w) n -> u j w n", w=VW)[:, :, HD, :].rearrange("u j n -> (u j) n")
                sp.dma_start(den[:, :], src).then_inc(den_in, 16)
                sp.wait_ge(inv_ready, 1)
                sp.dma_start(inverse, inv[:, :]).then_inc(inv_sent, 16)
                sp.wait_ge(inv_sent, 16)

            @block.vector
            def _(dve):
                dve.wait_ge(den_in, 16)
                nc.vector.reciprocal(inv[:, :], den[:, :]).then_inc(inv_ready, 1)
        p.clear()




def load_attention_out(eng, out_rows, inverse, oT, inv, b, arrived):
    for c in range(KC):
        for u in range(GROUPS // KC):
            src = out_rows[b * GROUPS + (c * (GROUPS // KC) + u), :, :].rearrange("(j w) n -> j w n", w=VW)
            eng.dma_start(oT[u * GR:(u + 1) * GR, c, :], src[:, 0:HD, :]).then_inc(arrived, 16)
        heads = HEADS // KC
        src = inverse[bass.ds(b * HEADS + c * heads, heads), :].unsqueeze(1).broadcast_to([heads, HD, SEQ])
        eng.dma_start(inv[:, c, :], src).then_inc(arrived, 16)


ATT_LOADS = 16 * (GROUPS + KC)


def project_self(nc, x_in, out_rows, inverse, x1_rows, h0_rows, q_parts, k_parts, v_rows, keep, batches):
    with ExitStack() as stack:
        p = Prog(nc, stack, "slf_")
        oT = p.sb("oT", [P, KC, SEQ])
        inv = p.sb("inv_rows", [P, KC, SEQ])
        on = p.sb("o_normed", [P, KC, SEQ])
        x = p.sb("x_rows", [P, QT, DIM])
        xb = p.sb("x_biased", [P, QT, DIM])
        x1 = p.sb("x1", [P, QT, DIM])
        h0 = p.sb("h0", [P, QT, DIM])
        xr = p.sb("x_rms", [P, QT, DIM])
        norm = Norms(p)
        xT = p.sb("xT", [P, KC, SEQ])
        t1 = [p.sb(f"rope_cos{w}", [P, KC, SEQ]) for w in range(2)]
        t2 = [p.sb(f"rope_sin{w}", [P, KC, SEQ]) for w in range(2)]
        full = [p.sb(f"roped{w}", [P, KC, SEQ]) for w in range(2)]
        rest = [p.sb(f"roped_rest{w}", [P, KC, SEQ]) for w in range(2)]
        parts = [[p.sb(f"roped_part{w}{a}", [P, KC, SEQ], BF16) for a in range(3)] for w in range(2)]
        vpad = p.sb("v_pad", [P, QT, HEADS, VW])
        ps_o = p.ps("ps_o", [P, QT, DIM])
        ps_t = p.ps("ps_t", [P, KC, SEQ])
        ps_a = p.ps("ps_a", [P, KC, SEQ])
        ps_b = p.ps("ps_b", [P, KC, SEQ])
        att_in = p.sem("att_in")
        x_came = p.sem("x_came")
        on_ready = p.sem("on_ready")
        xb_ready = p.sem("xb_ready")
        o_done = p.sem("o_done")
        x1_ready = p.sem("x1_ready")
        mv_ready = p.sem("mv_ready")
        std_ready = p.sem("std_ready")
        h0_ready = p.sem("h0_ready")
        ms_ready = p.sem("ms_ready")
        rms_ready = p.sem("rms_ready")
        rrms_ready = p.sem("rrms_ready")
        xr_ready = p.sem("xr_ready")
        turned = p.sem("turned")
        xT_ready = p.sem("xT_ready")
        rope_done = p.sem("rope_done")
        rope_read = p.sem("rope_read")
        full_ready = [p.sem(f"full_ready{w}") for w in range(2)]
        hi_ready = [p.sem(f"hi_ready{w}") for w in range(2)]
        rest_ready = [p.sem(f"rest_ready{w}") for w in range(2)]
        mid_ready = [p.sem(f"mid_ready{w}") for w in range(2)]
        low_ready = [p.sem(f"low_ready{w}") for w in range(2)]
        sent = [p.sem(f"sent{w}") for w in range(2)]
        v_done = p.sem("v_done")
        v_ready = p.sem("v_ready")
        rows_sent = p.sem("rows_sent")
        v_sent = p.sem("v_sent")
        pads = p.sem("pads")
        pool_turn = p.sem("pool_turn")
        SENT = 16 * 3 * KC

        with nc.Block() as block:
            @block.sync
            def _(sp):
                def load(b):
                    sp.wait_ge(on_ready, b + 1)
                    load_attention_out(sp, out_rows, inverse, oT, inv, b, att_in)
                    sp.wait_ge(xb_ready, b + 1)
                    sp.dma_start(x[:, :, :], x_in[bass.ds(b * SEQ, SEQ), :].rearrange("(t p) d -> p t d", p=P))\
                      .then_inc(x_came, 16)

                def store_rows(b):
                    sp.wait_ge(h0_ready, b + 1)
                    for src, dst in ((x1, x1_rows), (h0, h0_rows)):
                        sp.dma_start(dst[bass.ds(b * SEQ, SEQ), :].rearrange("(t p) d -> p t d", p=P), src[:, :, :])\
                          .then_inc(rows_sent, 16)

                def store_parts(w, b):
                    sp.wait_ge(low_ready[w], b + 2)
                    for a in range(3):
                        for i in range(KC):
                            sp.dma_start((q_parts, k_parts)[w][bass.ds(b * GROUPS + i * 2, 2), a, :, :],
                                         parts[w][a][:, i, :]).then_inc(sent[w], 16)

                def store_q(b):
                    store_parts(0, b)

                def store_k(b):
                    store_parts(1, b)

                def store_v(b):
                    sp.wait_ge(v_ready, b + 2)
                    for g in range(GROUPS):
                        sp.dma_start(v_rows[b * GROUPS + g, :, :].rearrange("(t p) v -> p t v", p=P),
                                     vpad[:, :, g * GH:(g + 1) * GH, :].rearrange("p t h v -> p t (h v)"))\
                          .then_inc(v_sent, 16)

                for i in range(2):
                    sp.sem_inc(sent[i], SENT)
                sp.sem_inc(v_sent, 16 * GROUPS)
                sp.sem_inc(rows_sent, 32)
                turns(sp, batches, ((0, load), (4, store_k), (3, store_v), (2, store_rows), (3, store_q)))
                for i in range(2):
                    sp.wait_ge(sent[i], SENT * (batches + 1))
                sp.wait_ge(v_sent, 16 * GROUPS * (batches + 1))
                sp.wait_ge(rows_sent, 32 * (batches + 1))

            @block.tensor
            def _(pe):
                def out_product(b):
                    pe.wait_ge(on_ready, b + 2)
                    for t in range(QT):
                        for i in range(KC):
                            last = nc.tensor.matmul(ps_o[:, t, :], on[:, i, t * P:(t + 1) * P], keep["WoT"][:, i, :],
                                                    start=(i == 0), stop=(i == KC - 1))
                    last.then_inc(o_done, 1)

                def turn_rows(b):
                    pe.wait_ge(xr_ready, b + 2)
                    pe.wait_ge(v_ready, b + 1)
                    for t in range(QT):
                        for i in range(KC):
                            last = nc.tensor.transpose(ps_t[:, i, t * P:(t + 1) * P], xr[:, t, i * P:(i + 1) * P],
                                                       keep["ident"][:, :])
                    last.then_inc(turned, 1)

                def rope_products(w, b):
                    pe.wait_ge(rope_read, b * 2 + w + 1)
                    for ps, weights in ((ps_a, ("wq", "wk")[w]), (ps_b, ("wq_rot", "wk_rot")[w])):
                        for o in range(KC):
                            for i in range(KC):
                                last = nc.tensor.matmul(ps[:, o, :], keep[weights][:, i, o * P:(o + 1) * P],
                                                        xT[:, i, :], start=(i == 0), stop=(i == KC - 1))
                    last.then_inc(rope_done, 1)

                def q_products(b):
                    pe.wait_ge(xT_ready, b + 1)
                    rope_products(0, b)

                def k_products(b):
                    rope_products(1, b)

                def v_product(b):
                    for t in range(QT):
                        for i in range(KC):
                            last = nc.tensor.matmul(ps_t[:, t // 2, t % 2 * DIM:(t % 2 + 1) * DIM],
                                                    xT[:, i, t * P:(t + 1) * P],
                                                    keep["wv"][:, i, :], start=(i == 0), stop=(i == KC - 1))
                    last.then_inc(v_done, 1)

                turns(pe, batches, ((1, turn_rows), (0, out_product), (1, q_products), (1, v_product),
                                    (1, k_products)))

            @block.vector
            def _(dve):
                nc.vector.memset(vpad[:, :, :, HD:VW], 0.0)
                dve.drain()
                nc.vector.memset(vpad[:, :, :, HD:HD + 1], 1.0).then_inc(pads, 1)
                for s in (on_ready, x1_ready, rope_read, *rest_ready):
                    dve.sem_inc(s, 1)

                def divide(b):
                    dve.wait_ge(att_in, (b + 1) * ATT_LOADS)
                    nc.vector.tensor_tensor(on[:, :, :], oT[:, :, :], inv[:, :, :], ALU.mult).then_inc(on_ready, 1)

                def residual(b):
                    dve.wait_ge(o_done, b + 1)
                    dve.wait_ge(xb_ready, b + 2)
                    dve.wait_ge(rows_sent, (b + 1) * 32)
                    nc.vector.tensor_tensor(x1[:, :, :], ps_o[:, :, :], xb[:, :, :], ALU.add).then_inc(x1_ready, 1)
                    dve.drain()
                    norm.moments(nc, dve, x1).then_inc(mv_ready, 1)

                def layer_norm(b):
                    dve.wait_ge(std_ready, b + 1)
                    nc.vector.reciprocal(norm.rstd[:, :], norm.std[:, :])
                    dve.drain()
                    dve.wait_ge(xr_ready, b + 1)
                    for t in range(QT):
                        last = nc.vector.tensor_scalar(h0[:, t, :], x1[:, t, :], norm.mv[:, t, 0:1],
                                                       norm.rstd[:, t:t + 1], ALU.subtract, ALU.mult)
                    last.then_inc(h0_ready, 1)
                    dve.drain()
                    norm.mean_square(nc, dve, h0).then_inc(ms_ready, 1)

                def rms_inverse(b):
                    dve.wait_ge(rms_ready, b + 1)
                    nc.vector.reciprocal(norm.rrms[:, :], norm.rms[:, :]).then_inc(rrms_ready, 1)

                def rope(w, b):
                    dve.wait_ge(rope_done, b * 2 + w + 1)
                    dve.wait_ge(full_ready[w], b + 1)
                    for i in range(KC):
                        nc.vector.tensor_tensor(t1[w][:, i, :], ps_a[:, i, :], keep["cos_" + "qk"[w]][:, :], ALU.mult)
                        last = nc.vector.tensor_tensor(t2[w][:, i, :], ps_b[:, i, :], keep["sin_" + "qk"[w]][:, :],
                                                       ALU.mult)
                    last.then_inc(rope_read, 1)

                def subtract_high(w, b):
                    dve.wait_ge(hi_ready[w], b + 1)
                    dve.wait_ge(low_ready[w], b + 1)
                    nc.vector.tensor_tensor(rest[w][:, :, :], full[w][:, :, :], parts[w][0][:, :, :], ALU.subtract)\
                      .then_inc(rest_ready[w], 1)

                turns(dve, batches, ((3, lambda b: subtract_high(1, b)), (1, residual), (0, divide),
                                     (2, lambda b: rope(0, b)), (1, layer_norm), (1, rms_inverse),
                                     (2, lambda b: subtract_high(0, b)), (2, lambda b: rope(1, b))))

            @block.scalar
            def _(act):
                act.sem_inc(xr_ready, 1)
                act.sem_inc(v_ready, 1)

                def deviation(b):
                    act.wait_ge(mv_ready, b + 1)
                    nc.scalar.activation(norm.std[:, :], norm.mv[:, :, 1], ACT.Sqrt, bias=keep["ln_eps"][:, :])\
                       .then_inc(std_ready, 1)

                def root_mean_square(b):
                    act.wait_ge(ms_ready, b + 1)
                    nc.scalar.activation(norm.rms[:, :], norm.ms[:, :], ACT.Sqrt, bias=keep["rms_eps"][:, :])\
                       .then_inc(rms_ready, 1)

                def scale_rows(b):
                    act.wait_ge(rrms_ready, b + 1)
                    for t in range(QT):
                        last = nc.scalar.activation(xr[:, t, :], h0[:, t, :], ACT.Copy, scale=norm.rrms[:, t:t + 1])
                    last.then_inc(xr_ready, 1)

                def take_turned(b):
                    act.wait_ge(turned, b + 1)
                    for i in range(KC):
                        last = nc.scalar.activation(xT[:, i, :], ps_t[:, i, :], ACT.Copy, scale=keep["g1"][:, i:i + 1])
                    last.then_inc(xT_ready, 1)

                def take_v(b):
                    act.wait_ge(v_done, b + 1)
                    act.wait_ge(v_sent, (b + 1) * 16 * GROUPS)
                    for t in range(QT):
                        last = nc.scalar.copy(vpad[:, t, :, 0:HD],
                                              ps_t[:, t // 2, t % 2 * DIM:(t % 2 + 1) * DIM]
                                              .rearrange("p (h d) -> p h d", d=HD))
                    last.then_inc(v_ready, 1)

                def high(w, b):
                    act.wait_ge(full_ready[w], b + 2)
                    act.wait_ge(sent[w], (b + 1) * SENT)
                    nc.scalar.copy(parts[w][0][:, :, :], full[w][:, :, :]).then_inc(hi_ready[w], 1)

                act.wait_ge(pads, 1)
                turns(act, batches, ((1, take_turned), (2, lambda b: high(1, b)), (0, deviation), (1, take_v),
                                     (1, lambda b: high(0, b)), (0, root_mean_square), (0, scale_rows)))

            @block.gpsimd
            def _(pool):
                for s in (*full_ready, *low_ready, xb_ready):
                    pool.sem_inc(s, 1)

                def add_bias(b):
                    pool.wait_ge(x_came, (b + 1) * 16)
                    pool.wait_ge(x1_ready, b + 1)
                    for t in range(QT):
                        last = nc.gpsimd.tensor_tensor(xb[:, t, :], x[:, t, :], keep["bo"][:, :], ALU.add)
                    last.then_inc(xb_ready, 1)

                def add_and_split(w, b):
                    pool.wait_ge(rope_read, b * 2 + w + 2)
                    pool.wait_ge(rest_ready[w], b + 1)
                    nc.gpsimd.tensor_tensor(full[w][:, :, :], t1[w][:, :, :], t2[w][:, :, :], ALU.add)\
                      .then_inc(full_ready[w], 1)
                    pool.wait_ge(rest_ready[w], b + 2)
                    pool.sem_inc(pool_turn, 1)
                    nc.gpsimd.tensor_copy(parts[w][1][:, :, :], rest[w][:, :, :]).then_inc(mid_ready[w], 1)
                    pool.wait_ge(mid_ready[w], b + 1)
                    nc.gpsimd.tensor_tensor(parts[w][2][:, :, :], rest[w][:, :, :], parts[w][1][:, :, :],
                                            ALU.subtract).then_inc(low_ready[w], 1)

                turns(pool, batches, ((3, lambda b: add_and_split(1, b)), (0, add_bias),
                                      (2, lambda b: add_and_split(0, b))))
        p.clear()


def finish_self(nc, out_rows, inverse, x1_rows, h0_rows, y_rows, hn_rows, keep, batches):
    logits = keep["logits"]
    with ExitStack() as stack:
        p = Prog(nc, stack, "fin_")
        oT = p.sb("oT", [P, KC, SEQ])
        inv = p.sb("inv_rows", [P, KC, SEQ])
        on = p.sb("o_normed", [P, KC, SEQ])
        x1 = p.sb("x1", [P, QT, DIM])
        h0 = p.sb("h0", [P, QT, DIM])
        h = p.sb("h", [P, QT, DIM])
        y = p.sb("y", [P, QT, DIM])
        hr = p.sb("h_rms", [P, QT, DIM])
        hn = p.sb("h_normed", [P, QT, DIM])
        norm = Norms(p)
        hT = p.sb("hT", [P, KC, SEQ])
        ps_o = p.ps("ps_o", [P, QT, DIM])
        ps_t = p.ps("ps_t", [P, KC, SEQ])
        ps_l = p.ps("ps_l", [P, QT, EXPERTS])
        att_in = p.sem("att_in")
        rows_in = p.sem("rows_in")
        on_ready = p.sem("on_ready")
        o_done = p.sem("o_done")
        h_ready = p.sem("h_ready")
        y_ready = p.sem("y_ready")
        ms_ready = p.sem("ms_ready")
        rms_ready = p.sem("rms_ready")
        rrms_ready = p.sem("rrms_ready")
        hr_ready = p.sem("hr_ready")
        hn_ready = p.sem("hn_ready")
        turned = p.sem("turned")
        hT_ready = p.sem("hT_ready")
        l_done = p.sem("l_done")
        l_ready = p.sem("l_ready")
        y_sent = p.sem("y_sent")
        hn_sent = p.sem("hn_sent")

        with nc.Block() as block:
            @block.sync
            def _(sp):
                def load_attention(b):
                    sp.wait_ge(on_ready, b + 1)
                    load_attention_out(sp, out_rows, inverse, oT, inv, b, att_in)

                def load_rows(b):
                    sp.wait_ge(y_ready, b + 1)
                    for src, dst in ((x1_rows, x1), (h0_rows, h0)):
                        sp.dma_start(dst[:, :, :], src[bass.ds(b * SEQ, SEQ), :].rearrange("(t p) d -> p t d", p=P))\
                          .then_inc(rows_in, 16)

                turns(sp, batches, ((1, load_rows), (0, load_attention)))

            @block.tensor
            def _(pe):
                pe.sem_inc(turned, 1)

                def out_product(b):
                    pe.wait_ge(on_ready, b + 2)
                    for t in range(QT):
                        for i in range(KC):
                            last = nc.tensor.matmul(ps_o[:, t, :], on[:, i, t * P:(t + 1) * P], keep["wo"][:, i, :],
                                                    start=(i == 0), stop=(i == KC - 1))
                    last.then_inc(o_done, 1)

                def turn_rows(b):
                    pe.wait_ge(hn_ready, b + 2)
                    for t in range(QT):
                        for i in range(KC):
                            last = nc.tensor.transpose(ps_t[:, i, t * P:(t + 1) * P], hn[:, t, i * P:(i + 1) * P],
                                                       keep["ident"][:, :])
                    last.then_inc(turned, 1)

                def router(b):
                    pe.wait_ge(hT_ready, b + 1)
                    pe.wait_ge(l_ready, b + 1)
                    for t in range(QT):
                        for i in range(KC):
                            last = nc.tensor.matmul(ps_l[:, t, :], hT[:, i, t * P:(t + 1) * P],
                                                    keep["w_router"][:, i, :], start=(i == 0), stop=(i == KC - 1))
                    last.then_inc(l_done, 1)

                turns(pe, batches, ((2, turn_rows), (0, out_product), (2, router)))

            @block.vector
            def _(dve):
                dve.sem_inc(on_ready, 1)
                dve.sem_inc(l_ready, 1)

                def divide(b):
                    dve.wait_ge(att_in, (b + 1) * ATT_LOADS)
                    nc.vector.tensor_tensor(on[:, :, :], oT[:, :, :], inv[:, :, :], ALU.mult).then_inc(on_ready, 1)

                def residual(b):
                    dve.wait_ge(o_done, b + 1)
                    dve.wait_ge(rows_in, (b + 1) * 32)
                    dve.wait_ge(y_ready, b + 1)
                    dve.wait_ge(hr_ready, b + 1)
                    nc.vector.tensor_tensor(h[:, :, :], ps_o[:, :, :], h0[:, :, :], ALU.add).then_inc(h_ready, 1)

                def mean_square(b):
                    dve.wait_ge(h_ready, b + 1)
                    norm.mean_square(nc, dve, h).then_inc(ms_ready, 1)

                def rms_inverse(b):
                    dve.wait_ge(rms_ready, b + 1)
                    nc.vector.reciprocal(norm.rrms[:, :], norm.rms[:, :]).then_inc(rrms_ready, 1)

                def take_logits(b):
                    dve.wait_ge(l_done, b + 1)
                    nc.vector.tensor_copy(logits[:, bass.ds(b * QT, QT), :], ps_l[:, :, :]).then_inc(l_ready, 1)

                turns(dve, batches, ((1, residual), (0, divide), (1, mean_square), (1, rms_inverse),
                                     (3, take_logits)))

            @block.scalar
            def _(act):
                act.sem_inc(hr_ready, 1)

                def root_mean_square(b):
                    act.wait_ge(ms_ready, b + 1)
                    nc.scalar.activation(norm.rms[:, :], norm.ms[:, :], ACT.Sqrt, bias=keep["rms_eps"][:, :])\
                       .then_inc(rms_ready, 1)

                def scale_rows(b):
                    act.wait_ge(rrms_ready, b + 1)
                    act.wait_ge(hn_ready, b + 1)
                    for t in range(QT):
                        last = nc.scalar.activation(hr[:, t, :], h[:, t, :], ACT.Copy, scale=norm.rrms[:, t:t + 1])
                    last.then_inc(hr_ready, 1)

                def take_turned(b):
                    act.wait_ge(turned, b + 2)
                    nc.scalar.copy(hT[:, :, :], ps_t[:, :, :]).then_inc(hT_ready, 1)

                def store_y(b):
                    act.wait_ge(y_ready, b + 2)
                    act.dma_start(y_rows[bass.ds(b * SEQ, SEQ), :].rearrange("(t p) d -> p t d", p=P), y[:, :, :])\
                      .then_inc(y_sent, 16)

                def store_normed(b):
                    act.wait_ge(hn_ready, b + 2)
                    act.dma_start(hn_rows[bass.ds(b * SEQ, SEQ), :].rearrange("(t p) d -> p t d", p=P), hn[:, :, :])\
                      .then_inc(hn_sent, 16)

                act.sem_inc(y_sent, 16)
                act.sem_inc(hn_sent, 16)
                turns(act, batches, ((2, take_turned), (0, root_mean_square), (0, scale_rows), (0, store_y),
                                     (1, store_normed)))
                act.wait_ge(y_sent, 16 * (batches + 1))
                act.wait_ge(hn_sent, 16 * (batches + 1))

            @block.gpsimd
            def _(pool):
                pool.sem_inc(y_ready, 1)
                pool.sem_inc(hn_ready, 1)

                def add(b):
                    pool.wait_ge(h_ready, b + 1)
                    pool.wait_ge(y_sent, (b + 1) * 16)
                    nc.gpsimd.tensor_tensor(y[:, :, :], x1[:, :, :], h[:, :, :], ALU.add).then_inc(y_ready, 1)

                def weigh(b):
                    pool.wait_ge(hr_ready, b + 2)
                    pool.wait_ge(turned, b + 1)
                    pool.wait_ge(hn_sent, (b + 1) * 16)
                    for t in range(QT):
                        last = nc.gpsimd.tensor_tensor(hn[:, t, :], hr[:, t, :], keep["g2"][:, :], ALU.mult)
                    last.then_inc(hn_ready, 1)

                turns(pool, batches, ((0, add), (0, weigh)))
        p.clear()



def route(nc, keep, tokens):
    T = tokens // P
    E = EXPERTS
    TILES = 2 * T + E
    logits, slots, weights, expert = keep["logits"], keep["slots"], keep["pair_weights"], keep["tile_expert"]
    with ExitStack() as stack:
        p = Prog(nc, stack, "route_")
        probs = p.sb("probs", [P, T, E])
        work = p.sb("work", [P, T, E])
        chosen = p.sb("chosen", [P, T, E], BF16)
        first = p.sb("first_choice", [P, T, E])
        second = p.sb("second_choice", [P, T, E])
        row = p.sb("row_max", [P, T])
        left = p.sb("left", [P, T])
        top = [p.sb(f"top{i}", [P, T]) for i in range(2)]
        run = [p.sb(f"run{i}", [P, T, E]) for i in range(2)]
        place = p.sb("place", [P, T, E])
        compare = p.sb("compare", [P, E, 64])
        used = p.sb("used_tiles", [P, E])
        begin = p.sb("begin", [P, E])
        end = p.sb("end", [P, E])
        pairs = p.sb("pairs", [P, E, E])
        tile_cmp = p.sb("tile_cmp", [P, 96, E])
        tile_f = p.sb("tile_f", [P, 96])
        slot_f = p.sb("slot_f", [P, 2, T])
        ones = p.sb("ones", [P, P], BF16)
        ps_rank = p.ps("ps_rank", [P, T, E])
        ps_total = p.ps("ps_total", [P, T, E])
        shifted = p.sem("shifted")
        exp_ready = p.sem("exp_ready")
        chosen_ready = p.sem("chosen_ready")
        ranks_done = p.sem("ranks_done")
        routed = p.sem("routed")

        def over_e(a, n=T):
            return a.unsqueeze(2).broadcast_to([P, n, E])

        left_of = keep["iota_left"][:, :].unsqueeze(1).broadcast_to([P, T, E])

        with nc.Block() as block:
            @block.vector
            def _(dve):
                def tt(out, a, b, op):
                    nc.vector.tensor_tensor(out, a, b, op)
                    dve.drain()

                def reduce(out, a, op):
                    nc.vector.tensor_reduce(out, a, AX.X, op)
                    dve.drain()

                nc.vector.memset(ones[:, :], 1.0)
                reduce(row[:, :], logits[:, :, :], ALU.max)
                nc.vector.tensor_tensor(work[:, :, :], logits[:, :, :], over_e(row[:, :]), ALU.subtract)\
                  .then_inc(shifted, 1)
                dve.wait_ge(exp_ready, 1)
                reduce(row[:, :], probs[:, :, :], ALU.add)
                nc.vector.reciprocal(left[:, :], row[:, :])
                dve.drain()
                tt(probs[:, :, :], probs[:, :, :], over_e(left[:, :]), ALU.mult)
                for k, pick in enumerate((first, second)):
                    reduce(top[k][:, :], probs[:, :, :], ALU.max)
                    tt(work[:, :, :], probs[:, :, :], over_e(top[k][:, :]), ALU.is_equal)
                    tt(work[:, :, :], work[:, :, :], left_of, ALU.mult)
                    reduce(left[:, :], work[:, :, :], ALU.max)
                    tt(pick[:, :, :], over_e(left[:, :]), left_of, ALU.is_equal)
                    if k == 0:
                        nc.vector.scalar_tensor_tensor(out=probs[:, :, :], in0=pick[:, :, :], scalar=-2.0,
                                                       in1=probs[:, :, :], op0=ALU.mult, op1=ALU.add)
                        dve.drain()
                nc.vector.tensor_tensor(chosen[:, :, :], first[:, :, :], second[:, :, :], ALU.add)\
                  .then_inc(chosen_ready, 1)
                tt(row[:, :], top[0][:, :], top[1][:, :], ALU.add)
                nc.vector.reciprocal(left[:, :], row[:, :])
                dve.drain()
                for k in range(2):
                    tt(weights[:, k, :], top[k][:, :], left[:, :], ALU.mult)
                dve.wait_ge(ranks_done, 1)
                nc.vector.tensor_copy(run[0][:, :, :], ps_total[:, :, :])
                dve.drain()
                src, step = 0, 1
                while step < T:
                    a, b = run[src], run[1 - src]
                    nc.vector.tensor_copy(b[:, 0:step, :], a[:, 0:step, :])
                    tt(b[:, step:T, :], a[:, step:T, :], a[:, 0:T - step, :], ALU.add)
                    src, step = 1 - src, step * 2
                total = run[src]
                n = T + 1
                tt(compare[:, :, 0:n], total[:, T - 1, :].unsqueeze(2).broadcast_to([P, E, n]),
                   keep["iota_count"][:, 0:n].unsqueeze(1).broadcast_to([P, E, n]), ALU.is_gt)
                reduce(used[:, :], compare[:, :, 0:n], ALU.add)
                tt(pairs[:, :, :], used[:, :].unsqueeze(1).broadcast_to([P, E, E]),
                   keep["lt8"][:, :].rearrange("p (a b) -> p a b", b=E), ALU.mult)
                reduce(begin[:, :], pairs[:, :, :], ALU.add)
                tt(end[:, :], begin[:, :], used[:, :], ALU.add)
                tt(tile_cmp[:, 0:TILES, :], over_e(keep["iota_tile"][:, 0:TILES], TILES),
                   end[:, :].unsqueeze(1).broadcast_to([P, TILES, E]), ALU.is_ge)
                reduce(tile_f[:, 0:TILES], tile_cmp[:, 0:TILES, :], ALU.add)
                nc.vector.tensor_scalar(expert[:, 0:TILES], tile_f[:, 0:TILES], E - 1.0, None, ALU.min)
                tt(place[:, :, :], total[:, :, :], ps_total[:, :, :], ALU.subtract)
                tt(place[:, :, :], place[:, :, :], ps_rank[:, :, :], ALU.add)
                nc.vector.scalar_tensor_tensor(out=place[:, :, :], in0=begin[:, :].unsqueeze(1).broadcast_to([P, T, E]),
                                               scalar=float(P), in1=place[:, :, :], op0=ALU.mult, op1=ALU.add)
                dve.drain()
                for k, pick in enumerate((first, second)):
                    tt(work[:, :, :], pick[:, :, :], place[:, :, :], ALU.mult)
                    reduce(slot_f[:, k, :], work[:, :, :], ALU.add)
                nc.vector.tensor_copy(slots[:, :, :], slot_f[:, :, :]).then_inc(routed, 1)
                dve.wait_ge(routed, 1)

            @block.scalar
            def _(act):
                act.wait_ge(shifted, 1)
                nc.scalar.activation(probs[:, :, :], work[:, :, :], ACT.Exp).then_inc(exp_ready, 1)

            @block.tensor
            def _(pe):
                pe.wait_ge(chosen_ready, 1)
                nc.tensor.matmul(ps_rank[:, :, :].rearrange("p t e -> p (t e)"), keep["before_b"][:, :],
                                 chosen[:, :, :].rearrange("p t e -> p (t e)"), start=True, stop=True)
                nc.tensor.matmul(ps_total[:, :, :].rearrange("p t e -> p (t e)"), ones[:, :],
                                 chosen[:, :, :].rearrange("p t e -> p (t e)"), start=True, stop=True)\
                  .then_inc(ranks_done, 1)
        p.clear()


def scatter_rows(nc, hn_rows, in_sorted, wd, keep, tokens):
    T = tokens // P
    slots = keep["slots"]
    D = 4
    CH = -(-HHALF // P)
    with ExitStack() as stack:
        p = Prog(nc, stack, "scat_")
        rows = [[p.sb(f"token_rows{g}{k}", [P, DIM]) for k in range(D)] for g in range(2)]
        index = [p.sb(f"index{g}", [P, 2, D], I32) for g in range(2)]
        rows_in = [p.sem(f"rows_in{g}") for g in range(2)]
        index_ready = p.sem("index_ready")
        gone = [p.sem(f"gone{g}") for g in range(2)]
        done = p.sem("done")
        pool_turn = p.sem("pool_turn")
        wd_in = keep["wd_in"]
        with nc.Block() as block:
            @block.sync
            def _(sp):
                sp.sem_inc(done, 2)
                with sp.Fori(0, T // (2 * D)) as i:
                    for g in range(2):
                        sp.wait_ge(done, i * 2 + g + 1)
                        for k in range(D):
                            sp.dma_start(rows[g][k][:, :], hn_rows[bass.ds(((i * 2 + g) * D + k) * P, P), :])\
                              .then_inc(rows_in[g], 16)

            @block.scalar
            def _(act):
                full, rest = HHALF // P, HHALF % P
                with act.Fori(0, EXPERTS) as e:
                    for half in range(2):
                        src = wd[bass.ds(e, 1), half * HHALF:(half + 1) * HHALF, :].rearrange("e r n -> (e r) n")
                        at = (e * 2 + half) * (CH * DIM)
                        act.dma_start(keep["wd_sb"][:, bass.ds(at, full * DIM)].rearrange("p (c n) -> p c n", n=DIM),
                                      src[0:full * P, :].rearrange("(c p) n -> p c n", p=P)).then_inc(wd_in, 16)
                        act.dma_start(keep["wd_sb"][0:rest, bass.ds(at + full * DIM, DIM)],
                                      src[full * P:HHALF, :]).then_inc(wd_in, 16)

            @block.vector
            def _(dve):
                with dve.Fori(0, T // (2 * D)) as i:
                    for g in range(2):
                        dve.wait_ge(done, i * 2 + g + 1)
                        nc.vector.tensor_copy(index[g][:, :, :], slots[:, :, bass.ds((i * 2 + g) * D, D)])\
                          .then_inc(index_ready, 1)

            @block.gpsimd
            def _(pool):
                def ended(i, g):
                    pool.wait_ge(gone[g], (i + 1) * 32 * D)
                    pool.sem_inc(done, 1)

                def scatter(i, g):
                    pool.wait_ge(rows_in[g], (i + 1) * 16 * D)
                    pool.wait_ge(index_ready, i * 2 + g + 1)
                    pool.sem_inc(pool_turn, 1)
                    for k in range(D):
                        for c in range(2):
                            pool.indirect_dma_start(
                                out=in_sorted,
                                out_offset=bass.IndirectOffsetOnAxis(ap=index[g][:, c, k:k + 1], axis=0),
                                in_=rows[g][k][:, :], in_offset=None).then_inc(gone[g], 16)

                scatter(0, 0)
                with pool.Fori(0, T // (2 * D) - 1) as i:
                    scatter(i, 1)
                    ended(i, 0)
                    scatter(i + 1, 0)
                    ended(i, 1)
                scatter(T // (2 * D) - 1, 1)
                for g in range(2):
                    ended(T // (2 * D) - 1, g)
        p.clear()


def experts(nc, in_sorted, out_sorted, keep, tiles):
    HALVES = 2
    CH = -(-HHALF // P)
    CW = [min(P, HHALF - c * P) for c in range(CH)]
    with ExitStack() as stack:
        p = Prog(nc, stack, "moe_")
        rows = [p.sb(f"rows{i}", [P, DIM]) for i in range(2)]
        xT = [p.sb(f"rowsT{i}", [P, KC, P]) for i in range(2)]
        sil = [p.sb(f"silu{i}", [P, HHALF]) for i in range(2)]
        h = [p.sb(f"hidden{i}", [P, HHALF]) for i in range(2)]
        hT = [p.sb(f"hiddenT{i}", [P, CH, P]) for i in range(2)]
        y = [p.sb(f"y{i}", [P, DIM]) for i in range(2)]
        ps_g = [p.ps(f"ps_g{i}", [P, SEQ]) for i in range(2)]
        ps_u = [p.ps(f"ps_u{i}", [P, SEQ]) for i in range(2)]
        ps_h = [p.ps(f"ps_h{i}", [P, CH, P]) for i in range(2)]
        ps_x = p.ps("ps_x", [P, KC, P])
        ps_y = p.ps("ps_y", [P, DIM])
        rows_in = [p.sem(f"rows_in{i}") for i in range(2)]
        turned = p.sem("turned")
        xT_ready = p.sem("xT_ready")
        gu_done = p.sem("gu_done")
        sil_ready = p.sem("sil_ready")
        h_ready = p.sem("h_ready")
        h_turned = p.sem("h_turned")
        hT_ready = p.sem("hT_ready")
        down_done = p.sem("down_done")
        y_ready = p.sem("y_ready")
        sent = [p.sem(f"sent{i}") for i in range(2)]

        class Tile:

            def __init__(self, i, r):
                self.i, self.r = i, r
                self.n = i * 2 + r
                self.par = r % 2
                self.turn = i + r // 2

            def next(self, d):
                return Tile(self.i, self.r + d)

        def tile_turns(eng, first, step, last):
            first(Tile(0, 0))
            with eng.Fori(0, (tiles - 3) // 2) as i:
                step(Tile(i, 1), True)
                step(Tile(i, 2), True)
            step(Tile(0, tiles - 2), True)
            step(Tile(0, tiles - 1), False)
            last(Tile(0, tiles - 1))

        assert tiles % 2 == 1
        with nc.Block() as block:
            @block.sync
            def _(sp):
                sp.sem_inc(turned, 2)
                for i in range(2):
                    sp.sem_inc(sent[i], 16)

                def load(t):
                    sp.wait_ge(turned, t.n + 1)
                    sp.dma_start(rows[t.par][:, :], in_sorted[bass.ds(t.n * P, P), :]).then_inc(rows_in[t.par], 16)

                def store(t):
                    sp.wait_ge(y_ready, t.n + 2)
                    sp.dma_start(out_sorted[bass.ds(t.n * P, P), :], y[t.par][:, :]).then_inc(sent[t.par], 16)

                for t in range(3):
                    load(Tile(0, t))
                with sp.Fori(0, (tiles - 3) // 2) as i:
                    for r in range(2):
                        load(Tile(i, r + 3))
                        store(Tile(i, r))
                for t in range(tiles - 3, tiles):
                    store(Tile(0, t))
                for i in range(2):
                    sp.wait_ge(sent[i], 16 * ((tiles + 1 - i) // 2 + 1))

            @block.tensor
            def _(pe):
                pe.sem_inc(h_turned, 2)
                pe.sem_inc(down_done, 1)
                pe.wait_ge(keep["gate_up_in"], 16 * 2 * KC * EXPERTS)
                pe.wait_ge(keep["wd_in"], 16 * 4 * EXPERTS)
                wg, wu, wd = keep["wg_sb"], keep["wu_sb"], keep["wd_sb"]

                def expert_of(t):
                    return pe.value_load(keep["tile_expert"][0:1, bass.ds(t.n, 1)], min_val=0, max_val=EXPERTS - 1)

                def turn_rows(t):
                    pe.wait_ge(rows_in[t.par], (t.turn + 1) * 16)
                    pe.wait_ge(xT_ready, t.n + 1)
                    for i in range(KC):
                        last = nc.tensor.transpose(ps_x[:, i, :], rows[t.par][:, i * P:(i + 1) * P],
                                                   keep["ident"][:, :])
                    last.then_inc(turned, 1)

                def gate_up(t, half, e):
                    if half == 0:
                        pe.wait_ge(xT_ready, t.n + 2)
                    pe.wait_ge(h_ready, t.n * 2 + half + 1)
                    for ps, wt in ((ps_g, wg), (ps_u, wu)):
                        for i in range(KC):
                            at = e * (KC * HIDDEN) + i * HIDDEN + half * HHALF
                            last = nc.tensor.matmul(ps[half][:, 0:HHALF], xT[t.par][:, i, :],
                                                    wt[:, bass.ds(at, HHALF)], start=(i == 0), stop=(i == KC - 1))
                    last.then_inc(gu_done, 1)

                def turn_hidden(t, half):
                    pe.wait_ge(h_ready, t.n * 2 + half + 3)
                    pe.wait_ge(hT_ready, t.n * 2 + half + 1)
                    for c in range(CH):
                        last = nc.tensor.transpose(ps_h[half][0:CW[c], c, :], h[half][:, c * P:c * P + CW[c]],
                                                   keep["ident"][:, :])
                    last.then_inc(h_turned, 1)

                def down(t, e):
                    pe.wait_ge(y_ready, t.n + 1)
                    pe.wait_ge(hT_ready, t.n * 2 + 4)
                    for half in range(HALVES):
                        for c in range(CH):
                            at = e * (HALVES * CH * DIM) + (half * CH + c) * DIM
                            last = nc.tensor.matmul(ps_y[:, :], hT[half][0:CW[c], c, :],
                                                    wd[0:CW[c], bass.ds(at, DIM)],
                                                    start=(half == 0 and c == 0), stop=(half == 1 and c == CH - 1))
                    last.then_inc(down_done, 1)

                def first(t):
                    e = expert_of(t)
                    turn_rows(t)
                    turn_rows(t.next(1))
                    gate_up(t, 0, e)
                    gate_up(t, 1, e)
                    turn_hidden(t, 0)

                def step(t, following):
                    before, e = expert_of(t.next(-1)), expert_of(t)
                    if following:
                        turn_rows(t.next(1))
                    gate_up(t, 0, e)
                    turn_hidden(t.next(-1), 1)
                    gate_up(t, 1, e)
                    down(t.next(-1), before)
                    turn_hidden(t, 0)

                def last(t):
                    e = expert_of(t)
                    turn_hidden(t, 1)
                    down(t, e)

                tile_turns(pe, first, step, last)

            @block.scalar
            def _(act):
                act.sem_inc(xT_ready, 1)
                act.sem_inc(y_ready, 1)

                def turned_rows(t):
                    act.wait_ge(turned, t.n + 3)
                    nc.scalar.copy(xT[t.par][:, :, :], ps_x[:, :, :]).then_inc(xT_ready, 1)

                def silu(t, half):
                    act.wait_ge(gu_done, t.n * 2 + half + 1)
                    act.wait_ge(h_ready, t.n * 2 + half + 1)
                    nc.scalar.activation(sil[half][:, :], ps_g[half][:, 0:HHALF], ACT.Silu).then_inc(sil_ready, 1)

                def result(t):
                    act.wait_ge(down_done, t.n + 2)
                    act.wait_ge(sent[t.par], (t.turn + 1) * 16)
                    nc.scalar.copy(y[t.par][:, :], ps_y[:, :]).then_inc(y_ready, 1)

                def first(t):
                    turned_rows(t)
                    turned_rows(t.next(1))
                    silu(t, 0)
                    silu(t, 1)

                def step(t, following):
                    if following:
                        turned_rows(t.next(1))
                    silu(t, 0)
                    silu(t, 1)
                    result(t.next(-1))

                tile_turns(act, first, step, result)

            @block.vector
            def _(dve):
                dve.sem_inc(h_ready, 2)
                dve.sem_inc(hT_ready, 2)

                def multiply(t, half):
                    dve.wait_ge(sil_ready, t.n * 2 + half + 1)
                    dve.wait_ge(h_turned, t.n * 2 + half + 1)
                    nc.vector.tensor_tensor(h[half][:, :], ps_u[half][:, 0:HHALF], sil[half][:, :], ALU.mult)\
                      .then_inc(h_ready, 1)

                def turned_hidden(t, half):
                    dve.wait_ge(h_turned, t.n * 2 + half + 3)
                    dve.wait_ge(down_done, t.n + 1)
                    nc.vector.tensor_copy(hT[half][:, 0:CH - 1, :], ps_h[half][:, 0:CH - 1, :])
                    nc.vector.tensor_copy(hT[half][0:CW[-1], CH - 1, :], ps_h[half][0:CW[-1], CH - 1, :])\
                      .then_inc(hT_ready, 1)

                def first(t):
                    multiply(t, 0)
                    multiply(t, 1)
                    turned_hidden(t, 0)

                def step(t, following):
                    turned_hidden(t.next(-1), 1)
                    multiply(t, 0)
                    multiply(t, 1)
                    turned_hidden(t, 0)

                tile_turns(dve, first, step, lambda t: turned_hidden(t, 1))
        p.clear()


def combine(nc, out_sorted, y_rows, out, keep, tokens):
    T = tokens // P
    slots, weights = keep["slots"], keep["pair_weights"]
    D = 4
    with ExitStack() as stack:
        p = Prog(nc, stack, "comb_")
        index = [p.sb(f"index{g}", [P, 2, D], I32) for g in range(2)]
        wt = [p.sb(f"pair{g}", [P, 2, D]) for g in range(2)]
        r = [[[p.sb(f"row{g}{k}{c}", [P, DIM]) for c in range(2)] for k in range(D)] for g in range(2)]
        y = [p.sb(f"y{g}", [P, D, DIM]) for g in range(2)]
        y_in = [p.sem(f"y_in{g}") for g in range(2)]
        index_ready = p.sem("index_ready")
        pool_turn = p.sem("pool_turn")
        got = [[p.sem(f"got{g}{k}") for k in range(D)] for g in range(2)]
        half_summed = p.sem("half_summed")
        summed = p.sem("summed")
        sent = [p.sem(f"sent{g}") for g in range(2)]
        with nc.Block() as block:
            @block.sync
            def _(sp):
                def rows_of(a, i, g):
                    return a[bass.ds((i * 2 + g) * (D * P), D * P), :].rearrange("(t p) d -> p t d", p=P)

                def load(i, g):
                    sp.wait_ge(sent[g], (i + 1) * 16)
                    sp.dma_start(y[g][:, :, :], rows_of(y_rows, i, g)).then_inc(y_in[g], 16)

                def store(i, g):
                    sp.wait_ge(summed, i * 2 + g + 1)
                    sp.dma_start(rows_of(out, i, g), y[g][:, :, :]).then_inc(sent[g], 16)

                for g in range(2):
                    sp.sem_inc(sent[g], 16)
                    load(0, g)
                with sp.Fori(0, T // (2 * D) - 1) as i:
                    for g in range(2):
                        store(i, g)
                        load(i + 1, g)
                for g in range(2):
                    store(T // (2 * D) - 1, g)
                for g in range(2):
                    sp.wait_ge(sent[g], 16 * (T // (2 * D) + 1))

            @block.gpsimd
            def _(pool):
                with pool.Fori(0, T // (2 * D)) as i:
                    for g in range(2):
                        pool.wait_ge(index_ready, i * 2 + g + 1)
                        pool.sem_inc(pool_turn, 1)
                        for k in range(D):
                            for c in range(2):
                                pool.indirect_dma_start(
                                    out=r[g][k][c][:, :], out_offset=None, in_=out_sorted,
                                    in_offset=bass.IndirectOffsetOnAxis(ap=index[g][:, c, k:k + 1], axis=0))\
                                    .then_inc(got[g][k], 16)

            @block.vector
            def _(dve):
                def prepare(i, g):
                    at = (i * 2 + g) * D
                    nc.vector.tensor_copy(wt[g][:, :, :], weights[:, :, bass.ds(at, D)])
                    nc.vector.tensor_copy(index[g][:, :, :], slots[:, :, bass.ds(at, D)]).then_inc(index_ready, 1)

                def add(i, g):
                    dve.wait_ge(y_in[g], (i + 1) * 16)
                    for k in range(D):
                        dve.wait_ge(got[g][k], (i + 1) * 32)
                        nc.vector.scalar_tensor_tensor(out=y[g][:, k, :], in0=r[g][k][0][:, :],
                                                       scalar=wt[g][:, 0, k:k + 1], in1=y[g][:, k, :],
                                                       op0=ALU.mult, op1=ALU.add).then_inc(half_summed, 1)
                        dve.wait_ge(half_summed, (i * 2 + g) * D + k + 1)
                        last = nc.vector.scalar_tensor_tensor(out=y[g][:, k, :], in0=r[g][k][1][:, :],
                                                              scalar=wt[g][:, 1, k:k + 1], in1=y[g][:, k, :],
                                                              op0=ALU.mult, op1=ALU.add)
                    last.then_inc(summed, 1)
                    dve.wait_ge(summed, i * 2 + g + 1)

                for g in range(2):
                    prepare(0, g)
                with dve.Fori(0, T // (2 * D) - 1) as i:
                    for g in range(2):
                        add(i, g)
                        prepare(i + 1, g)
                for g in range(2):
                    add(T // (2 * D) - 1, g)
        p.clear()


def shape_constants():
    import numpy as np
    i = np.arange(P)
    later = (i[None, :] > i[:, None]).astype(np.float32) * np.float32(MASKED)
    t = np.arange(SEQ, dtype=np.float32)
    inv_freq = 1.0 / 10000.0 ** (np.arange(0, HD, 2, dtype=np.float32) / HD)
    angle = np.einsum("i,j->ij", t, inv_freq.astype(np.float32)).astype(np.float32)
    cos = np.tile(np.cos(angle).T, (P // (HD // 2), 1)).astype(np.float32)
    sin = np.tile(np.sin(angle).T, (P // (HD // 2), 1)).astype(np.float32)
    e = np.arange(EXPERTS, dtype=np.float32)
    out = {
        "ident": np.eye(P, dtype=np.float32),
        "mask_q": later,
        "mask_kv": np.ascontiguousarray(later.T),
        "before": (i[:, None] < i[None, :]).astype(np.float32),
        "cos_q": cos * np.float32(SCALE), "sin_q": sin * np.float32(SCALE), "cos_k": cos, "sin_k": sin,
        "iota_left": np.tile(EXPERTS - e, (P, 1)),
        "iota_tile": np.tile(np.arange(96, dtype=np.float32), (P, 1)),
        "iota_count": np.tile(np.arange(64, dtype=np.float32) * P, (P, 1)),
        "lt8": np.tile((e[None, :] < e[:, None]).astype(np.float32).reshape(1, -1), (P, 1)),
    }
    return {k: np.ascontiguousarray(v, dtype=np.float32) for k, v in out.items()}


def zeros_beside(nc, in_sorted, stack, tiles, units):
    share = tiles // (units // 4)
    part = share // 3
    assert part * 3 * (units // 4) == tiles
    p = Prog(nc, stack, "zero_")
    zeros = p.sb("zeros", [P, part, DIM])
    zeros_set = p.sem("zeros_set")
    zeroed = p.sem("zeroed")

    def first(dve):
        nc.vector.memset(zeros[:, :, :], 0.0).then_inc(zeros_set, 1)

    def unit(pool, i, r):
        if r < 3:
            pool.wait_ge(zeros_set, 1)
            pool.dma_start(in_sorted[bass.ds(i * (share * P) + r * (part * P), part * P), :]
                           .rearrange("(t p) d -> p t d", p=P), zeros[:, :, :]).then_inc(zeroed, 16)

    def last(pool):
        pool.wait_ge(zeroed, 16 * 3 * (units // 4))

    return p, (first, unit, last)


def gate_up_beside(nc, a, keep, p, units):
    assert units // 4 == EXPERTS and KC == 2
    keep["wg_sb"] = p.sb("wg_sb", [P, EXPERTS * KC * HIDDEN])
    keep["wu_sb"] = p.sb("wu_sb", [P, EXPERTS * KC * HIDDEN])
    keep["gate_up_in"] = p.sem("gate_up_in")

    def unit(pool, e, r):
        n, c = ("wg", "wu")[r // 2], r % 2
        pool.dma_start(keep[n + "_sb"][:, bass.ds(e * (KC * HIDDEN) + c * HIDDEN, HIDDEN)],
                       a[n][bass.ds(e, 1), c * P:(c + 1) * P, :].rearrange("e p n -> p (e n)"))\
            .then_inc(keep["gate_up_in"], 16)

    return (None, unit, None)


KEEP_SHAPES = {"WqT": 0, "WkT": 0, "WvT": 0, "WoT": 0, "wq": 0, "wk": 0, "wv": 0, "wo": 0, "wq_rot": 0, "wk_rot": 0}


def build(nc, a, out, batches=8):
    units = batches * GROUPS
    dram = lambda name, shape, dt=F32: nc.dram_tensor(name, shape, dt, kind="Internal").ap()
    k_parts = dram("k_parts", [units, 3, GR, CTX], BF16)
    q_parts = dram("q_parts", [units, 3, GR, SEQ], BF16)
    v_rows = dram("v_rows", [units, CTX, GH * VW])
    out_rows = dram("out_rows", [units, P, SEQ])
    inverse = dram("inverse", [units * GH, SEQ])
    k2_parts = dram("k2_parts", [units, 3, GR, SEQ], BF16)
    q2_parts = dram("q2_parts", [units, 3, GR, SEQ], BF16)
    v2_rows = dram("v2_rows", [units, SEQ, GH * VW])
    out2_rows = dram("out2_rows", [units, P, SEQ])
    inverse2 = dram("inverse2", [units * GH, SEQ])
    tokens = batches * SEQ
    x1_rows = dram("x1_rows", [tokens, DIM])
    h0_rows = dram("h0_rows", [tokens, DIM])
    y_rows = dram("y_rows", [tokens, DIM])
    hn_rows = dram("hn_rows", [tokens, DIM])
    tiles = 2 * tokens // P + EXPERTS
    in_sorted = dram("in_sorted", [tiles * P, DIM])
    out_sorted = dram("out_sorted", [(tiles - 1) * P, DIM])
    with ExitStack() as stack:
        p = Prog(nc, stack, "top_")
        keep = {n: p.sb(f"keep_{n}", [P, KC, DIM]) for n in KEEP_SHAPES}
        for n, w in (("ident", P), ("mask_q", P), ("mask_kv", P), ("before", P), ("cos_q", SEQ), ("sin_q", SEQ),
                     ("cos_k", SEQ), ("sin_k", SEQ), ("iota_left", EXPERTS), ("iota_tile", 96), ("iota_count", 64),
                     ("lt8", EXPERTS * EXPERTS), ("bq", KC), ("bk", KC), ("g1", KC), ("bv", DIM), ("bo", DIM),
                     ("g2", DIM), ("ln_eps", 1), ("rms_eps", 1)):
            keep[n] = p.sb(f"keep_{n}", [P, w])
        for n in ("ident", "mask_q", "mask_kv", "before"):
            keep[n + "_b"] = p.sb(f"keep_{n}_b", [P, P], BF16)
        keep["w_router"] = p.sb("keep_w_router", [P, KC, EXPERTS])
        prepare_weights(nc, a, keep)
        project_context(nc, a["ctx"], k_parts, v_rows, keep, batches)
        project_queries(nc, a["x"], q_parts, keep, batches)
        with ExitStack() as zeros_stack:
            z, beside = zeros_beside(nc, in_sorted, zeros_stack, tiles, units)
            attention(nc, q_parts, k_parts, v_rows, out_rows, CTX, False, keep, units, beside)
            z.clear()
        invert_denominators(nc, out_rows, inverse, False, units)
        project_self(nc, a["x"], out_rows, inverse, x1_rows, h0_rows, q2_parts, k2_parts, v2_rows, keep, batches)
        beside = gate_up_beside(nc, a, keep, p, units)
        attention(nc, q2_parts, k2_parts, v2_rows, out2_rows, SEQ, True, keep, units, beside)
        invert_denominators(nc, out2_rows, inverse2, True, units)
        keep["logits"] = p.sb("logits", [P, tokens // P, EXPERTS])
        keep["slots"] = p.sb("slots", [P, 2, tokens // P], I32)
        keep["pair_weights"] = p.sb("pair_weights", [P, 2, tokens // P])
        keep["tile_expert"] = p.sb("tile_expert", [P, tiles], I32)
        finish_self(nc, out2_rows, inverse2, x1_rows, h0_rows, y_rows, hn_rows, keep, batches)
        route(nc, keep, tokens)
        keep["wd_in"] = p.sem("wd_in")
        keep["wd_sb"] = p.sb("wd_sb", [P, EXPERTS * 2 * -(-HHALF // P) * DIM])
        scatter_rows(nc, hn_rows, in_sorted, a["wd"], keep, tokens)
        experts(nc, in_sorted, out_sorted, keep, tiles - 1)
        combine(nc, out_sorted, y_rows, out, keep, tokens)


WEIGHTS = {n: f"L0_xattn_{n}" for n in ("Wq", "bq", "Wk", "bk", "Wv", "bv", "Wo", "bo")}
WEIGHTS.update({n: f"L0_ffn_{n}" for n in ("wq", "wk", "wv", "wo", "w_router", "wg", "wu", "wd", "g1", "g2")})


def kernel(**inputs):
    import numpy as _np
    import concourse.bacc as _bacc
    from concourse import mybir as _mybir
    from concourse.bass_utils import run_bass_kernel_spmd as _run

    x = _np.ascontiguousarray(inputs["x"])
    data = {"x": x.reshape(-1, DIM), "ctx": _np.ascontiguousarray(inputs["ctx_1024"]).reshape(-1, DIM)}
    data.update({n: _np.ascontiguousarray(inputs[full]) for n, full in WEIGHTS.items()})
    data.update(shape_constants())
    nc = _bacc.Bacc("TRN2", target_bir_lowering=False, num_devices=1)
    arrays, args = {}, {}
    for n, v in data.items():
        arrays[f"in_{n}_dram"] = v
        args[n] = nc.dram_tensor(f"in_{n}_dram", v.shape, _mybir.dt.from_np(v.dtype), kind="ExternalInput").ap()
    out = nc.dram_tensor("out_dram", data["x"].shape, _mybir.dt.from_np(x.dtype), kind="ExternalOutput").ap()
    build(nc, args, out, x.shape[0])
    got = _run(nc, [arrays], core_ids=[0]).results[0]["out_dram"]
    return got.reshape(x.shape)
```

```python
import concourse.bass as bass
from concourse import mybir
from contextlib import ExitStack

F32 = mybir.dt.float32
BF16 = mybir.dt.bfloat16
I32 = mybir.dt.int32
U32 = mybir.dt.uint32
ALU = mybir.AluOpType
ACT = mybir.ActivationFunctionType
AX = mybir.AxisListType

P = 128
DIM = 256
KC = DIM // P
HEADS = 16
HD = DIM // HEADS
GH = 4
GROUPS = HEADS // GH
GR = GH * HD
SEQ = 512
QT = SEQ // P
CTX = 1601
EXPERTS = 8
HIDDEN = 704
HC = -(-HIDDEN // P)
HLAST = HIDDEN - (HC - 1) * P
HHALF = HIDDEN // 2
SCALE = HD ** -0.5
MASKED = -1e30
LN_EPS = 1e-5
RMS_EPS = 1e-6

K_PARTS = (0, 1, 2, 0, 1, 0)
Q_PARTS = (0, 0, 0, 1, 1, 2)
PAIRS = len(K_PARTS)
SROWS = PAIRS * HD
MROWS = SROWS + 3
VW = 32


class Prog:

    def __init__(self, nc, stack, stage):
        self.nc, self.stack, self.stage, self.sems = nc, stack, stage, []

    def sb(self, name, shape, dt=F32):
        return self.stack.enter_context(self.nc.sbuf_tensor(self.stage + name, shape, dt))

    def ps(self, name, shape, dt=F32):
        return self.stack.enter_context(self.nc.psum_tensor(self.stage + name, shape, dt))

    def sem(self, name):
        self.sems.append(self.stack.enter_context(self.nc.semaphore(self.stage + name)))
        return self.sems[-1]

    def clear(self):
        for s in self.sems:
            self.nc.sync.sem_clear(s)
        self.nc.all_engine_barrier()


def prepare_weights(nc, w, keep):
    with ExitStack() as stack:
        p = Prog(nc, stack, "prep_")
        raw = {n: p.sb(f"raw_{n}", [P, KC, DIM]) for n in ("Wq", "Wk", "Wv", "Wo")}
        turned = [p.ps(f"turned{i}", [P, KC, DIM]) for i in range(4)]
        consts_in = p.sem("consts_in")
        raw_in = p.sem("raw_in")
        small_in = p.sem("small_in")
        turned_ready = p.sem("turned_ready")
        turned_kept = p.sem("turned_kept")
        rot_ready = p.sem("rot_ready")

        with nc.Block() as block:
            @block.sync
            def _(sp):
                sp.dma_start(keep["constants"][:, :], w["constants"]).then_inc(consts_in, 16)
                for n in ("Wq", "Wk", "Wv", "Wo"):
                    sp.dma_start(raw[n][:, :, :], w[n].rearrange("(c p) i -> p c i", p=P)).then_inc(raw_in, 16)

            @block.scalar
            def _(act):
                for n in ("bq", "bk", "g1"):
                    act.dma_start(keep[n][:, :], w[n].rearrange("(c p) -> p c", p=P),
                                  allow_slow_non_contiguous=True).then_inc(small_in, 16)
                for n in ("bv", "bo", "g2"):
                    act.dma_start(keep[n][:, :], w[n].partition_broadcast(P)).then_inc(small_in, 16)
                for n in ("wq", "wk", "wv", "wo"):
                    act.dma_start(keep[n][:, :, :], w[n].rearrange("(c p) o -> p c o", p=P)).then_inc(small_in, 16)
                act.dma_start(keep["w_router"][:, :, :], w["w_router"].rearrange("(c p) e -> p c e", p=P))\
                   .then_inc(small_in, 16)
                act.wait_ge(small_in, 16 * 11)
                nc.scalar.mul(keep["bq"][:, :], keep["bq"][:, :], SCALE)
                for src, dst in (("wq", "wq_rot"), ("wk", "wk_rot")):
                    s = keep[src][:, :, :].rearrange("p c (h t d) -> p (c h) t d", t=2, d=HD // 2)
                    d = keep[dst][:, :, :].rearrange("p c (h t d) -> p (c h) t d", t=2, d=HD // 2)
                    nc.scalar.mul(d[:, :, 0, :], s[:, :, 1, :], -1.0)
                    last = nc.scalar.copy(d[:, :, 1, :], s[:, :, 0, :])
                last.then_inc(rot_ready, 1)
                act.wait_ge(rot_ready, 1)

            @block.tensor
            def _(pe):
                pe.wait_ge(consts_in, 16)
                pe.wait_ge(raw_in, 16 * 4)
                for k, n in enumerate(("Wq", "Wk", "Wv", "Wo")):
                    for i in range(KC):
                        for o in range(KC):
                            last = nc.tensor.transpose(turned[k][:, i, o * P:(o + 1) * P],
                                                       raw[n][:, o, i * P:(i + 1) * P], keep["ident"][:, :])
                    last.then_inc(turned_ready, 1)

            @block.vector
            def _(dve):
                nc.vector.memset(keep["ln_eps"][:, :], LN_EPS)
                nc.vector.memset(keep["rms_eps"][:, :], RMS_EPS)
                for k, n in enumerate(("WqT", "WkT", "WvT", "WoT")):
                    dve.wait_ge(turned_ready, k + 1)
                    nc.vector.tensor_copy(keep[n][:, :, :], turned[k][:, :, :])
                dve.wait_ge(consts_in, 16)
                for n in ("ident", "mask_q", "mask_kv", "before"):
                    last = nc.vector.tensor_copy(keep[n + "_b"][:, :], keep[n][:, :])
                last.then_inc(turned_kept, 1)
                dve.wait_ge(turned_kept, 1)
        p.clear()


def turns(eng, steps, parts):
    deep = max(lag for lag, _ in parts)
    for t in range(deep):
        for lag, part in parts:
            if t >= lag:
                part(t - lag)
    with eng.Fori(0, steps - deep) as i:
        for lag, part in parts:
            part(i + (deep - lag))
    for t in range(steps, steps + deep):
        for lag, part in parts:
            if t - lag < steps:
                part(t - lag)


class Norms:

    def __init__(self, p):
        self.stats = p.sb("norm_stats", [P, QT, 6])
        self.mv = p.sb("norm_mean_var", [P, QT, 2])
        self.std = p.sb("norm_std", [P, QT])
        self.rstd = p.sb("norm_std_inv", [P, QT])
        self.stats2 = p.sb("norm_stats2", [P, QT, 6])
        self.mv2 = p.sb("norm_mean_var2", [P, QT, 2])
        self.square = p.sb("norm_mean2", [P, QT])
        self.ms = p.sb("norm_mean_square", [P, QT])
        self.rms = p.sb("norm_rms", [P, QT])
        self.rrms = p.sb("norm_rms_inv", [P, QT])

    def sums(self, nc, dve, rows, stats, mv):
        for t in range(QT):
            nc.vector.bn_stats(stats[:, t, :], rows[:, t, :])
        dve.drain()
        for t in range(QT):
            last = nc.vector.bn_aggr(mv[:, t, :], stats[:, t, :])
        return last

    def moments(self, nc, dve, rows):
        return self.sums(nc, dve, rows, self.stats, self.mv)

    def mean_square(self, nc, dve, rows):
        self.sums(nc, dve, rows, self.stats2, self.mv2)
        dve.drain()
        nc.vector.tensor_tensor(self.square[:, :], self.mv2[:, :, 0], self.mv2[:, :, 0], ALU.mult)
        dve.drain()
        return nc.vector.tensor_tensor(self.ms[:, :], self.square[:, :], self.mv2[:, :, 1], ALU.add)


def with_next(eng, batches, N, body, ahead=1):
    def at(b, c):
        return (b + c // N, c % N)

    with eng.Fori(0, batches - 1) as b:
        for c in range(N):
            body((b, c), at(b, c + ahead))
    for c in range(N):
        body((batches - 1, c), (batches - 1, c + ahead) if c + ahead < N else None)


def project_inputs(nc, ctx_in, x_in, k_parts, v_rows, q_parts, keep, batches):
    chunks = [(o, min(SEQ, CTX - o)) for o in range(0, CTX, SEQ)]
    CHUNKS = len(chunks)
    ITEMS = CHUNKS + 1
    N = 2 * ITEMS
    assert CHUNKS % 2 == 0 and batches % 2 == 0

    class Step:

        def __init__(self, at):
            self.pair, self.c = at
            self.n = self.pair * N + self.c
            self.par = self.c % 2
            self.item = self.c % ITEMS
            self.tokens = self.item == CHUNKS
            self.row = self.pair * 2 + self.c // ITEMS
            self.start, self.size = (0, SEQ) if self.tokens else chunks[self.item]
            self.chunk = self.row * CHUNKS + self.item

        def tiles(self):
            return [(t, min(P, self.size - t * P)) for t in range(-(-self.size // P))]

    def steps(eng, body, ahead=1):
        with_next(eng, batches // 2, N, lambda now, later: body(Step(now), later and Step(later)), ahead)

    with ExitStack() as stack:
        p = Prog(nc, stack, "in_")
        rows = [p.sb(f"rows{i}", [P, QT, DIM]) for i in range(ITEMS)]
        normed = p.sb("x_normed", [P, QT, DIM])
        norm = Norms(p)
        xT = [p.sb(f"rowsT{i}", [P, KC, SEQ]) for i in range(2)]
        full = [p.sb(f"full{i}", [P, KC, SEQ]) for i in range(2)]
        rest = [p.sb(f"rest{i}", [P, KC, SEQ]) for i in range(2)]
        parts = [[p.sb(f"part{i}{a}", [P, KC, SEQ], BF16) for a in range(3)] for i in range(ITEMS)]
        vpad = [p.sb(f"v_pad{i}", [P, QT, HEADS, VW]) for i in range(2)]
        ps_t = [p.ps(f"ps_t{i}", [P, KC, SEQ]) for i in range(2)]
        ps_k = p.ps("ps_k", [P, KC, SEQ])
        ps_v = p.ps("ps_v", [P, QT, DIM])
        rows_in = [p.sem(f"rows_in{i}") for i in range(ITEMS)]
        sent = [p.sem(f"sent{i}") for i in range(ITEMS)]
        v_sent = [p.sem(f"v_sent{i}") for i in range(2)]
        mv_ready = p.sem("mv_ready")
        std_ready = p.sem("std_ready")
        norm_ready = p.sem("norm_ready")
        turned = p.sem("turned")
        xT_ready = p.sem("xT_ready")
        k_done = p.sem("k_done")
        v_done = p.sem("v_done")
        high_ready = p.sem("high_ready")
        v_ready = p.sem("v_ready")
        rest_ready = p.sem("rest_ready")
        mid_ready = p.sem("mid_ready")
        low_ready = p.sem("low_ready")
        pads = p.sem("pads")
        pool_turn = p.sem("pool_turn")
        SENT = 16 * 3 * KC
        VSENT = 16 * GROUPS

        with nc.Block() as block:
            @block.sync
            def _(sp):
                for s in v_sent:
                    sp.sem_inc(s, VSENT)
                for s in sent:
                    sp.sem_inc(s, SENT)

                def load(st):
                    source, length = (x_in, SEQ) if st.tokens else (ctx_in, CTX)
                    src = source[bass.ds(st.row * length + st.start, st.size), :]
                    if st.size >= P:
                        sp.dma_start(rows[st.item][:, 0:st.size // P, :], src.rearrange("(t p) d -> p t d", p=P))\
                          .then_inc(rows_in[st.item], 16)
                    else:
                        sp.dma_start(rows[st.item][0:st.size, 0, :], src).then_inc(rows_in[st.item], 16)

                def step(st, later):
                    if later and st.tokens:
                        sp.wait_ge(norm_ready, st.row + 1)
                        load(later)
                    elif later:
                        sp.wait_ge(turned, st.n + 1)
                        load(later)
                    if not st.tokens:
                        sp.wait_ge(v_ready, st.chunk + 2)
                        for g in range(GROUPS):
                            dst = v_rows[st.row * GROUPS + g, st.start:st.start + st.size, :]
                            if st.size >= P:
                                sp.dma_start(dst.rearrange("(t p) v -> p t v", p=P),
                                             vpad[st.item % 2][:, 0:st.size // P, g * GH:(g + 1) * GH, :]
                                             .rearrange("p t h v -> p t (h v)")).then_inc(v_sent[st.item % 2], 16)
                            else:
                                sp.dma_start(dst, vpad[st.item % 2][0:st.size, 0, g * GH:(g + 1) * GH, :]
                                             .rearrange("p h v -> p (h v)")).then_inc(v_sent[st.item % 2], 16)
                    sp.wait_ge(low_ready, st.n + 3)
                    dst = q_parts if st.tokens else k_parts
                    for a in range(3):
                        for i in range(KC):
                            sp.dma_start(dst[bass.ds(st.row * GROUPS + i * 2, 2), a, :, st.start:st.start + st.size],
                                         parts[st.item][a][:, i, 0:st.size]).then_inc(sent[st.item], 16)

                for c in range(ITEMS):
                    load(Step((0, c)))
                steps(sp, step, ahead=ITEMS)
                for s in v_sent:
                    sp.wait_ge(s, VSENT * (batches * (CHUNKS // 2) + 1))
                for s in sent:
                    sp.wait_ge(s, SENT * (batches + 1))

            @block.tensor
            def _(pe):
                pe.sem_inc(k_done, 2)

                def turn(st):
                    if st.tokens:
                        pe.wait_ge(norm_ready, st.row + 1)
                    else:
                        pe.wait_ge(rows_in[st.item], (st.row + 1) * 16)
                    pe.wait_ge(xT_ready, st.n + 1)
                    src = normed if st.tokens else rows[st.item]
                    for t, m in st.tiles():
                        for i in range(KC):
                            last = nc.tensor.transpose(ps_t[st.par][:, i, t * P:t * P + m],
                                                       src[0:m, t, i * P:(i + 1) * P], keep["ident"][0:m, 0:m])
                    last.then_inc(turned, 1)

                def step(st, later):
                    if later:
                        turn(later)
                    pe.wait_ge(xT_ready, st.n + 3)
                    pe.wait_ge(high_ready, st.n + 1)
                    weights = keep["WqT" if st.tokens else "WkT"]
                    for o in range(KC):
                        for i in range(KC):
                            last = nc.tensor.matmul(ps_k[:, o, 0:st.size], weights[:, i, o * P:(o + 1) * P],
                                                    xT[st.par][:, i, 0:st.size], start=(i == 0), stop=(i == KC - 1))
                    last.then_inc(k_done, 1)
                    if st.tokens:
                        return
                    pe.wait_ge(v_ready, st.chunk + 1)
                    for t, m in st.tiles():
                        for i in range(KC):
                            last = nc.tensor.matmul(ps_v[0:m, t, :], xT[st.par][:, i, t * P:t * P + m],
                                                    keep["WvT"][:, i, :], start=(i == 0), stop=(i == KC - 1))
                    last.then_inc(v_done, 1)

                turn(Step((0, 0)))
                steps(pe, step)

            @block.vector
            def _(dve):
                for i in range(2):
                    nc.vector.memset(vpad[i][:, :, :, HD:VW], 0.0).then_inc(pads, 1)
                dve.wait_ge(pads, 2)
                for i in range(2):
                    nc.vector.memset(vpad[i][:, :, :, HD:HD + 1], 1.0).then_inc(pads, 1)
                dve.wait_ge(pads, 4)
                dve.sem_inc(xT_ready, 2)
                dve.sem_inc(v_ready, 1)
                dve.sem_inc(rest_ready, 2)

                def copy(st):
                    dve.wait_ge(turned, st.n + 1)
                    dve.wait_ge(k_done, st.n + 1)
                    nc.vector.tensor_copy(xT[st.par][:, :, 0:st.size], ps_t[st.par][:, :, 0:st.size])\
                      .then_inc(xT_ready, 1)

                def moments(row):
                    dve.wait_ge(rows_in[CHUNKS], (row + 1) * 16)
                    norm.moments(nc, dve, rows[CHUNKS]).then_inc(mv_ready, 1)

                def normalise(row):
                    dve.wait_ge(std_ready, row + 1)
                    nc.vector.reciprocal(norm.rstd[:, :], norm.std[:, :])
                    dve.drain()
                    for t in range(QT):
                        last = nc.vector.tensor_scalar(normed[:, t, :], rows[CHUNKS][:, t, :], norm.mv[:, t, 0:1],
                                                       norm.rstd[:, t:t + 1], ALU.subtract, ALU.mult)
                    last.then_inc(norm_ready, 1)

                def take_v(st):
                    dve.wait_ge(v_done, st.chunk + 1)
                    dve.wait_ge(v_sent[st.item % 2], (st.row * (CHUNKS // 2) + st.item // 2 + 1) * VSENT)
                    for t, m in st.tiles():
                        last = nc.vector.tensor_tensor(vpad[st.item % 2][0:m, t, :, 0:HD],
                                                       ps_v[0:m, t, :].rearrange("p (h d) -> p h d", d=HD),
                                                       keep["bv"][0:m, :].rearrange("p (h d) -> p h d", d=HD), ALU.add)
                    last.then_inc(v_ready, 1)

                def step(st, later):
                    if later:
                        copy(later)
                    dve.wait_ge(high_ready, st.n + 2)
                    dve.wait_ge(low_ready, st.n + 1)
                    nc.vector.tensor_tensor(rest[st.par][:, :, 0:st.size], full[st.par][:, :, 0:st.size],
                                            parts[st.item][0][:, :, 0:st.size], ALU.subtract).then_inc(rest_ready, 1)
                    if not st.tokens:
                        take_v(st)
                    if st.item == 0:
                        moments(st.row)
                    if st.item == 1:
                        normalise(st.row)

                copy(Step((0, 0)))
                steps(dve, step)

            @block.scalar
            def _(act):
                act.sem_inc(high_ready, 1)

                def step(st, later):
                    act.wait_ge(k_done, st.n + 3)
                    act.wait_ge(rest_ready, st.n + 1)
                    act.wait_ge(sent[st.item], (st.row + 1) * SENT)
                    bias, scale = (keep["bq"], SCALE) if st.tokens else (keep["bk"], 1.0)
                    for i in range(KC):
                        for dst in (full[st.par], parts[st.item][0]):
                            last = nc.scalar.activation(dst[:, i, 0:st.size], ps_k[:, i, 0:st.size], ACT.Identity,
                                                        bias=bias[:, i:i + 1], scale=scale)
                    last.then_inc(high_ready, 1)
                    if st.item == 0:
                        act.wait_ge(mv_ready, st.row + 1)
                        nc.scalar.activation(norm.std[:, :], norm.mv[:, :, 1], ACT.Sqrt, bias=keep["ln_eps"][:, :])\
                           .then_inc(std_ready, 1)

                steps(act, step)

            @block.gpsimd
            def _(pool):
                pool.sem_inc(low_ready, 2)

                def step(st, later):
                    mid, low = parts[st.item][1:]
                    pool.wait_ge(rest_ready, st.n + 3)
                    pool.sem_inc(pool_turn, 1)
                    nc.gpsimd.tensor_copy(mid[:, :, 0:st.size], rest[st.par][:, :, 0:st.size]).then_inc(mid_ready, 1)
                    pool.wait_ge(mid_ready, st.n + 1)
                    nc.gpsimd.tensor_tensor(low[:, :, 0:st.size], rest[st.par][:, :, 0:st.size],
                                            mid[:, :, 0:st.size], ALU.subtract).then_inc(low_ready, 1)

                steps(pool, step)
        p.clear()


def attention(nc, q_parts, k_parts, v_rows, out_rows, kv, causal, keep, units, beside=None):
    tiles = [(t, min(P, kv - t * P)) for t in range(-(-kv // P))]
    NT = len(tiles)
    STEPS = NT * GH
    RING = 8
    LAG = 5
    BUFS = 4
    VBUFS = 4 if causal else 2
    if causal:
        pieces = [(j, q, [(0, (q + 1) * P)]) for j in range(GH) for q in range(QT)]
        PIECES = 1
    else:
        span = -(-kv // 4)
        starts = [min(i * (kv // 4), kv - span) for i in range(4)]
        pieces = [(j, q, [(s, span) for s in starts[h * 2:h * 2 + 2]])
                  for j in range(GH) for q in range(QT) for h in range(2)]
        PIECES = 2
    NP = len(pieces)
    SLOTS = NP + 1
    TAIL = 11 if causal else 15
    KT = 3
    step_of = [STEPS - TAIL + (k - NP) * STEPS / NP for k in range(NP)]
    EARLY = sum(s < 0 for s in step_of)
    assert EARLY > KT and (units - 4) % 4 == 0
    with ExitStack() as stack:
        p = Prog(nc, stack, "att_self_" if causal else "att_cross_")
        kp = [p.sb(f"k_pack{i}", [P, GH, kv], BF16) for i in range(BUFS)]
        qp = [p.sb(f"q_pack{i}", [P, GH, SEQ], BF16) for i in range(BUFS)]
        va = [p.sb(f"v_tiles{i}", [P, NT, GH * VW]) for i in range(VBUFS)]
        pr = p.sb("probs", [P, RING, SEQ])
        nmax = [p.sb(f"neg_max{i}", [P, GH * QT, PIECES]) for i in range(2)]
        nm = p.sb("neg_max_merged", [P, GH * QT])
        nm_rest = p.sb("neg_max_rest", [P, GH * QT])
        nm_parts = p.sb("neg_max_parts", [P, P // (GH * QT), GH * QT], BF16)
        nm_rows = p.sb("neg_max_rows", [3 * GH * QT, P], BF16)
        ob = [p.sb(f"out_buf{i}", [P, SEQ]) for i in range(2)]
        ps_s = [p.ps(f"ps_s{i}", [P, 2, SEQ]) for i in range(2)]
        ps_st = [p.ps(f"ps_st{i}", [P, SEQ]) for i in range(3)]
        ps_o = p.ps("ps_o", [P, SEQ])
        ones_set = p.sem("ones_set")
        kq_in = [p.sem(f"kq_in{i}") for i in range(BUFS)]
        v_in = [p.sem(f"v_in{i}") for i in range(VBUFS)]
        m_rows_in = p.sem("m_rows_in")
        st_done = p.sem("st_done")
        exp_done = p.sem("exp_done")
        pv_done = p.sem("pv_done")
        s_done = p.sem("s_done")
        s_read = p.sem("s_read")
        m_merged = p.sem("m_merged")
        m_step = p.sem("m_step")
        m_split = p.sem("m_split")
        m_read = p.sem("m_read")
        pool_turn = p.sem("pool_turn")
        o_read = p.sem("o_read")
        o_sent = [p.sem(f"o_sent{i}") for i in range(2)]
        KQ = 16 * 2 * PAIRS
        VLOADS = 16 * ((1 if kv >= P else 0) + (1 if kv % P else 0))

        bank_of_step = [s % 3 for s in range(STEPS - 1)] + [1]
        assert STEPS % 3 == 1

        def bank_age(s):
            return next(d for d in range(1, 6) if bank_of_step[(s - d) % STEPS] == bank_of_step[s])

        class Unit:

            def __init__(self, i, r):
                self.i, self.r = i, r
                self.n = i * 4 + r
                self.odd = r % 2
                self.buf = r % BUFS
                self.vbuf = r % VBUFS

            def next(self, d):
                return Unit(self.i, self.r + d)

            def loads(self, bufs):
                return self.i * (4 // bufs) + self.r // bufs + 1

        def turn(v, k):
            return v.n * SLOTS + (k + (k >= KT) - 1)

        def bank_of(v, k):
            return (v.r * SLOTS + k + (k >= KT) - 1) % 2

        def bank_of_max(v, last):
            return ((v.r + 1) * SLOTS - 1 + (0 if last else KT)) % 2

        def in_order(u, after):
            out = []
            if after >= 1:
                out += [(step_of[k], "piece", u.next(1), k) for k in range(EARLY, NP)]
                out.append((step_of[NP - 1], "split", u.next(1), 0))
                if after >= 2:
                    out += [(step_of[k] + STEPS, "piece", u.next(2), k) for k in range(KT)]
                out.append((step_of[KT] + STEPS, "turn", u.next(1), int(after < 2)))
                if after >= 2:
                    out += [(step_of[k] + STEPS, "piece", u.next(2), k) for k in range(KT, EARLY)]
            return out

        def before_all():
            u0 = Unit(0, 0)
            out = [(0, "piece0", u0, k) for k in range(NP)] + [(0, "split", u0, 0)]
            out += [(0, "piece", u0.next(1), k) for k in range(KT)] + [(0, "turn", u0, 0)]
            return out + [(0, "piece", u0.next(1), k) for k in range(KT, EARLY)]

        with nc.Block() as block:
            @block.sync
            def _(sp):
                def load_kq(v):
                    for r in range(PAIRS):
                        sp.dma_start(kp[v.buf][r * HD:(r + 1) * HD, :, :],
                                     k_parts[v.n, K_PARTS[r], :, :].rearrange("(j d) n -> d j n", d=HD))\
                          .then_inc(kq_in[v.buf], 16)
                        sp.dma_start(qp[v.buf][r * HD:(r + 1) * HD, :, :],
                                     q_parts[v.n, Q_PARTS[r], :, :].rearrange("(j d) n -> d j n", d=HD))\
                          .then_inc(kq_in[v.buf], 16)

                def load_v(v):
                    if kv >= P:
                        sp.dma_start(va[v.vbuf][:, 0:kv // P, :],
                                     v_rows[v.n, 0:kv // P * P, :].rearrange("(t p) v -> p t v", p=P))\
                          .then_inc(v_in[v.vbuf], 16)
                    if kv % P:
                        sp.dma_start(va[v.vbuf][0:kv % P, kv // P, :], v_rows[v.n, kv // P * P:kv, :])\
                          .then_inc(v_in[v.vbuf], 16)

                def send_out(v):
                    sp.wait_ge(o_read, v.n + 2)
                    sp.dma_start(out_rows[v.n, :, :], ob[v.odd][:, :]).then_inc(o_sent[v.odd], 16)

                def unit(u, after, before=True):
                    if after >= VBUFS - 1:
                        if before:
                            sp.wait_ge(pv_done, u.n * STEPS + RING)
                        load_v(u.next(VBUFS - 1))
                    if after >= 3:
                        if before:
                            sp.wait_ge(st_done, u.n * STEPS + RING)
                        load_kq(u.next(3))
                    if before:
                        send_out(u.next(-1))

                for k in range(2):
                    sp.sem_inc(o_sent[k], 16)
                for r in range(3):
                    load_kq(Unit(0, r))
                for r in range(VBUFS - 1):
                    load_v(Unit(0, r))
                unit(Unit(0, 0), units - 1, False)
                with sp.Fori(0, units // 4 - 1) as i:
                    for r in range(1, 5):
                        unit(Unit(i, r), 3)
                for r in range(1, 4):
                    unit(Unit(units // 4 - 1, r), 3 - r)
                send_out(Unit(units // 4 - 1, 3))
                for k in range(2):
                    sp.wait_ge(o_sent[k], 16 * (units // 2 + 1))

            @block.tensor
            def _(pe):
                pe.sem_inc(st_done, RING)
                pe.sem_inc(pv_done, RING)

                def maxima(what, v, k):
                    if what in ("piece", "piece0"):
                        j, q, spans = pieces[k]
                        bank = bank_of(v, k) if what == "piece" else k % 2
                        if k == 0:
                            pe.wait_ge(kq_in[v.buf], v.loads(BUFS) * KQ)
                        if what == "piece" and k == KT + 1:
                            pe.wait_ge(m_read, v.n)
                        else:
                            pe.wait_ge(s_read, v.n * NP + (k + 1 + (what == "piece" and k == KT)))
                        for n, (s, w) in enumerate(spans):
                            last = nc.tensor.matmul(ps_s[bank][:, n, 0:w], qp[v.buf][0:SROWS, j, q * P:(q + 1) * P],
                                                    kp[v.buf][0:SROWS, j, s:s + w], start=True, stop=not causal)
                            if causal:
                                last = nc.tensor.matmul(ps_s[bank][:, n, w - P:w], keep["ident_b"][:, :],
                                                        keep["mask_q_b"][:, :], start=False, stop=True)
                        last.then_inc(s_done, 1)
                    elif what == "turn":
                        pe.wait_ge(s_read, (v.n + 1) * NP + (1 if k else KT + 1))
                        pe.wait_ge(m_split, v.n + 1)
                        nc.tensor.transpose(ps_s[bank_of_max(v, k)][:, 0, 0:P // 2].bitcast(BF16),
                                            nm_parts[:, :, :].rearrange("p a q -> p (a q)"), keep["ident_b"][:, :])\
                          .then_inc(s_done, 1)

                def scores(u, s):
                    t, j = s // GH, s % GH
                    rows = tiles[t][1]
                    q0 = t * P if causal else 0
                    pe.wait_ge(exp_done, u.n * STEPS + s - bank_age(s) + 4)
                    mm = nc.tensor.matmul(ps_st[bank_of_step[s]][0:rows, q0:SEQ], kp[u.buf][0:MROWS, j, t * P:t * P + rows],
                                          qp[u.buf][0:MROWS, j, q0:SEQ], start=True, stop=not causal)
                    if causal:
                        mm = nc.tensor.matmul(ps_st[bank_of_step[s]][0:rows, q0:q0 + P], keep["ident_b"][:, :],
                                              keep["mask_kv_b"][:, :], start=False, stop=True)
                    mm.then_inc(st_done, 1)

                def product(u, s):
                    t, j = s // GH, s % GH
                    rows = tiles[t][1]
                    q0 = t * P if causal else 0
                    if s == 0:
                        pe.wait_ge(v_in[u.vbuf], u.loads(VBUFS) * VLOADS)
                        pe.wait_ge(o_read, u.n + 1)
                    pe.wait_ge(exp_done, u.n * STEPS + s + 4)
                    nc.tensor.matmul(ps_o[j * VW:(j + 1) * VW, q0:SEQ],
                                     va[u.vbuf][0:rows, t, j * VW:(j + 1) * VW],
                                     pr[0:rows, (u.odd * STEPS + s) % RING, q0:SEQ],
                                     start=(t == 0), stop=(t == NT - 1)).then_inc(pv_done, 1)

                def unit(u, after, before=True):
                    todo = in_order(u, after)
                    pe.wait_ge(m_rows_in, (u.n + 1) * 16 + 1)
                    for s in range(STEPS):
                        scores(u, s)
                        while todo and todo[0][0] < s + 0.5:
                            maxima(*todo.pop(0)[1:])
                        if s > LAG:
                            if s == LAG + 1:
                                product(u, 0)
                            product(u, s - LAG)
                        elif s < LAG and before:
                            product(u.next(-1), STEPS - LAG + s)
                        while todo and (todo[0][0] < s + 1 or s == STEPS - 1):
                            maxima(*todo.pop(0)[1:])

                for event in before_all():
                    maxima(*event[1:])
                pe.wait_ge(ones_set, BUFS + 1)
                unit(Unit(0, 0), units - 1, False)
                with pe.Fori(0, units // 4 - 1) as i:
                    for r in range(1, 5):
                        unit(Unit(i, r), 3)
                for r in range(1, 4):
                    unit(Unit(units // 4 - 1, r), 3 - r)
                for s in range(STEPS - LAG, STEPS):
                    product(Unit(units // 4 - 1, 3), s)

            @block.vector
            def _(dve):
                dve.sem_inc(s_read, 2)
                if beside and beside[0]:
                    beside[0](dve)

                def maxima(what, v, k):
                    if what == "split" and PIECES == 2:
                        dve.wait_ge(s_read, (v.n + 1) * NP + 2)
                        nc.vector.tensor_tensor(nm[:, :], nmax[v.odd][:, :, 0], nmax[v.odd][:, :, 1], ALU.min)\
                          .then_inc(m_merged, 1)
                    if what not in ("piece", "piece0"):
                        return
                    j, q, spans = pieces[k]
                    at, bank = (turn(v, k), bank_of(v, k)) if what == "piece" else (k, k % 2)
                    col, half = j * QT + q, k % PIECES
                    dve.wait_ge(s_done, at + 1)
                    nc.vector.tensor_reduce(nmax[v.odd][:, col, half:half + 1], ps_s[bank][:, 0:len(spans), 0:spans[0][1]],
                                            AX.XY, ALU.max, negate=True).then_inc(s_read, 1)

                def unit(u, after):
                    for event in in_order(u, after):
                        maxima(*event[1:])

                for event in before_all():
                    maxima(*event[1:])
                unit(Unit(0, 0), units - 1)
                with dve.Fori(0, units // 4 - 1) as i:
                    for r in range(1, 5):
                        unit(Unit(i, r), 3)
                for r in range(1, 4):
                    unit(Unit(units // 4 - 1, r), 3 - r)

            @block.gpsimd
            def _(pool):
                for k in range(BUFS):
                    nc.gpsimd.memset(kp[k][SROWS:MROWS, :, :], 1.0).then_inc(ones_set, 1)
                pool.wait_ge(ones_set, BUFS)
                nc.gpsimd.memset(nm_parts[:, 3:, :], 0.0).then_inc(ones_set, 1)
                pool.wait_ge(ones_set, BUFS + 1)
                LINKS = 3

                def split(v):
                    done = [0]

                    def link(ins):
                        done[0] += 1
                        ins.then_inc(m_step, 1)
                        pool.wait_ge(m_step, v.n * LINKS + done[0])

                    if PIECES == 2:
                        pool.wait_ge(m_merged, v.n + 1)
                        full = nm[:, :]
                    else:
                        pool.wait_ge(s_read, (v.n + 1) * NP + 2)
                        full = nmax[v.odd][:, :, 0]
                    pool.sem_inc(pool_turn, 1)
                    link(nc.gpsimd.tensor_copy(nm_parts[:, 0, :], full))
                    link(nc.gpsimd.tensor_tensor(nm_rest[:, :], full, nm_parts[:, 0, :], ALU.subtract))
                    pool.sem_inc(pool_turn, 1)
                    link(nc.gpsimd.tensor_copy(nm_parts[:, 1, :], nm_rest[:, :]))
                    nc.gpsimd.tensor_tensor(nm_parts[:, 2, :], nm_rest[:, :], nm_parts[:, 1, :], ALU.subtract)\
                      .then_inc(m_split, 1)

                with pool.Fori(0, units // 4) as i:
                    for r in range(4):
                        split(Unit(i, r))
                        if beside:
                            beside[1](pool, i, r)
                if beside and beside[2]:
                    beside[2](pool)

            @block.scalar
            def _(act):
                act.sem_inc(exp_done, 3)
                act.sem_inc(o_read, 1)
                act.sem_inc(m_rows_in, 1)
                assert 2 * STEPS % RING == 0

                def exponential(u, s):
                    t = s // GH
                    rows = tiles[t][1]
                    q0 = t * P if causal else 0
                    act.wait_ge(st_done, u.n * STEPS + s + 1 + RING)
                    act.wait_ge(pv_done, u.n * STEPS + s + 1)
                    nc.scalar.activation(pr[0:rows, (u.odd * STEPS + s) % RING, q0:SEQ],
                                         ps_st[bank_of_step[s]][0:rows, q0:SEQ], ACT.Exp).then_inc(exp_done, 1)

                def copy_max(v, last):
                    act.wait_ge(s_done, (v.n + 1) * SLOTS + (0 if last else KT))
                    act.wait_ge(m_rows_in, v.n * 16 + 1)
                    nc.scalar.copy(nm_rows[:, :], ps_s[bank_of_max(v, last)][0:3 * GH * QT, 0, 0:P // 2]
                                   .bitcast(BF16)).then_inc(m_read, 1)

                def send_max(v):
                    act.wait_ge(m_read, v.n + 1)
                    act.dma_start(qp[v.buf][SROWS:MROWS, :, :].rearrange("a j n -> a (j n)"), nm_rows[:, :])\
                       .then_inc(m_rows_in, 16)

                def take_out(u):
                    act.wait_ge(pv_done, (u.n + 1) * STEPS + RING)
                    act.wait_ge(o_sent[u.odd], u.loads(2) * 16)
                    nc.scalar.copy(ob[u.odd][:, :], ps_o[:, :]).then_inc(o_read, 1)

                def unit(u, after, before=True):
                    turned_at = [int(e[0]) for e in in_order(u, after) if e[1] == "turn"]
                    for s in range(STEPS):
                        if s == LAG and before:
                            take_out(u.next(-1))
                        exponential(u, s)
                        if turned_at and s == min(turned_at[0], STEPS - 1):
                            copy_max(u.next(1), after < 2)
                        if turned_at and s == min(turned_at[0] + 1, STEPS - 1):
                            send_max(u.next(1))

                copy_max(Unit(0, 0), False)
                send_max(Unit(0, 0))
                unit(Unit(0, 0), units - 1, False)
                with act.Fori(0, units // 4 - 1) as i:
                    for r in range(1, 5):
                        unit(Unit(i, r), 3)
                for r in range(1, 4):
                    unit(Unit(units // 4 - 1, r), 3 - r)
                take_out(Unit(units // 4 - 1, 3))

        p.clear()


def invert_denominators(nc, out_rows, inverse, own, units):
    n = units * GH
    with ExitStack() as stack:
        p = Prog(nc, stack, "inv_self_" if own else "inv_cross_")
        den = p.sb("den", [n, SEQ])
        inv = p.sb("inv", [n, SEQ])
        den_in = p.sem("den_in")
        inv_ready = p.sem("inv_ready")
        inv_sent = p.sem("inv_sent")
        with nc.Block() as block:
            @block.sync
            def _(sp):
                src = out_rows.rearrange("u (j w) n -> u j w n", w=VW)[:, :, HD, :].rearrange("u j n -> (u j) n")
                sp.dma_start(den[:, :], src).then_inc(den_in, 16)
                sp.wait_ge(inv_ready, 1)
                sp.dma_start(inverse, inv[:, :]).then_inc(inv_sent, 16)
                sp.wait_ge(inv_sent, 16)

            @block.vector
            def _(dve):
                dve.wait_ge(den_in, 16)
                nc.vector.reciprocal(inv[:, :], den[:, :]).then_inc(inv_ready, 1)
        p.clear()




def load_attention_out(eng, out_rows, inverse, oT, inv, b, arrived):
    for c in range(KC):
        for u in range(GROUPS // KC):
            src = out_rows[b * GROUPS + (c * (GROUPS // KC) + u), :, :].rearrange("(j w) n -> j w n", w=VW)
            eng.dma_start(oT[u * GR:(u + 1) * GR, c, :], src[:, 0:HD, :]).then_inc(arrived, 16)
        heads = HEADS // KC
        src = inverse[bass.ds(b * HEADS + c * heads, heads), :].unsqueeze(1).broadcast_to([heads, HD, SEQ])
        eng.dma_start(inv[:, c, :], src).then_inc(arrived, 16)


ATT_LOADS = 16 * (GROUPS + KC)


def project_self(nc, x_in, out_rows, inverse, x1_rows, h0_rows, q_parts, k_parts, v_rows, keep, batches):
    with ExitStack() as stack:
        p = Prog(nc, stack, "slf_")
        oT = p.sb("oT", [P, KC, SEQ])
        inv = p.sb("inv_rows", [P, KC, SEQ])
        on = p.sb("o_normed", [P, KC, SEQ])
        x = p.sb("x_rows", [P, QT, DIM])
        xb = p.sb("x_biased", [P, QT, DIM])
        x1 = p.sb("x1", [P, QT, DIM])
        h0 = p.sb("h0", [P, QT, DIM])
        xr = p.sb("x_rms", [P, QT, DIM])
        norm = Norms(p)
        xT = p.sb("xT", [P, KC, SEQ])
        t1 = [p.sb(f"rope_cos{w}", [P, KC, SEQ]) for w in range(2)]
        t2 = [p.sb(f"rope_sin{w}", [P, KC, SEQ]) for w in range(2)]
        full = [p.sb(f"roped{w}", [P, KC, SEQ]) for w in range(2)]
        rest = [p.sb(f"roped_rest{w}", [P, KC, SEQ]) for w in range(2)]
        parts = [[p.sb(f"roped_part{w}{a}", [P, KC, SEQ], BF16) for a in range(3)] for w in range(2)]
        vpad = p.sb("v_pad", [P, QT, HEADS, VW])
        ps_o = p.ps("ps_o", [P, QT, DIM])
        ps_t = p.ps("ps_t", [P, KC, SEQ])
        ps_a = p.ps("ps_a", [P, KC, SEQ])
        ps_b = p.ps("ps_b", [P, KC, SEQ])
        att_in = p.sem("att_in")
        x_came = p.sem("x_came")
        on_ready = p.sem("on_ready")
        xb_ready = p.sem("xb_ready")
        o_done = p.sem("o_done")
        x1_ready = p.sem("x1_ready")
        mv_ready = p.sem("mv_ready")
        std_ready = p.sem("std_ready")
        h0_ready = p.sem("h0_ready")
        ms_ready = p.sem("ms_ready")
        rms_ready = p.sem("rms_ready")
        rrms_ready = p.sem("rrms_ready")
        xr_ready = p.sem("xr_ready")
        turned = p.sem("turned")
        xT_ready = p.sem("xT_ready")
        rope_done = p.sem("rope_done")
        rope_read = p.sem("rope_read")
        full_ready = [p.sem(f"full_ready{w}") for w in range(2)]
        hi_ready = [p.sem(f"hi_ready{w}") for w in range(2)]
        rest_ready = [p.sem(f"rest_ready{w}") for w in range(2)]
        mid_ready = [p.sem(f"mid_ready{w}") for w in range(2)]
        low_ready = [p.sem(f"low_ready{w}") for w in range(2)]
        sent = [p.sem(f"sent{w}") for w in range(2)]
        v_done = p.sem("v_done")
        v_ready = p.sem("v_ready")
        rows_sent = p.sem("rows_sent")
        v_sent = p.sem("v_sent")
        pads = p.sem("pads")
        SENT = 16 * 3 * KC

        with nc.Block() as block:
            @block.sync
            def _(sp):
                def load(b):
                    sp.wait_ge(on_ready, b + 1)
                    load_attention_out(sp, out_rows, inverse, oT, inv, b, att_in)
                    sp.wait_ge(xb_ready, b + 1)
                    sp.dma_start(x[:, :, :], x_in[bass.ds(b * SEQ, SEQ), :].rearrange("(t p) d -> p t d", p=P))\
                      .then_inc(x_came, 16)

                def store_rows(b):
                    sp.wait_ge(h0_ready, b + 1)
                    for src, dst in ((x1, x1_rows), (h0, h0_rows)):
                        sp.dma_start(dst[bass.ds(b * SEQ, SEQ), :].rearrange("(t p) d -> p t d", p=P), src[:, :, :])\
                          .then_inc(rows_sent, 16)

                def store_parts(w, b):
                    sp.wait_ge(low_ready[w], b + 2)
                    for a in range(3):
                        for i in range(KC):
                            sp.dma_start((q_parts, k_parts)[w][bass.ds(b * GROUPS + i * 2, 2), a, :, :],
                                         parts[w][a][:, i, :]).then_inc(sent[w], 16)

                def store_q(b):
                    store_parts(0, b)

                def store_k(b):
                    store_parts(1, b)

                def store_v(b):
                    sp.wait_ge(v_ready, b + 2)
                    for g in range(GROUPS):
                        sp.dma_start(v_rows[b * GROUPS + g, :, :].rearrange("(t p) v -> p t v", p=P),
                                     vpad[:, :, g * GH:(g + 1) * GH, :].rearrange("p t h v -> p t (h v)"))\
                          .then_inc(v_sent, 16)

                for i in range(2):
                    sp.sem_inc(sent[i], SENT)
                sp.sem_inc(v_sent, 16 * GROUPS)
                sp.sem_inc(rows_sent, 32)
                turns(sp, batches, ((0, load), (4, store_k), (3, store_v), (2, store_rows), (3, store_q)))
                for i in range(2):
                    sp.wait_ge(sent[i], SENT * (batches + 1))
                sp.wait_ge(v_sent, 16 * GROUPS * (batches + 1))
                sp.wait_ge(rows_sent, 32 * (batches + 1))

            @block.tensor
            def _(pe):
                def out_product(b):
                    pe.wait_ge(on_ready, b + 2)
                    for t in range(QT):
                        for i in range(KC):
                            last = nc.tensor.matmul(ps_o[:, t, :], on[:, i, t * P:(t + 1) * P], keep["WoT"][:, i, :],
                                                    start=(i == 0), stop=(i == KC - 1))
                    last.then_inc(o_done, 1)

                def turn_rows(b):
                    pe.wait_ge(xr_ready, b + 2)
                    pe.wait_ge(v_ready, b + 1)
                    for t in range(QT):
                        for i in range(KC):
                            last = nc.tensor.transpose(ps_t[:, i, t * P:(t + 1) * P], xr[:, t, i * P:(i + 1) * P],
                                                       keep["ident"][:, :])
                    last.then_inc(turned, 1)

                def rope_products(w, b):
                    pe.wait_ge(rope_read, b * 2 + w + 1)
                    for ps, weights in ((ps_a, ("wq", "wk")[w]), (ps_b, ("wq_rot", "wk_rot")[w])):
                        for o in range(KC):
                            for i in range(KC):
                                last = nc.tensor.matmul(ps[:, o, :], keep[weights][:, i, o * P:(o + 1) * P],
                                                        xT[:, i, :], start=(i == 0), stop=(i == KC - 1))
                    last.then_inc(rope_done, 1)

                def q_products(b):
                    pe.wait_ge(xT_ready, b + 1)
                    rope_products(0, b)

                def k_products(b):
                    rope_products(1, b)

                def v_product(b):
                    for t in range(QT):
                        for i in range(KC):
                            last = nc.tensor.matmul(ps_t[:, t // 2, t % 2 * DIM:(t % 2 + 1) * DIM],
                                                    xT[:, i, t * P:(t + 1) * P],
                                                    keep["wv"][:, i, :], start=(i == 0), stop=(i == KC - 1))
                    last.then_inc(v_done, 1)

                turns(pe, batches, ((1, turn_rows), (0, out_product), (1, q_products), (1, v_product),
                                    (1, k_products)))

            @block.vector
            def _(dve):
                nc.vector.memset(vpad[:, :, :, HD:VW], 0.0)
                dve.drain()
                nc.vector.memset(vpad[:, :, :, HD:HD + 1], 1.0).then_inc(pads, 1)
                for s in (on_ready, x1_ready, rope_read, *rest_ready):
                    dve.sem_inc(s, 1)

                def divide(b):
                    dve.wait_ge(att_in, (b + 1) * ATT_LOADS)
                    nc.vector.tensor_tensor(on[:, :, :], oT[:, :, :], inv[:, :, :], ALU.mult).then_inc(on_ready, 1)

                def residual(b):
                    dve.wait_ge(o_done, b + 1)
                    dve.wait_ge(xb_ready, b + 2)
                    dve.wait_ge(rows_sent, (b + 1) * 32)
                    nc.vector.tensor_tensor(x1[:, :, :], ps_o[:, :, :], xb[:, :, :], ALU.add).then_inc(x1_ready, 1)
                    dve.drain()
                    norm.moments(nc, dve, x1).then_inc(mv_ready, 1)

                def layer_norm(b):
                    dve.wait_ge(std_ready, b + 1)
                    nc.vector.reciprocal(norm.rstd[:, :], norm.std[:, :])
                    dve.drain()
                    dve.wait_ge(xr_ready, b + 1)
                    for t in range(QT):
                        last = nc.vector.tensor_scalar(h0[:, t, :], x1[:, t, :], norm.mv[:, t, 0:1],
                                                       norm.rstd[:, t:t + 1], ALU.subtract, ALU.mult)
                    last.then_inc(h0_ready, 1)
                    dve.drain()
                    norm.mean_square(nc, dve, h0).then_inc(ms_ready, 1)

                def rms_inverse(b):
                    dve.wait_ge(rms_ready, b + 1)
                    nc.vector.reciprocal(norm.rrms[:, :], norm.rms[:, :]).then_inc(rrms_ready, 1)

                def rope(w, b):
                    dve.wait_ge(rope_done, b * 2 + w + 1)
                    dve.wait_ge(full_ready[w], b + 1)
                    for i in range(KC):
                        nc.vector.tensor_tensor(t1[w][:, i, :], ps_a[:, i, :], keep["cos_" + "qk"[w]][:, :], ALU.mult)
                        last = nc.vector.tensor_tensor(t2[w][:, i, :], ps_b[:, i, :], keep["sin_" + "qk"[w]][:, :],
                                                       ALU.mult)
                    last.then_inc(rope_read, 1)

                def subtract_high(w, b):
                    dve.wait_ge(hi_ready[w], b + 1)
                    dve.wait_ge(low_ready[w], b + 1)
                    nc.vector.tensor_tensor(rest[w][:, :, :], full[w][:, :, :], parts[w][0][:, :, :], ALU.subtract)\
                      .then_inc(rest_ready[w], 1)

                turns(dve, batches, ((3, lambda b: subtract_high(1, b)), (1, residual), (0, divide),
                                     (2, lambda b: rope(0, b)), (1, layer_norm), (1, rms_inverse),
                                     (2, lambda b: subtract_high(0, b)), (2, lambda b: rope(1, b))))

            @block.scalar
            def _(act):
                act.sem_inc(xr_ready, 1)
                act.sem_inc(v_ready, 1)

                def deviation(b):
                    act.wait_ge(mv_ready, b + 1)
                    nc.scalar.activation(norm.std[:, :], norm.mv[:, :, 1], ACT.Sqrt, bias=keep["ln_eps"][:, :])\
                       .then_inc(std_ready, 1)

                def root_mean_square(b):
                    act.wait_ge(ms_ready, b + 1)
                    nc.scalar.activation(norm.rms[:, :], norm.ms[:, :], ACT.Sqrt, bias=keep["rms_eps"][:, :])\
                       .then_inc(rms_ready, 1)

                def scale_rows(b):
                    act.wait_ge(rrms_ready, b + 1)
                    for t in range(QT):
                        last = nc.scalar.activation(xr[:, t, :], h0[:, t, :], ACT.Copy, scale=norm.rrms[:, t:t + 1])
                    last.then_inc(xr_ready, 1)

                def take_turned(b):
                    act.wait_ge(turned, b + 1)
                    for i in range(KC):
                        last = nc.scalar.activation(xT[:, i, :], ps_t[:, i, :], ACT.Copy, scale=keep["g1"][:, i:i + 1])
                    last.then_inc(xT_ready, 1)

                def take_v(b):
                    act.wait_ge(v_done, b + 1)
                    act.wait_ge(v_sent, (b + 1) * 16 * GROUPS)
                    for t in range(QT):
                        last = nc.scalar.copy(vpad[:, t, :, 0:HD],
                                              ps_t[:, t // 2, t % 2 * DIM:(t % 2 + 1) * DIM]
                                              .rearrange("p (h d) -> p h d", d=HD))
                    last.then_inc(v_ready, 1)

                def high(w, b):
                    act.wait_ge(full_ready[w], b + 2)
                    act.wait_ge(sent[w], (b + 1) * SENT)
                    nc.scalar.copy(parts[w][0][:, :, :], full[w][:, :, :]).then_inc(hi_ready[w], 1)

                def middle(w, b):
                    act.wait_ge(rest_ready[w], b + 2)
                    nc.scalar.copy(parts[w][1][:, :, :], rest[w][:, :, :]).then_inc(mid_ready[w], 1)

                act.wait_ge(pads, 1)
                turns(act, batches, ((1, take_turned), (2, lambda b: high(1, b)), (0, deviation),
                                     (2, lambda b: middle(1, b)), (1, take_v), (1, lambda b: high(0, b)),
                                     (0, root_mean_square), (0, scale_rows), (1, lambda b: middle(0, b))))

            @block.gpsimd
            def _(pool):
                for s in (*full_ready, *low_ready, xb_ready):
                    pool.sem_inc(s, 1)

                def add_bias(b):
                    pool.wait_ge(x_came, (b + 1) * 16)
                    pool.wait_ge(x1_ready, b + 1)
                    for t in range(QT):
                        last = nc.gpsimd.tensor_tensor(xb[:, t, :], x[:, t, :], keep["bo"][:, :], ALU.add)
                    last.then_inc(xb_ready, 1)

                def add_and_split(w, b):
                    pool.wait_ge(rope_read, b * 2 + w + 2)
                    pool.wait_ge(rest_ready[w], b + 1)
                    nc.gpsimd.tensor_tensor(full[w][:, :, :], t1[w][:, :, :], t2[w][:, :, :], ALU.add)\
                      .then_inc(full_ready[w], 1)
                    pool.wait_ge(mid_ready[w], b + 1)
                    nc.gpsimd.tensor_tensor(parts[w][2][:, :, :], rest[w][:, :, :], parts[w][1][:, :, :],
                                            ALU.subtract).then_inc(low_ready[w], 1)

                turns(pool, batches, ((3, lambda b: add_and_split(1, b)), (0, add_bias),
                                      (2, lambda b: add_and_split(0, b))))
        p.clear()


def finish_self(nc, out_rows, inverse, x1_rows, h0_rows, y_rows, hn_rows, keep, batches):
    logits = keep["logits"]
    with ExitStack() as stack:
        p = Prog(nc, stack, "fin_")
        oT = p.sb("oT", [P, KC, SEQ])
        inv = p.sb("inv_rows", [P, KC, SEQ])
        on = p.sb("o_normed", [P, KC, SEQ])
        x1 = p.sb("x1", [P, QT, DIM])
        h0 = p.sb("h0", [P, QT, DIM])
        h = p.sb("h", [P, QT, DIM])
        y = p.sb("y", [P, QT, DIM])
        hr = p.sb("h_rms", [P, QT, DIM])
        hn = p.sb("h_normed", [P, QT, DIM])
        norm = Norms(p)
        hT = p.sb("hT", [P, KC, SEQ])
        ps_o = p.ps("ps_o", [P, QT, DIM])
        ps_t = p.ps("ps_t", [P, KC, SEQ])
        ps_l = p.ps("ps_l", [P, QT, EXPERTS])
        att_in = p.sem("att_in")
        rows_in = p.sem("rows_in")
        on_ready = p.sem("on_ready")
        o_done = p.sem("o_done")
        h_ready = p.sem("h_ready")
        y_ready = p.sem("y_ready")
        ms_ready = p.sem("ms_ready")
        rms_ready = p.sem("rms_ready")
        rrms_ready = p.sem("rrms_ready")
        hr_ready = p.sem("hr_ready")
        hn_ready = p.sem("hn_ready")
        turned = p.sem("turned")
        hT_ready = p.sem("hT_ready")
        l_done = p.sem("l_done")
        l_ready = p.sem("l_ready")
        y_sent = p.sem("y_sent")
        hn_sent = p.sem("hn_sent")

        with nc.Block() as block:
            @block.sync
            def _(sp):
                def load_attention(b):
                    sp.wait_ge(on_ready, b + 1)
                    load_attention_out(sp, out_rows, inverse, oT, inv, b, att_in)

                def load_rows(b):
                    sp.wait_ge(y_ready, b + 1)
                    for src, dst in ((x1_rows, x1), (h0_rows, h0)):
                        sp.dma_start(dst[:, :, :], src[bass.ds(b * SEQ, SEQ), :].rearrange("(t p) d -> p t d", p=P))\
                          .then_inc(rows_in, 16)

                turns(sp, batches, ((1, load_rows), (0, load_attention)))

            @block.tensor
            def _(pe):
                pe.sem_inc(turned, 1)

                def out_product(b):
                    pe.wait_ge(on_ready, b + 2)
                    for t in range(QT):
                        for i in range(KC):
                            last = nc.tensor.matmul(ps_o[:, t, :], on[:, i, t * P:(t + 1) * P], keep["wo"][:, i, :],
                                                    start=(i == 0), stop=(i == KC - 1))
                    last.then_inc(o_done, 1)

                def turn_rows(b):
                    pe.wait_ge(hn_ready, b + 2)
                    for t in range(QT):
                        for i in range(KC):
                            last = nc.tensor.transpose(ps_t[:, i, t * P:(t + 1) * P], hn[:, t, i * P:(i + 1) * P],
                                                       keep["ident"][:, :])
                    last.then_inc(turned, 1)

                def router(b):
                    pe.wait_ge(hT_ready, b + 1)
                    pe.wait_ge(l_ready, b + 1)
                    for t in range(QT):
                        for i in range(KC):
                            last = nc.tensor.matmul(ps_l[:, t, :], hT[:, i, t * P:(t + 1) * P],
                                                    keep["w_router"][:, i, :], start=(i == 0), stop=(i == KC - 1))
                    last.then_inc(l_done, 1)

                turns(pe, batches, ((2, turn_rows), (0, out_product), (2, router)))

            @block.vector
            def _(dve):
                dve.sem_inc(on_ready, 1)
                dve.sem_inc(l_ready, 1)

                def divide(b):
                    dve.wait_ge(att_in, (b + 1) * ATT_LOADS)
                    nc.vector.tensor_tensor(on[:, :, :], oT[:, :, :], inv[:, :, :], ALU.mult).then_inc(on_ready, 1)

                def residual(b):
                    dve.wait_ge(o_done, b + 1)
                    dve.wait_ge(rows_in, (b + 1) * 32)
                    dve.wait_ge(y_ready, b + 1)
                    dve.wait_ge(hr_ready, b + 1)
                    nc.vector.tensor_tensor(h[:, :, :], ps_o[:, :, :], h0[:, :, :], ALU.add).then_inc(h_ready, 1)

                def mean_square(b):
                    dve.wait_ge(h_ready, b + 1)
                    norm.mean_square(nc, dve, h).then_inc(ms_ready, 1)

                def rms_inverse(b):
                    dve.wait_ge(rms_ready, b + 1)
                    nc.vector.reciprocal(norm.rrms[:, :], norm.rms[:, :]).then_inc(rrms_ready, 1)

                def take_logits(b):
                    dve.wait_ge(l_done, b + 1)
                    nc.vector.tensor_copy(logits[:, bass.ds(b * QT, QT), :], ps_l[:, :, :]).then_inc(l_ready, 1)

                turns(dve, batches, ((1, residual), (0, divide), (1, mean_square), (1, rms_inverse),
                                     (3, take_logits)))

            @block.scalar
            def _(act):
                act.sem_inc(hr_ready, 1)

                def root_mean_square(b):
                    act.wait_ge(ms_ready, b + 1)
                    nc.scalar.activation(norm.rms[:, :], norm.ms[:, :], ACT.Sqrt, bias=keep["rms_eps"][:, :])\
                       .then_inc(rms_ready, 1)

                def scale_rows(b):
                    act.wait_ge(rrms_ready, b + 1)
                    act.wait_ge(hn_ready, b + 1)
                    for t in range(QT):
                        last = nc.scalar.activation(hr[:, t, :], h[:, t, :], ACT.Copy, scale=norm.rrms[:, t:t + 1])
                    last.then_inc(hr_ready, 1)

                def take_turned(b):
                    act.wait_ge(turned, b + 2)
                    nc.scalar.copy(hT[:, :, :], ps_t[:, :, :]).then_inc(hT_ready, 1)

                def store_y(b):
                    act.wait_ge(y_ready, b + 2)
                    act.dma_start(y_rows[bass.ds(b * SEQ, SEQ), :].rearrange("(t p) d -> p t d", p=P), y[:, :, :])\
                      .then_inc(y_sent, 16)

                def store_normed(b):
                    act.wait_ge(hn_ready, b + 2)
                    act.dma_start(hn_rows[bass.ds(b * SEQ, SEQ), :].rearrange("(t p) d -> p t d", p=P), hn[:, :, :])\
                      .then_inc(hn_sent, 16)

                act.sem_inc(y_sent, 16)
                act.sem_inc(hn_sent, 16)
                turns(act, batches, ((2, take_turned), (0, root_mean_square), (0, scale_rows), (0, store_y),
                                     (1, store_normed)))
                act.wait_ge(y_sent, 16 * (batches + 1))
                act.wait_ge(hn_sent, 16 * (batches + 1))

            @block.gpsimd
            def _(pool):
                pool.sem_inc(y_ready, 1)
                pool.sem_inc(hn_ready, 1)

                def add(b):
                    pool.wait_ge(h_ready, b + 1)
                    pool.wait_ge(y_sent, (b + 1) * 16)
                    nc.gpsimd.tensor_tensor(y[:, :, :], x1[:, :, :], h[:, :, :], ALU.add).then_inc(y_ready, 1)

                def weigh(b):
                    pool.wait_ge(hr_ready, b + 2)
                    pool.wait_ge(turned, b + 1)
                    pool.wait_ge(hn_sent, (b + 1) * 16)
                    for t in range(QT):
                        last = nc.gpsimd.tensor_tensor(hn[:, t, :], hr[:, t, :], keep["g2"][:, :], ALU.mult)
                    last.then_inc(hn_ready, 1)

                turns(pool, batches, ((0, add), (0, weigh)))
        p.clear()



def route(nc, keep, tokens):
    T = tokens // P
    E = EXPERTS
    TILES = 2 * T + E
    logits, slots, weights, expert = keep["logits"], keep["slots"], keep["pair_weights"], keep["tile_expert"]
    with ExitStack() as stack:
        p = Prog(nc, stack, "route_")
        probs = p.sb("probs", [P, T, E])
        work = p.sb("work", [P, T, E])
        chosen = p.sb("chosen", [P, T, E], BF16)
        first = p.sb("first_choice", [P, T, E])
        second = p.sb("second_choice", [P, T, E])
        row = p.sb("row_max", [P, T])
        left = p.sb("left", [P, T])
        top = [p.sb(f"top{i}", [P, T]) for i in range(2)]
        run = [p.sb(f"run{i}", [P, T, E]) for i in range(2)]
        place = p.sb("place", [P, T, E])
        compare = p.sb("compare", [P, E, 64])
        used = p.sb("used_tiles", [P, E])
        begin = p.sb("begin", [P, E])
        end = p.sb("end", [P, E])
        pairs = p.sb("pairs", [P, E, E])
        tile_cmp = p.sb("tile_cmp", [P, 96, E])
        tile_f = p.sb("tile_f", [P, 96])
        slot_f = p.sb("slot_f", [P, 2, T])
        ones = p.sb("ones", [P, P], BF16)
        ps_rank = p.ps("ps_rank", [P, T, E])
        ps_total = p.ps("ps_total", [P, T, E])
        shifted = p.sem("shifted")
        exp_ready = p.sem("exp_ready")
        chosen_ready = p.sem("chosen_ready")
        ranks_done = p.sem("ranks_done")
        routed = p.sem("routed")

        def over_e(a, n=T):
            return a.unsqueeze(2).broadcast_to([P, n, E])

        left_of = keep["iota_left"][:, :].unsqueeze(1).broadcast_to([P, T, E])

        with nc.Block() as block:
            @block.vector
            def _(dve):
                def tt(out, a, b, op):
                    nc.vector.tensor_tensor(out, a, b, op)
                    dve.drain()

                def reduce(out, a, op):
                    nc.vector.tensor_reduce(out, a, AX.X, op)
                    dve.drain()

                nc.vector.memset(ones[:, :], 1.0)
                reduce(row[:, :], logits[:, :, :], ALU.max)
                nc.vector.tensor_tensor(work[:, :, :], logits[:, :, :], over_e(row[:, :]), ALU.subtract)\
                  .then_inc(shifted, 1)
                dve.wait_ge(exp_ready, 1)
                reduce(row[:, :], probs[:, :, :], ALU.add)
                nc.vector.reciprocal(left[:, :], row[:, :])
                dve.drain()
                tt(probs[:, :, :], probs[:, :, :], over_e(left[:, :]), ALU.mult)
                for k, pick in enumerate((first, second)):
                    reduce(top[k][:, :], probs[:, :, :], ALU.max)
                    tt(work[:, :, :], probs[:, :, :], over_e(top[k][:, :]), ALU.is_equal)
                    tt(work[:, :, :], work[:, :, :], left_of, ALU.mult)
                    reduce(left[:, :], work[:, :, :], ALU.max)
                    tt(pick[:, :, :], over_e(left[:, :]), left_of, ALU.is_equal)
                    if k == 0:
                        nc.vector.scalar_tensor_tensor(out=probs[:, :, :], in0=pick[:, :, :], scalar=-2.0,
                                                       in1=probs[:, :, :], op0=ALU.mult, op1=ALU.add)
                        dve.drain()
                nc.vector.tensor_tensor(chosen[:, :, :], first[:, :, :], second[:, :, :], ALU.add)\
                  .then_inc(chosen_ready, 1)
                tt(row[:, :], top[0][:, :], top[1][:, :], ALU.add)
                nc.vector.reciprocal(left[:, :], row[:, :])
                dve.drain()
                for k in range(2):
                    tt(weights[:, k, :], top[k][:, :], left[:, :], ALU.mult)
                dve.wait_ge(ranks_done, 1)
                nc.vector.tensor_copy(run[0][:, :, :], ps_total[:, :, :])
                dve.drain()
                src, step = 0, 1
                while step < T:
                    a, b = run[src], run[1 - src]
                    nc.vector.tensor_copy(b[:, 0:step, :], a[:, 0:step, :])
                    tt(b[:, step:T, :], a[:, step:T, :], a[:, 0:T - step, :], ALU.add)
                    src, step = 1 - src, step * 2
                total = run[src]
                n = T + 1
                tt(compare[:, :, 0:n], total[:, T - 1, :].unsqueeze(2).broadcast_to([P, E, n]),
                   keep["iota_count"][:, 0:n].unsqueeze(1).broadcast_to([P, E, n]), ALU.is_gt)
                reduce(used[:, :], compare[:, :, 0:n], ALU.add)
                tt(pairs[:, :, :], used[:, :].unsqueeze(1).broadcast_to([P, E, E]),
                   keep["lt8"][:, :].rearrange("p (a b) -> p a b", b=E), ALU.mult)
                reduce(begin[:, :], pairs[:, :, :], ALU.add)
                tt(end[:, :], begin[:, :], used[:, :], ALU.add)
                tt(tile_cmp[:, 0:TILES, :], over_e(keep["iota_tile"][:, 0:TILES], TILES),
                   end[:, :].unsqueeze(1).broadcast_to([P, TILES, E]), ALU.is_ge)
                reduce(tile_f[:, 0:TILES], tile_cmp[:, 0:TILES, :], ALU.add)
                nc.vector.tensor_scalar(expert[:, 0:TILES], tile_f[:, 0:TILES], E - 1.0, None, ALU.min)
                tt(place[:, :, :], total[:, :, :], ps_total[:, :, :], ALU.subtract)
                tt(place[:, :, :], place[:, :, :], ps_rank[:, :, :], ALU.add)
                nc.vector.scalar_tensor_tensor(out=place[:, :, :], in0=begin[:, :].unsqueeze(1).broadcast_to([P, T, E]),
                                               scalar=float(P), in1=place[:, :, :], op0=ALU.mult, op1=ALU.add)
                dve.drain()
                for k, pick in enumerate((first, second)):
                    tt(work[:, :, :], pick[:, :, :], place[:, :, :], ALU.mult)
                    reduce(slot_f[:, k, :], work[:, :, :], ALU.add)
                nc.vector.tensor_copy(slots[:, :, :], slot_f[:, :, :]).then_inc(routed, 1)
                dve.wait_ge(routed, 1)

            @block.scalar
            def _(act):
                act.wait_ge(shifted, 1)
                nc.scalar.activation(probs[:, :, :], work[:, :, :], ACT.Exp).then_inc(exp_ready, 1)

            @block.tensor
            def _(pe):
                pe.wait_ge(chosen_ready, 1)
                nc.tensor.matmul(ps_rank[:, :, :].rearrange("p t e -> p (t e)"), keep["before_b"][:, :],
                                 chosen[:, :, :].rearrange("p t e -> p (t e)"), start=True, stop=True)
                nc.tensor.matmul(ps_total[:, :, :].rearrange("p t e -> p (t e)"), ones[:, :],
                                 chosen[:, :, :].rearrange("p t e -> p (t e)"), start=True, stop=True)\
                  .then_inc(ranks_done, 1)
        p.clear()


def scatter_rows(nc, hn_rows, in_sorted, wd, keep, tokens):
    T = tokens // P
    slots = keep["slots"]
    D = 4
    CH = -(-HHALF // P)
    with ExitStack() as stack:
        p = Prog(nc, stack, "scat_")
        rows = [[p.sb(f"token_rows{g}{k}", [P, DIM]) for k in range(D)] for g in range(2)]
        index = [p.sb(f"index{g}", [P, 2, D], I32) for g in range(2)]
        rows_in = [p.sem(f"rows_in{g}") for g in range(2)]
        index_ready = p.sem("index_ready")
        gone = [p.sem(f"gone{g}") for g in range(2)]
        done = p.sem("done")
        pool_turn = p.sem("pool_turn")
        wd_in = keep["wd_in"]
        with nc.Block() as block:
            @block.sync
            def _(sp):
                sp.sem_inc(done, 2)
                with sp.Fori(0, T // (2 * D)) as i:
                    for g in range(2):
                        sp.wait_ge(done, i * 2 + g + 1)
                        for k in range(D):
                            sp.dma_start(rows[g][k][:, :], hn_rows[bass.ds(((i * 2 + g) * D + k) * P, P), :])\
                              .then_inc(rows_in[g], 16)

            @block.scalar
            def _(act):
                full, rest = HHALF // P, HHALF % P
                with act.Fori(0, EXPERTS) as e:
                    for half in range(2):
                        src = wd[bass.ds(e, 1), half * HHALF:(half + 1) * HHALF, :].rearrange("e r n -> (e r) n")
                        at = (e * 2 + half) * (CH * DIM)
                        act.dma_start(keep["wd_sb"][:, bass.ds(at, full * DIM)].rearrange("p (c n) -> p c n", n=DIM),
                                      src[0:full * P, :].rearrange("(c p) n -> p c n", p=P)).then_inc(wd_in, 16)
                        act.dma_start(keep["wd_sb"][0:rest, bass.ds(at + full * DIM, DIM)],
                                      src[full * P:HHALF, :]).then_inc(wd_in, 16)

            @block.vector
            def _(dve):
                with dve.Fori(0, T // (2 * D)) as i:
                    for g in range(2):
                        dve.wait_ge(done, i * 2 + g + 1)
                        nc.vector.tensor_copy(index[g][:, :, :], slots[:, :, bass.ds((i * 2 + g) * D, D)])\
                          .then_inc(index_ready, 1)

            @block.gpsimd
            def _(pool):
                def ended(i, g):
                    pool.wait_ge(gone[g], (i + 1) * 32 * D)
                    pool.sem_inc(done, 1)

                def scatter(i, g):
                    pool.wait_ge(rows_in[g], (i + 1) * 16 * D)
                    pool.wait_ge(index_ready, i * 2 + g + 1)
                    pool.sem_inc(pool_turn, 1)
                    for k in range(D):
                        for c in range(2):
                            pool.indirect_dma_start(
                                out=in_sorted,
                                out_offset=bass.IndirectOffsetOnAxis(ap=index[g][:, c, k:k + 1], axis=0),
                                in_=rows[g][k][:, :], in_offset=None).then_inc(gone[g], 16)

                scatter(0, 0)
                with pool.Fori(0, T // (2 * D) - 1) as i:
                    scatter(i, 1)
                    ended(i, 0)
                    scatter(i + 1, 0)
                    ended(i, 1)
                scatter(T // (2 * D) - 1, 1)
                for g in range(2):
                    ended(T // (2 * D) - 1, g)
        p.clear()


def experts(nc, in_sorted, out_sorted, keep, tiles):
    HALVES = 2
    CH = -(-HHALF // P)
    CW = [min(P, HHALF - c * P) for c in range(CH)]
    with ExitStack() as stack:
        p = Prog(nc, stack, "moe_")
        rows = [p.sb(f"rows{i}", [P, DIM]) for i in range(2)]
        xT = [p.sb(f"rowsT{i}", [P, KC, P]) for i in range(2)]
        sil = [p.sb(f"silu{i}", [P, HHALF]) for i in range(2)]
        h = [p.sb(f"hidden{i}", [P, HHALF]) for i in range(2)]
        hT = [p.sb(f"hiddenT{i}", [P, CH, P]) for i in range(2)]
        y = [p.sb(f"y{i}", [P, DIM]) for i in range(2)]
        ps_g = [p.ps(f"ps_g{i}", [P, SEQ]) for i in range(2)]
        ps_u = [p.ps(f"ps_u{i}", [P, SEQ]) for i in range(2)]
        ps_h = [p.ps(f"ps_h{i}", [P, CH, P]) for i in range(2)]
        ps_x = p.ps("ps_x", [P, KC, P])
        ps_y = p.ps("ps_y", [P, DIM])
        rows_in = [p.sem(f"rows_in{i}") for i in range(2)]
        turned = p.sem("turned")
        xT_ready = p.sem("xT_ready")
        gu_done = p.sem("gu_done")
        sil_ready = p.sem("sil_ready")
        h_ready = p.sem("h_ready")
        h_turned = p.sem("h_turned")
        hT_ready = p.sem("hT_ready")
        down_done = p.sem("down_done")
        y_ready = p.sem("y_ready")
        sent = [p.sem(f"sent{i}") for i in range(2)]

        class Tile:

            def __init__(self, i, r):
                self.i, self.r = i, r
                self.n = i * 2 + r
                self.par = r % 2
                self.turn = i + r // 2

            def next(self, d):
                return Tile(self.i, self.r + d)

        def tile_turns(eng, first, step, last):
            first(Tile(0, 0))
            with eng.Fori(0, (tiles - 3) // 2) as i:
                step(Tile(i, 1), True)
                step(Tile(i, 2), True)
            step(Tile(0, tiles - 2), True)
            step(Tile(0, tiles - 1), False)
            last(Tile(0, tiles - 1))

        assert tiles % 2 == 1
        with nc.Block() as block:
            @block.sync
            def _(sp):
                sp.sem_inc(turned, 2)
                for i in range(2):
                    sp.sem_inc(sent[i], 16)

                def load(t):
                    sp.wait_ge(turned, t.n + 1)
                    sp.dma_start(rows[t.par][:, :], in_sorted[bass.ds(t.n * P, P), :]).then_inc(rows_in[t.par], 16)

                def store(t):
                    sp.wait_ge(y_ready, t.n + 2)
                    sp.dma_start(out_sorted[bass.ds(t.n * P, P), :], y[t.par][:, :]).then_inc(sent[t.par], 16)

                for t in range(3):
                    load(Tile(0, t))
                with sp.Fori(0, (tiles - 3) // 2) as i:
                    for r in range(2):
                        load(Tile(i, r + 3))
                        store(Tile(i, r))
                for t in range(tiles - 3, tiles):
                    store(Tile(0, t))
                for i in range(2):
                    sp.wait_ge(sent[i], 16 * ((tiles + 1 - i) // 2 + 1))

            @block.tensor
            def _(pe):
                pe.sem_inc(h_turned, 2)
                pe.sem_inc(down_done, 1)
                pe.wait_ge(keep["gate_up_in"], 16 * 2 * KC * EXPERTS)
                pe.wait_ge(keep["wd_in"], 16 * 4 * EXPERTS)
                wg, wu, wd = keep["wg_sb"], keep["wu_sb"], keep["wd_sb"]

                def expert_of(t):
                    return pe.value_load(keep["tile_expert"][0:1, bass.ds(t.n, 1)], min_val=0, max_val=EXPERTS - 1)

                def turn_rows(t):
                    pe.wait_ge(rows_in[t.par], (t.turn + 1) * 16)
                    pe.wait_ge(xT_ready, t.n + 1)
                    for i in range(KC):
                        last = nc.tensor.transpose(ps_x[:, i, :], rows[t.par][:, i * P:(i + 1) * P],
                                                   keep["ident"][:, :])
                    last.then_inc(turned, 1)

                def gate_up(t, half, e):
                    if half == 0:
                        pe.wait_ge(xT_ready, t.n + 2)
                    pe.wait_ge(h_ready, t.n * 2 + half + 1)
                    for ps, wt in ((ps_g, wg), (ps_u, wu)):
                        for i in range(KC):
                            at = e * (KC * HIDDEN) + i * HIDDEN + half * HHALF
                            last = nc.tensor.matmul(ps[half][:, 0:HHALF], xT[t.par][:, i, :],
                                                    wt[:, bass.ds(at, HHALF)], start=(i == 0), stop=(i == KC - 1))
                    last.then_inc(gu_done, 1)

                def turn_hidden(t, half):
                    pe.wait_ge(h_ready, t.n * 2 + half + 3)
                    pe.wait_ge(hT_ready, t.n * 2 + half + 1)
                    for c in range(CH):
                        last = nc.tensor.transpose(ps_h[half][0:CW[c], c, :], h[half][:, c * P:c * P + CW[c]],
                                                   keep["ident"][:, :])
                    last.then_inc(h_turned, 1)

                def down(t, e):
                    pe.wait_ge(y_ready, t.n + 1)
                    pe.wait_ge(hT_ready, t.n * 2 + 4)
                    for half in range(HALVES):
                        for c in range(CH):
                            at = e * (HALVES * CH * DIM) + (half * CH + c) * DIM
                            last = nc.tensor.matmul(ps_y[:, :], hT[half][0:CW[c], c, :],
                                                    wd[0:CW[c], bass.ds(at, DIM)],
                                                    start=(half == 0 and c == 0), stop=(half == 1 and c == CH - 1))
                    last.then_inc(down_done, 1)

                def first(t):
                    e = expert_of(t)
                    turn_rows(t)
                    turn_rows(t.next(1))
                    gate_up(t, 0, e)
                    gate_up(t, 1, e)
                    turn_hidden(t, 0)

                def step(t, following):
                    before, e = expert_of(t.next(-1)), expert_of(t)
                    if following:
                        turn_rows(t.next(1))
                    gate_up(t, 0, e)
                    turn_hidden(t.next(-1), 1)
                    gate_up(t, 1, e)
                    down(t.next(-1), before)
                    turn_hidden(t, 0)

                def last(t):
                    e = expert_of(t)
                    turn_hidden(t, 1)
                    down(t, e)

                tile_turns(pe, first, step, last)

            @block.scalar
            def _(act):
                act.sem_inc(xT_ready, 1)
                act.sem_inc(y_ready, 1)

                def turned_rows(t):
                    act.wait_ge(turned, t.n + 3)
                    nc.scalar.copy(xT[t.par][:, :, :], ps_x[:, :, :]).then_inc(xT_ready, 1)

                def silu(t, half):
                    act.wait_ge(gu_done, t.n * 2 + half + 1)
                    act.wait_ge(h_ready, t.n * 2 + half + 1)
                    nc.scalar.activation(sil[half][:, :], ps_g[half][:, 0:HHALF], ACT.Silu).then_inc(sil_ready, 1)

                def result(t):
                    act.wait_ge(down_done, t.n + 2)
                    act.wait_ge(sent[t.par], (t.turn + 1) * 16)
                    nc.scalar.copy(y[t.par][:, :], ps_y[:, :]).then_inc(y_ready, 1)

                def first(t):
                    turned_rows(t)
                    turned_rows(t.next(1))
                    silu(t, 0)
                    silu(t, 1)

                def step(t, following):
                    if following:
                        turned_rows(t.next(1))
                    silu(t, 0)
                    silu(t, 1)
                    result(t.next(-1))

                tile_turns(act, first, step, result)

            @block.vector
            def _(dve):
                dve.sem_inc(h_ready, 2)
                dve.sem_inc(hT_ready, 2)

                def multiply(t, half):
                    dve.wait_ge(sil_ready, t.n * 2 + half + 1)
                    dve.wait_ge(h_turned, t.n * 2 + half + 1)
                    nc.vector.tensor_tensor(h[half][:, :], ps_u[half][:, 0:HHALF], sil[half][:, :], ALU.mult)\
                      .then_inc(h_ready, 1)

                def turned_hidden(t, half):
                    dve.wait_ge(h_turned, t.n * 2 + half + 3)
                    dve.wait_ge(down_done, t.n + 1)
                    nc.vector.tensor_copy(hT[half][:, 0:CH - 1, :], ps_h[half][:, 0:CH - 1, :])
                    nc.vector.tensor_copy(hT[half][0:CW[-1], CH - 1, :], ps_h[half][0:CW[-1], CH - 1, :])\
                      .then_inc(hT_ready, 1)

                def first(t):
                    multiply(t, 0)
                    multiply(t, 1)
                    turned_hidden(t, 0)

                def step(t, following):
                    turned_hidden(t.next(-1), 1)
                    multiply(t, 0)
                    multiply(t, 1)
                    turned_hidden(t, 0)

                tile_turns(dve, first, step, lambda t: turned_hidden(t, 1))
        p.clear()


def combine(nc, out_sorted, y_rows, out, keep, tokens):
    T = tokens // P
    slots, weights = keep["slots"], keep["pair_weights"]
    D = 4
    with ExitStack() as stack:
        p = Prog(nc, stack, "comb_")
        index = [p.sb(f"index{g}", [P, 2, D], I32) for g in range(2)]
        wt = [p.sb(f"pair{g}", [P, 2, D]) for g in range(2)]
        r = [[[p.sb(f"row{g}{k}{c}", [P, DIM]) for c in range(2)] for k in range(D)] for g in range(2)]
        y = [p.sb(f"y{g}", [P, D, DIM]) for g in range(2)]
        y_in = [p.sem(f"y_in{g}") for g in range(2)]
        index_ready = p.sem("index_ready")
        pool_turn = p.sem("pool_turn")
        got = [[p.sem(f"got{g}{k}") for k in range(D)] for g in range(2)]
        half_summed = p.sem("half_summed")
        summed = p.sem("summed")
        sent = [p.sem(f"sent{g}") for g in range(2)]
        with nc.Block() as block:
            @block.sync
            def _(sp):
                def rows_of(a, i, g):
                    return a[bass.ds((i * 2 + g) * (D * P), D * P), :].rearrange("(t p) d -> p t d", p=P)

                def load(i, g):
                    sp.wait_ge(sent[g], (i + 1) * 16)
                    sp.dma_start(y[g][:, :, :], rows_of(y_rows, i, g)).then_inc(y_in[g], 16)

                def store(i, g):
                    sp.wait_ge(summed, i * 2 + g + 1)
                    sp.dma_start(rows_of(out, i, g), y[g][:, :, :]).then_inc(sent[g], 16)

                for g in range(2):
                    sp.sem_inc(sent[g], 16)
                    load(0, g)
                with sp.Fori(0, T // (2 * D) - 1) as i:
                    for g in range(2):
                        store(i, g)
                        load(i + 1, g)
                for g in range(2):
                    store(T // (2 * D) - 1, g)
                for g in range(2):
                    sp.wait_ge(sent[g], 16 * (T // (2 * D) + 1))

            @block.gpsimd
            def _(pool):
                with pool.Fori(0, T // (2 * D)) as i:
                    for g in range(2):
                        pool.wait_ge(index_ready, i * 2 + g + 1)
                        pool.sem_inc(pool_turn, 1)
                        for k in range(D):
                            for c in range(2):
                                pool.indirect_dma_start(
                                    out=r[g][k][c][:, :], out_offset=None, in_=out_sorted,
                                    in_offset=bass.IndirectOffsetOnAxis(ap=index[g][:, c, k:k + 1], axis=0))\
                                    .then_inc(got[g][k], 16)

            @block.vector
            def _(dve):
                def prepare(i, g):
                    at = (i * 2 + g) * D
                    nc.vector.tensor_copy(wt[g][:, :, :], weights[:, :, bass.ds(at, D)])
                    nc.vector.tensor_copy(index[g][:, :, :], slots[:, :, bass.ds(at, D)]).then_inc(index_ready, 1)

                def add(i, g):
                    dve.wait_ge(y_in[g], (i + 1) * 16)
                    for k in range(D):
                        dve.wait_ge(got[g][k], (i + 1) * 32)
                        nc.vector.scalar_tensor_tensor(out=y[g][:, k, :], in0=r[g][k][0][:, :],
                                                       scalar=wt[g][:, 0, k:k + 1], in1=y[g][:, k, :],
                                                       op0=ALU.mult, op1=ALU.add).then_inc(half_summed, 1)
                        dve.wait_ge(half_summed, (i * 2 + g) * D + k + 1)
                        last = nc.vector.scalar_tensor_tensor(out=y[g][:, k, :], in0=r[g][k][1][:, :],
                                                              scalar=wt[g][:, 1, k:k + 1], in1=y[g][:, k, :],
                                                              op0=ALU.mult, op1=ALU.add)
                    last.then_inc(summed, 1)
                    dve.wait_ge(summed, i * 2 + g + 1)

                for g in range(2):
                    prepare(0, g)
                with dve.Fori(0, T // (2 * D) - 1) as i:
                    for g in range(2):
                        add(i, g)
                        prepare(i + 1, g)
                for g in range(2):
                    add(T // (2 * D) - 1, g)
        p.clear()


CONSTANTS = (("ident", P), ("mask_q", P), ("mask_kv", P), ("before", P), ("cos_q", SEQ), ("sin_q", SEQ),
             ("cos_k", SEQ), ("sin_k", SEQ), ("iota_left", EXPERTS), ("iota_tile", 96), ("iota_count", 64),
             ("lt8", EXPERTS * EXPERTS))


def shape_constants():
    import numpy as np
    i = np.arange(P)
    later = (i[None, :] > i[:, None]).astype(np.float32) * np.float32(MASKED)
    t = np.arange(SEQ, dtype=np.float32)
    inv_freq = 1.0 / 10000.0 ** (np.arange(0, HD, 2, dtype=np.float32) / HD)
    angle = np.einsum("i,j->ij", t, inv_freq.astype(np.float32)).astype(np.float32)
    cos = np.tile(np.cos(angle).T, (P // (HD // 2), 1)).astype(np.float32)
    sin = np.tile(np.sin(angle).T, (P // (HD // 2), 1)).astype(np.float32)
    e = np.arange(EXPERTS, dtype=np.float32)
    out = {
        "ident": np.eye(P, dtype=np.float32),
        "mask_q": later,
        "mask_kv": np.ascontiguousarray(later.T),
        "before": (i[:, None] < i[None, :]).astype(np.float32),
        "cos_q": cos * np.float32(SCALE), "sin_q": sin * np.float32(SCALE), "cos_k": cos, "sin_k": sin,
        "iota_left": np.tile(EXPERTS - e, (P, 1)),
        "iota_tile": np.tile(np.arange(96, dtype=np.float32), (P, 1)),
        "iota_count": np.tile(np.arange(64, dtype=np.float32) * P, (P, 1)),
        "lt8": np.tile((e[None, :] < e[:, None]).astype(np.float32).reshape(1, -1), (P, 1)),
    }
    assert [(n, v.shape[1]) for n, v in out.items()] == list(CONSTANTS)
    return {"constants": np.ascontiguousarray(np.concatenate(list(out.values()), axis=1), dtype=np.float32)}


def zeros_beside(nc, in_sorted, stack, tiles, units):
    share = tiles // (units // 4)
    part = share // 3
    assert part * 3 * (units // 4) == tiles
    p = Prog(nc, stack, "zero_")
    zeros = p.sb("zeros", [P, part, DIM])
    zeros_set = p.sem("zeros_set")
    zeroed = p.sem("zeroed")

    def first(dve):
        nc.vector.memset(zeros[:, :, :], 0.0).then_inc(zeros_set, 1)

    def unit(pool, i, r):
        if r < 3:
            pool.wait_ge(zeros_set, 1)
            pool.dma_start(in_sorted[bass.ds(i * (share * P) + r * (part * P), part * P), :]
                           .rearrange("(t p) d -> p t d", p=P), zeros[:, :, :]).then_inc(zeroed, 16)

    def last(pool):
        pool.wait_ge(zeroed, 16 * 3 * (units // 4))

    return p, (first, unit, last)


def gate_up_beside(nc, a, keep, p, units):
    assert units // 4 == EXPERTS and KC == 2
    keep["wg_sb"] = p.sb("wg_sb", [P, EXPERTS * KC * HIDDEN])
    keep["wu_sb"] = p.sb("wu_sb", [P, EXPERTS * KC * HIDDEN])
    keep["gate_up_in"] = p.sem("gate_up_in")

    def unit(pool, e, r):
        n, c = ("wg", "wu")[r // 2], r % 2
        pool.dma_start(keep[n + "_sb"][:, bass.ds(e * (KC * HIDDEN) + c * HIDDEN, HIDDEN)],
                       a[n][bass.ds(e, 1), c * P:(c + 1) * P, :].rearrange("e p n -> p (e n)"))\
            .then_inc(keep["gate_up_in"], 16)

    return (None, unit, None)


KEEP_SHAPES = {"WqT": 0, "WkT": 0, "WvT": 0, "WoT": 0, "wq": 0, "wk": 0, "wv": 0, "wo": 0, "wq_rot": 0, "wk_rot": 0}


def build(nc, a, out, batches=8):
    units = batches * GROUPS
    dram = lambda name, shape, dt=F32: nc.dram_tensor(name, shape, dt, kind="Internal").ap()
    k_parts = dram("k_parts", [units, 3, GR, CTX], BF16)
    q_parts = dram("q_parts", [units, 3, GR, SEQ], BF16)
    v_rows = dram("v_rows", [units, CTX, GH * VW])
    out_rows = dram("out_rows", [units, P, SEQ])
    inverse = dram("inverse", [units * GH, SEQ])
    k2_parts = dram("k2_parts", [units, 3, GR, SEQ], BF16)
    q2_parts = dram("q2_parts", [units, 3, GR, SEQ], BF16)
    v2_rows = dram("v2_rows", [units, SEQ, GH * VW])
    out2_rows = dram("out2_rows", [units, P, SEQ])
    inverse2 = dram("inverse2", [units * GH, SEQ])
    tokens = batches * SEQ
    x1_rows = dram("x1_rows", [tokens, DIM])
    h0_rows = dram("h0_rows", [tokens, DIM])
    y_rows = dram("y_rows", [tokens, DIM])
    hn_rows = dram("hn_rows", [tokens, DIM])
    tiles = 2 * tokens // P + EXPERTS
    in_sorted = dram("in_sorted", [tiles * P, DIM])
    out_sorted = dram("out_sorted", [(tiles - 1) * P, DIM])
    with ExitStack() as stack:
        p = Prog(nc, stack, "top_")
        keep = {n: p.sb(f"keep_{n}", [P, KC, DIM]) for n in KEEP_SHAPES}
        keep["constants"] = p.sb("keep_constants", [P, sum(w for _, w in CONSTANTS)])
        column = 0
        for n, w in CONSTANTS:
            keep[n] = keep["constants"][:, column:column + w]
            column += w
        for n, w in (("bq", KC), ("bk", KC), ("g1", KC), ("bv", DIM), ("bo", DIM), ("g2", DIM), ("ln_eps", 1),
                     ("rms_eps", 1)):
            keep[n] = p.sb(f"keep_{n}", [P, w])
        for n in ("ident", "mask_q", "mask_kv", "before"):
            keep[n + "_b"] = p.sb(f"keep_{n}_b", [P, P], BF16)
        keep["w_router"] = p.sb("keep_w_router", [P, KC, EXPERTS])
        prepare_weights(nc, a, keep)
        project_inputs(nc, a["ctx"], a["x"], k_parts, v_rows, q_parts, keep, batches)
        with ExitStack() as zeros_stack:
            z, beside = zeros_beside(nc, in_sorted, zeros_stack, tiles, units)
            attention(nc, q_parts, k_parts, v_rows, out_rows, CTX, False, keep, units, beside)
            z.clear()
        invert_denominators(nc, out_rows, inverse, False, units)
        project_self(nc, a["x"], out_rows, inverse, x1_rows, h0_rows, q2_parts, k2_parts, v2_rows, keep, batches)
        beside = gate_up_beside(nc, a, keep, p, units)
        attention(nc, q2_parts, k2_parts, v2_rows, out2_rows, SEQ, True, keep, units, beside)
        invert_denominators(nc, out2_rows, inverse2, True, units)
        keep["logits"] = p.sb("logits", [P, tokens // P, EXPERTS])
        keep["slots"] = p.sb("slots", [P, 2, tokens // P], I32)
        keep["pair_weights"] = p.sb("pair_weights", [P, 2, tokens // P])
        keep["tile_expert"] = p.sb("tile_expert", [P, tiles], I32)
        finish_self(nc, out2_rows, inverse2, x1_rows, h0_rows, y_rows, hn_rows, keep, batches)
        route(nc, keep, tokens)
        keep["wd_in"] = p.sem("wd_in")
        keep["wd_sb"] = p.sb("wd_sb", [P, EXPERTS * 2 * -(-HHALF // P) * DIM])
        scatter_rows(nc, hn_rows, in_sorted, a["wd"], keep, tokens)
        experts(nc, in_sorted, out_sorted, keep, tiles - 1)
        combine(nc, out_sorted, y_rows, out, keep, tokens)


WEIGHTS = {n: f"L0_xattn_{n}" for n in ("Wq", "bq", "Wk", "bk", "Wv", "bv", "Wo", "bo")}
WEIGHTS.update({n: f"L0_ffn_{n}" for n in ("wq", "wk", "wv", "wo", "w_router", "wg", "wu", "wd", "g1", "g2")})


def kernel(**inputs):
    import numpy as _np
    import concourse.bacc as _bacc
    from concourse import mybir as _mybir
    from concourse.bass_utils import run_bass_kernel_spmd as _run

    x = _np.ascontiguousarray(inputs["x"])
    data = {"x": x.reshape(-1, DIM), "ctx": _np.ascontiguousarray(inputs["ctx_1024"]).reshape(-1, DIM)}
    data.update({n: _np.ascontiguousarray(inputs[full]) for n, full in WEIGHTS.items()})
    data.update(shape_constants())
    nc = _bacc.Bacc("TRN2", target_bir_lowering=False, num_devices=1)
    arrays, args = {}, {}
    for n, v in data.items():
        arrays[f"in_{n}_dram"] = v
        args[n] = nc.dram_tensor(f"in_{n}_dram", v.shape, _mybir.dt.from_np(v.dtype), kind="ExternalInput").ap()
    out = nc.dram_tensor("out_dram", data["x"].shape, _mybir.dt.from_np(x.dtype), kind="ExternalOutput").ap()
    build(nc, args, out, x.shape[0])
    got = _run(nc, [arrays], core_ids=[0]).results[0]["out_dram"]
    return got.reshape(x.shape)
```
